# Optimizing a Trainium2 kernel written in Bass

```python
import numpy as np
import jax
import jax.numpy as jnp

def _softmax(x, axis=-1):
    return jax.nn.softmax(x, axis=axis)

def _gelu(x):
    return jax.nn.gelu(x, approximate=True)

def _silu(x):
    return jax.nn.silu(x)

def _sigmoid(x):
    return jax.nn.sigmoid(x)

def _layernorm(x, axis=-1, eps=1e-05):
    m = jnp.mean(x, axis=axis, keepdims=True)
    v = jnp.var(x, axis=axis, keepdims=True)
    return (x - m) / jnp.sqrt(v + eps)

def _scatter_add(tgt, idx, src, axis=0):
    return tgt.at[idx].add(src)

def _segment_sum(src, seg, n):
    return jax.ops.segment_sum(src, seg, n)
kernel_name = 'mk_lm_tower_d2_tok_ids256_r4_81bd44'

def setup_inputs(seed: int=0):
    np.random.seed(seed)
    _w = jnp.asarray

    def _rec_inputs():
        import jax
        import jax.numpy as jnp
        _rk = jax.random.key(seed)
        x = jax.random.randint(jax.random.fold_in(_rk, 1), (8, 1024), 0, 12500, jnp.int32)
        return x
    x = _rec_inputs()

    def _L0_tok_setup():
        import jax, jax.numpy as jnp
        import numpy as np
        INP_SIZE = 12500
        HIDDEN = 64
        KERNEL = 5
        WEIGHTS = jnp.array([0.1, 0.2, 0.4, 0.2, 0.1], dtype=jnp.float32)
        key = jax.random.key(seed)
        k1, k2 = jax.random.split(key)
        x = jax.random.randint(k1, (8, 1024), 0, INP_SIZE, dtype=jnp.int32)
        emb = jax.random.normal(k2, (INP_SIZE, HIDDEN), dtype=jnp.float32)
        return {'x': x, 'emb': emb}
    _L0_tok_all = _L0_tok_setup()
    _L0_tok_in = {k: v for k, v in _L0_tok_all.items() if k in ('emb',)}
    del _L0_tok_all

    def _L0_attn_setup():
        import jax, jax.numpy as jnp
        import numpy as np
        from math import sqrt
        DIM = 64
        key = jax.random.key(seed)
        k1, k2, k3, k4 = jax.random.split(key, 4)
        B, T, D, H, R = (2, 1024, DIM, 8, 32)

        def xavier(k, shape, fan_in, fan_out):
            a = sqrt(6.0 / (fan_in + fan_out))
            return jax.random.uniform(k, shape, jnp.float32, -a, a)
        x = jax.random.normal(k1, (B, T, D), jnp.float32)
        Q = xavier(k2, (H, R, D), D, R)
        K = xavier(k3, (H, R, D), D, R)
        VO = xavier(k4, (H, D, D), D, D)
        return {'x': x, 'Q': Q, 'K': K, 'VO': VO}
    _L0_attn_all = _L0_attn_setup()
    _L0_attn_in = {k: v for k, v in _L0_attn_all.items() if k in ('Q', 'K', 'VO')}
    del _L0_attn_all

    def _L0_ffn_setup():
        import jax, jax.numpy as jnp
        import numpy as np
        C = 64
        HID = 256
        E = 8
        TEMP = 1.0
        key = jax.random.key(seed)
        ks = jax.random.split(key, 7)
        x = jax.random.normal(ks[0], (8, 4096, C), dtype=jnp.float32)
        W1 = jax.random.normal(ks[1], (C, HID), dtype=jnp.float32) * 0.02
        b1 = jnp.zeros((HID,), dtype=jnp.float32)
        Wg = jax.random.normal(ks[2], (HID, E), dtype=jnp.float32) * 0.02
        bg = jnp.zeros((E,), dtype=jnp.float32)
        Wd = jax.random.normal(ks[3], (E, HID, C), dtype=jnp.float32) * 0.02
        bd = jnp.zeros((E, C), dtype=jnp.float32)
        return {'x': x, 'W1': W1, 'b1': b1, 'Wg': Wg, 'bg': bg, 'Wd': Wd, 'bd': bd}
    _L0_ffn_all = _L0_ffn_setup()
    _L0_ffn_in = {k: v for k, v in _L0_ffn_all.items() if k in ('W1', 'b1', 'Wg', 'bg', 'Wd', 'bd')}
    del _L0_ffn_all

    def _L1_attn_setup():
        import jax, jax.numpy as jnp
        import numpy as np
        B, N, D = (8, 512, 64)
        key = jax.random.key(seed)
        k1, k2, k3, k4 = jax.random.split(key, 4)
        s = D ** (-0.5)
        return {'x': jax.random.normal(k1, (B, N, D), dtype=jnp.float32), 'Wq': jax.random.normal(k2, (D, D), dtype=jnp.float32) * s, 'Wk': jax.random.normal(k3, (D, D), dtype=jnp.float32) * s, 'Wv': jax.random.normal(k4, (D, D), dtype=jnp.float32) * s}
    _L1_attn_all = _L1_attn_setup()
    _L1_attn_in = {k: v for k, v in _L1_attn_all.items() if k in ('Wq', 'Wk', 'Wv')}
    del _L1_attn_all

    def _L1_ffn_setup():
        import jax, jax.numpy as jnp
        import numpy as np
        B, N, D = (16, 1024, 64)
        NUM_EXPERTS, TOP_K, HEADS = (4, 2, 4)
        N_EDGES = 262144
        LN_EPS = 1e-05

        def _layernorm(x, g, b):
            mu = x.mean(-1, keepdims=True)
            var = ((x - mu) ** 2).mean(-1, keepdims=True)
            return (x - mu) * jax.lax.rsqrt(var + LN_EPS) * g + b

        def _forward(x, edge_index, W_gat, att_src, att_dst, b_gat, ln_gamma, ln_beta, W1, b1, W2, b2):
            Bc, Nc, Dc = x.shape
            M = Bc * Nc
            x_flat = x.reshape(M, Dc)
            h = (x_flat @ W_gat).reshape(M, HEADS, NUM_EXPERTS)
            loops = jnp.arange(M, dtype=edge_index.dtype)
            src = jnp.concatenate([edge_index[0], loops])
            dst = jnp.concatenate([edge_index[1], loops])
            a_src = (h * att_src).sum(-1)
            a_dst = (h * att_dst).sum(-1)
            e = jax.nn.leaky_relu(a_src[src] + a_dst[dst], negative_slope=0.2)
            e_max = jax.ops.segment_max(e, dst, num_segments=M)
            ee = jnp.exp(e - e_max[dst])
            denom = jax.ops.segment_sum(ee, dst, num_segments=M)
            alpha = ee / (denom[dst] + 1e-16)
            msg = h[src] * alpha[:, :, None]
            agg = jax.ops.segment_sum(msg, dst, num_segments=M).reshape(M, HEADS * NUM_EXPERTS) + b_gat
            scores = _layernorm(agg, ln_gamma, ln_beta).reshape(M, HEADS, NUM_EXPERTS).mean(1)
            scores = scores.reshape(Bc, Nc, NUM_EXPERTS)
            topk_s, topk_i = jax.lax.top_k(scores, TOP_K)
            w = jax.nn.softmax(topk_s, axis=-1)
            out = jnp.zeros_like(x)
            for ei in range(NUM_EXPERTS):
                g = jnp.where(topk_i == ei, w, 0.0).sum(-1)
                hh = jax.nn.gelu(x @ W1[ei] + b1[ei], approximate=False)
                out = out + g[..., None] * (hh @ W2[ei] + b2[ei])
            return out
        key = jax.random.key(seed)
        ks = jax.random.split(key, 8)
        s = 0.05
        return {'x': jax.random.normal(ks[0], (B, N, D), jnp.float32), 'W_gat': jax.random.normal(ks[1], (D, HEADS * NUM_EXPERTS), jnp.float32) * s, 'att_src': jax.random.normal(ks[2], (HEADS, NUM_EXPERTS), jnp.float32) * s, 'att_dst': jax.random.normal(ks[3], (HEADS, NUM_EXPERTS), jnp.float32) * s, 'b_gat': jnp.zeros((HEADS * NUM_EXPERTS,), jnp.float32), 'ln_gamma': jnp.ones((HEADS * NUM_EXPERTS,), jnp.float32), 'ln_beta': jnp.zeros((HEADS * NUM_EXPERTS,), jnp.float32), 'W1': jax.random.normal(ks[4], (NUM_EXPERTS, D, 2 * D), jnp.float32) * s, 'b1': jnp.zeros((NUM_EXPERTS, 2 * D), jnp.float32), 'W2': jax.random.normal(ks[5], (NUM_EXPERTS, 2 * D, D), jnp.float32) * s, 'b2': jnp.zeros((NUM_EXPERTS, D), jnp.float32), 'edge_index': jax.random.randint(ks[6], (2, N_EDGES), 0, B * N, jnp.int32)}
    _L1_ffn_all = _L1_ffn_setup()
    _L1_ffn_in = {k: v for k, v in _L1_ffn_all.items() if k in ('W_gat', 'att_src', 'att_dst', 'b_gat', 'ln_gamma', 'ln_beta', 'W1', 'b1', 'W2', 'b2', 'edge_index')}
    del _L1_ffn_all
    return {'x': x, 'L0_tok_emb': _L0_tok_in['emb'], 'L0_attn_Q': _L0_attn_in['Q'], 'L0_attn_K': _L0_attn_in['K'], 'L0_attn_VO': _L0_attn_in['VO'], 'L0_ffn_W1': _L0_ffn_in['W1'], 'L0_ffn_b1': _L0_ffn_in['b1'], 'L0_ffn_Wg': _L0_ffn_in['Wg'], 'L0_ffn_bg': _L0_ffn_in['bg'], 'L0_ffn_Wd': _L0_ffn_in['Wd'], 'L0_ffn_bd': _L0_ffn_in['bd'], 'L1_attn_Wq': _L1_attn_in['Wq'], 'L1_attn_Wk': _L1_attn_in['Wk'], 'L1_attn_Wv': _L1_attn_in['Wv'], 'L1_ffn_W_gat': _L1_ffn_in['W_gat'], 'L1_ffn_att_src': _L1_ffn_in['att_src'], 'L1_ffn_att_dst': _L1_ffn_in['att_dst'], 'L1_ffn_b_gat': _L1_ffn_in['b_gat'], 'L1_ffn_ln_gamma': _L1_ffn_in['ln_gamma'], 'L1_ffn_ln_beta': _L1_ffn_in['ln_beta'], 'L1_ffn_W1': _L1_ffn_in['W1'], 'L1_ffn_b1': _L1_ffn_in['b1'], 'L1_ffn_W2': _L1_ffn_in['W2'], 'L1_ffn_b2': _L1_ffn_in['b2'], 'L1_ffn_edge_index': _L1_ffn_in['edge_index']}

def reference(x, L0_tok_emb, L0_attn_Q, L0_attn_K, L0_attn_VO, L0_ffn_W1, L0_ffn_b1, L0_ffn_Wg, L0_ffn_bg, L0_ffn_Wd, L0_ffn_bd, L1_attn_Wq, L1_attn_Wk, L1_attn_Wv, L1_ffn_W_gat, L1_ffn_att_src, L1_ffn_att_dst, L1_ffn_b_gat, L1_ffn_ln_gamma, L1_ffn_ln_beta, L1_ffn_W1, L1_ffn_b1, L1_ffn_W2, L1_ffn_b2, L1_ffn_edge_index):
    import jax
    import jax.numpy as jnp

    def _L0_tok_ref(x, emb):
        import jax, jax.numpy as jnp
        import numpy as np
        INP_SIZE = 12500
        HIDDEN = 64
        KERNEL = 5
        WEIGHTS = jnp.array([0.1, 0.2, 0.4, 0.2, 0.1], dtype=jnp.float32)
        offsets = jnp.arange(-(KERNEL // 2), KERNEL // 2 + 1)
        idx = jnp.clip(x[..., None] + offsets, 0, INP_SIZE - 1)
        gathered = emb[idx]
        return jnp.einsum('btkh,k->bth', gathered, WEIGHTS)

    def _L0_attn_ref(x, Q, K, VO):
        import jax, jax.numpy as jnp
        import numpy as np
        from math import sqrt
        DIM = 64
        d = x.shape[-1]
        q = jnp.einsum('btd,hrd->bhtr', x, Q)
        k = jnp.einsum('bud,hrd->bhur', x, K)
        scores = jnp.einsum('bhtr,bhur->bhtu', q, k) / sqrt(d)
        attn = jax.nn.softmax(scores, axis=-1)
        ctx = jnp.einsum('bhtu,bud->bhtd', attn, x)
        out = jnp.einsum('bhtd,hde->bte', ctx, VO)
        return out

    def _L0_ffn_ref(x, W1, b1, Wg, bg, Wd, bd):
        import jax, jax.numpy as jnp
        import numpy as np
        C = 64
        HID = 256
        E = 8
        TEMP = 1.0
        orig_shape = x.shape
        xf = x.reshape(-1, orig_shape[-1])
        H = jax.nn.gelu(xf @ W1 + b1, approximate=False)
        probs = jax.nn.softmax((H @ Wg + bg) / TEMP, axis=-1)
        assign = jnp.argmax(probs, axis=-1)
        out = jnp.zeros_like(xf)
        for e in range(Wd.shape[0]):
            y = H @ Wd[e] + bd[e]
            sel = (assign == e)[:, None]
            out = out + jnp.where(sel, probs[:, e:e + 1] * y, 0.0)
        return out.reshape(orig_shape)

    def _L1_attn_ref(x, Wq, Wk, Wv):
        import jax, jax.numpy as jnp
        import numpy as np
        B, N, D = (8, 512, 64)
        q = jnp.einsum('bnd,ed->bne', x, Wq)
        k = jnp.einsum('bnd,ed->bne', x, Wk)
        v = jnp.einsum('bnd,ed->bne', x, Wv)
        energy = jnp.einsum('bqd,bkd->bqk', q, k)
        scaling = jnp.asarray(x.shape[-1] ** (-0.5), x.dtype)
        att = jax.nn.softmax(energy, axis=-1) * scaling
        out = jnp.einsum('bqk,bkv->bqv', att, v)
        return out

    def _L1_ffn_ref(x, W_gat, att_src, att_dst, b_gat, ln_gamma, ln_beta, W1, b1, W2, b2, edge_index):
        import jax, jax.numpy as jnp
        import numpy as np
        B, N, D = (16, 1024, 64)
        NUM_EXPERTS, TOP_K, HEADS = (4, 2, 4)
        N_EDGES = 262144
        LN_EPS = 1e-05

        def _layernorm(x, g, b):
            mu = x.mean(-1, keepdims=True)
            var = ((x - mu) ** 2).mean(-1, keepdims=True)
            return (x - mu) * jax.lax.rsqrt(var + LN_EPS) * g + b

        def _forward(x, edge_index, W_gat, att_src, att_dst, b_gat, ln_gamma, ln_beta, W1, b1, W2, b2):
            Bc, Nc, Dc = x.shape
            M = Bc * Nc
            x_flat = x.reshape(M, Dc)
            h = (x_flat @ W_gat).reshape(M, HEADS, NUM_EXPERTS)
            loops = jnp.arange(M, dtype=edge_index.dtype)
            src = jnp.concatenate([edge_index[0], loops])
            dst = jnp.concatenate([edge_index[1], loops])
            a_src = (h * att_src).sum(-1)
            a_dst = (h * att_dst).sum(-1)
            e = jax.nn.leaky_relu(a_src[src] + a_dst[dst], negative_slope=0.2)
            e_max = jax.ops.segment_max(e, dst, num_segments=M)
            ee = jnp.exp(e - e_max[dst])
            denom = jax.ops.segment_sum(ee, dst, num_segments=M)
            alpha = ee / (denom[dst] + 1e-16)
            msg = h[src] * alpha[:, :, None]
            agg = jax.ops.segment_sum(msg, dst, num_segments=M).reshape(M, HEADS * NUM_EXPERTS) + b_gat
            scores = _layernorm(agg, ln_gamma, ln_beta).reshape(M, HEADS, NUM_EXPERTS).mean(1)
            scores = scores.reshape(Bc, Nc, NUM_EXPERTS)
            topk_s, topk_i = jax.lax.top_k(scores, TOP_K)
            w = jax.nn.softmax(topk_s, axis=-1)
            out = jnp.zeros_like(x)
            for ei in range(NUM_EXPERTS):
                g = jnp.where(topk_i == ei, w, 0.0).sum(-1)
                hh = jax.nn.gelu(x @ W1[ei] + b1[ei], approximate=False)
                out = out + g[..., None] * (hh @ W2[ei] + b2[ei])
            return out
        return _forward(x, edge_index, W_gat, att_src, att_dst, b_gat, ln_gamma, ln_beta, W1, b1, W2, b2)
    h = _L0_tok_ref(x, L0_tok_emb)
    h = h + _L0_attn_ref(_layernorm(h, axis=-1), L0_attn_Q, L0_attn_K, L0_attn_VO)
    h = h + _L0_ffn_ref(_layernorm(h, axis=-1), L0_ffn_W1, L0_ffn_b1, L0_ffn_Wg, L0_ffn_bg, L0_ffn_Wd, L0_ffn_bd)
    h = h + _L1_attn_ref(_layernorm(h, axis=-1), L1_attn_Wq, L1_attn_Wk, L1_attn_Wv)
    h = h + _L1_ffn_ref(_layernorm(h, axis=-1), L1_ffn_W_gat, L1_ffn_att_src, L1_ffn_att_dst, L1_ffn_b_gat, L1_ffn_ln_gamma, L1_ffn_ln_beta, L1_ffn_W1, L1_ffn_b1, L1_ffn_W2, L1_ffn_b2, L1_ffn_edge_index)
    return h

_drawn_inputs = setup_inputs


def setup_inputs(seed=0):
    import zlib

    import numpy as np

    out = dict(_drawn_inputs(seed))
    spreads = {'L0_ffn_b1': (0.0, 0.652),
     'L0_ffn_bg': (0.0, 0.1),
     'L0_ffn_bd': (0.0, 0.1),
     'L1_ffn_b_gat': (0.0, 0.1),
     'L1_ffn_ln_gamma': (1.0, 0.6),
     'L1_ffn_ln_beta': (0.0, 0.794),
     'L1_ffn_b1': (0.0, 0.268),
     'L1_ffn_b2': (0.0, 0.1)}
    factors = {'L0_ffn_W1': 3.937,
     'L0_ffn_Wg': 8.0,
     'L0_ffn_Wd': 3.8,
     'L1_ffn_att_src': 25.216,
     'L1_ffn_att_dst': 37.352}
    for name, (base, spread) in spreads.items():
        noise = np.random.default_rng([zlib.crc32(name.encode()), seed]).standard_normal(out[name].shape)
        drawn = base * np.exp(spread * noise) if base else spread * noise
        out[name] = jnp.asarray(drawn.astype(out[name].dtype))
    for name, factor in factors.items():
        out[name] = (out[name] * factor).astype(out[name].dtype)
    return out
```

```python
from contextlib import ExitStack

import concourse.bass as bass
from concourse import mybir

F32 = mybir.dt.float32
BF16 = mybir.dt.bfloat16
I32 = mybir.dt.int32
ALU = mybir.AluOpType
ACT = mybir.ActivationFunctionType
X = mybir.AxisListType.X

P = 128
BIG = 1.0e30

NODE_BITS = 13
KEY_BASE = 0x40000000


class Store:
    pass


class Shapes:

    def __init__(self, x, emb, q, w1, wd, w1x, edge_index):
        self.rows, self.steps = x.shape
        self.vocab, self.dim = emb.shape
        self.heads, self.rank, _ = q.shape
        self.hidden = w1.shape[1]
        self.experts0 = wd.shape[0]
        self.experts1, _, self.hidden1 = w1x.shape
        self.edges = edge_index.shape[1]
        self.nodes = self.rows * self.steps
        self.cols = self.nodes // P
        self.tiles = self.steps // P
        self.per_part = self.edges // P
        self.group_t = 64
        self.groups = self.edges // (P * self.group_t)
        self.query_cols = 17
        assert self.nodes == 1 << NODE_BITS and self.edges == 1 << 18
        assert self.rows * self.query_cols * P > 2 * self.nodes


class Core:

    def __init__(self, nc, ctx):
        self.nc, self.ctx = nc, ctx
        self.sems = {}

    def sb(self, name, shape, dt=F32, ctx=None):
        return (ctx or self.ctx).enter_context(self.nc.sbuf_tensor(name, shape, dt))

    def ps(self, name, shape, ctx):
        return ctx.enter_context(self.nc.psum_tensor(name, shape, F32))

    def sem(self, name):
        assert name not in self.sems
        self.sems[name] = self.ctx.enter_context(self.nc.semaphore(name))
        return self.sems[name]

    def dram(self, name, shape, dt=F32):
        return self.nc.dram_tensor(name, shape, dt, kind="Internal").ap()

    def clear(self, sems, gathers=()):
        with self.nc.Block() as block:
            @block.sync
            def _(sp):
                for s in sems:
                    sp.sem_clear(s)

            @block.gpsimd
            def _(pool):
                for s in gathers:
                    pool.dma_reset(range(s.num, s.num + 1))
                    pool.sem_clear(s)


def gather(pool, out, table, index):
    return pool.indirect_dma_start(out=out, out_offset=None, in_=table,
                                   in_offset=bass.IndirectOffsetOnAxis(ap=index, axis=0))


def load_weights(core, s, m, w):
    nc = core.nc
    H, R, D = s.heads, s.rank, s.dim
    per = P // R
    groups = H // per
    hc = s.hidden // P
    n1 = s.experts1
    sb = core.sb
    m.ident = sb("ident", [P, P])
    m.wqT = sb("wqT", [D, groups, P])
    m.wkT = sb("wkT", [D, groups, P])
    m.vo = sb("vo", [D, H, D])
    m.w1 = sb("w1", [D, s.hidden])
    m.b1 = sb("b1", [P, hc])
    m.wg = sb("wg", [P, hc, s.experts0])
    m.bg = sb("bg", [P, s.experts0])
    m.wd = sb("wd", [P, hc, s.experts0, D])
    m.bd = sb("bd", [P, s.experts0, D])
    m.wq1T = sb("wq1T", [D, D])
    m.wk1T = sb("wk1T", [D, D])
    m.wv1T = sb("wv1T", [D, D])
    m.wnode = sb("wnode", [D, 24])
    m.bgat = sb("bgat", [P, 16])
    m.gamma = sb("gamma", [P, 16])
    m.beta = sb("beta", [P, 16])
    m.w1x = sb("w1x", [D, n1, s.hidden1])
    m.b1x = sb("b1x", [P, n1])
    m.w2x = sb("w2x", [P, n1, D])
    m.b2x = sb("b2x", [P, n1, D])
    m.first_slot = sb("first_slot", [P, 8])
    m.minus_half = sb("minus_half", [P, s.cols])
    m.iota_t = sb("iota_t", [P, 8], I32)
    m.part_sign = sb("part_sign", [P, 1])
    m.query = sb("query", [P, s.rows, s.query_cols], I32)
    m.tok = sb("tok", [P, s.cols], I32)

    weights_in = core.sem("weights_in")
    raw_in = core.sem("raw_in")
    ident_made = core.sem("ident_made")
    turned = core.sem("turned")
    unturned = core.sem("unturned")
    toks_float = core.sem("toks_float")
    with ExitStack() as ctx:
        qraw = sb("qraw", [P, 2, groups, D], F32, ctx)
        raw1 = sb("raw1", [D, 3, D], F32, ctx)
        att = sb("att", [D, 2, 4, 4], F32, ctx)
        prod = sb("prod", [D, 2, 4, 4], F32, ctx)
        tok_in = sb("tok_in", [s.cols, P], I32, ctx)
        tok_f = sb("tok_f", [s.cols, P], F32, ctx)
        pidx = sb("pidx", [P, 1], I32, ctx)
        turn_ps = core.ps("turn_ps", [P, 8, 512], ctx)
        with nc.Block() as block:
            @block.sync
            def _(sp):
                for g in range(groups):
                    for i, a in enumerate((w["L0_attn_Q"], w["L0_attn_K"])):
                        sp.dma_start(qraw[:, i, g, :], a.rearrange("(g h) r d -> g (h r) d", g=groups)[g]).then_inc(raw_in, 16)
                for i, a in enumerate((w["L1_attn_Wq"], w["L1_attn_Wk"], w["L1_attn_Wv"])):
                    sp.dma_start(raw1[:, i, :], a).then_inc(raw_in, 16)
                sp.dma_start(tok_in[:], w["x"].rearrange("b (c p) -> (b c) p", p=P)).then_inc(raw_in, 16)
                sp.dma_start(m.wnode[:, 0:16], w["L1_ffn_W_gat"]).then_inc(raw_in, 16)
                for i, a in enumerate((w["L1_ffn_att_src"], w["L1_ffn_att_dst"])):
                    sp.dma_start(att[:, i, :, :].rearrange("p a b -> p (a b)"),
                                 a.rearrange("(o h) e -> o (h e)", o=1).to_broadcast([D, 16])).then_inc(raw_in, 16)
                sp.dma_start(m.vo[:], w["L0_attn_VO"].rearrange("h d e -> d h e")).then_inc(weights_in, 16)
                sp.dma_start(m.w1[:], w["L0_ffn_W1"]).then_inc(weights_in, 16)
                sp.dma_start(m.wg[:], w["L0_ffn_Wg"].rearrange("(c p) e -> p c e", p=P)).then_inc(weights_in, 16)
                for c in range(hc):
                    sp.dma_start(m.wd[:, c, :, :], w["L0_ffn_Wd"].rearrange("e (c p) d -> c p e d", p=P)[c]).then_inc(weights_in, 16)
                sp.dma_start(m.w1x[:], w["L1_ffn_W1"].rearrange("e d f -> d e f")).then_inc(weights_in, 16)
                sp.dma_start(m.w2x[:], w["L1_ffn_W2"].rearrange("e f d -> f e d")).then_inc(weights_in, 16)
                rows = ((m.bg[:], w["L0_ffn_bg"]), (m.bgat[:], w["L1_ffn_b_gat"]), (m.gamma[:], w["L1_ffn_ln_gamma"]),
                        (m.beta[:], w["L1_ffn_ln_beta"]))
                for to, a in rows:
                    sp.dma_start(to, a.rearrange("(o n) -> o n", o=1).to_broadcast([P, a.shape[0]])).then_inc(weights_in, 16)
                for to, a in ((m.bd, w["L0_ffn_bd"]), (m.b2x, w["L1_ffn_b2"])):
                    sp.dma_start(to[:].rearrange("p e d -> p (e d)"),
                                 a.rearrange("(o e) d -> o (e d)", o=1).to_broadcast([P, a.shape[0] * D])).then_inc(weights_in, 16)
                with nc.allow_non_contiguous_dma(reason="bias columns, a few hundred elements"):
                    sp.dma_start(m.b1[:], w["L0_ffn_b1"].rearrange("(c p) -> p c", p=P)).then_inc(weights_in, 16)
                    sp.dma_start(m.b1x[:], w["L1_ffn_b1"].rearrange("e p -> p e")).then_inc(weights_in, 16)
                sp.wait_ge(weights_in, 16 * (6 + hc + 4 + 2 + 2 - 1))

            @block.gpsimd
            def _(pool):
                pool.memset(m.ident[:], 0.0)
                pool.memset(m.minus_half[:], -0.5)
                pool.iota(m.iota_t[:], [[-1, 8]], base=8, channel_multiplier=0)
                pool.iota(pidx[:], [[0, 1]], base=0, channel_multiplier=1)
                pool.iota(m.query[:], [[P * s.query_cols, s.rows], [P, s.query_cols]], base=0, channel_multiplier=1)
                pool.drain()
                pool.affine_select(out=m.ident[:], in_=m.ident[:], compare_op=ALU.not_equal, fill=1.0, base=0,
                                   pattern=[[-1, P]], channel_multiplier=1).then_inc(ident_made, 1)

            @block.tensor
            def _(pe):
                pe.wait_ge(ident_made, 1)
                pe.wait_ge(toks_float, 1)
                pe.wait_ge(raw_in, 16 * (2 * groups + 7))
                n = 0
                for i in range(2):
                    for g in range(groups):
                        pe.transpose(turn_ps[0:D, n, 0:P], qraw[:, i, g, :], m.ident[:]).then_inc(turned, 1)
                        n += 1
                for i in range(3):
                    pe.transpose(turn_ps[0:D, n, 0:D], raw1[:, i, :], m.ident[0:D, 0:D]).then_inc(turned, 1)
                    n += 1
                pe.transpose(turn_ps[:, n, 0:s.cols], tok_f[:], m.ident[0:s.cols, 0:s.cols]).then_inc(turned, 1)

            @block.vector
            def _(v):
                v.wait_ge(raw_in, 16 * (2 * groups + 7))
                v.tensor_copy(tok_f[:], tok_in[:]).then_inc(toks_float, 1)
                v.tensor_tensor(prod[:], att[:], m.wnode[:, 0:16].rearrange("p (h e) -> p h e", h=4)[:, None, :, :].to_broadcast([D, 2, 4, 4]), ALU.mult)
                v.drain()
                v.tensor_reduce(m.wnode[:, 16:24].rearrange("p (i h) -> p i h", i=2), prod[:], X, ALU.add)
                v.wait_ge(ident_made, 1)
                v.tensor_copy(m.first_slot[:], m.iota_t[:])
                v.tensor_scalar(pidx[:], pidx[:], 1, None, ALU.bitwise_and)
                v.tensor_scalar(m.query[:], m.query[:], NODE_BITS, KEY_BASE, ALU.logical_shift_left, ALU.bitwise_or)
                v.drain()
                v.tensor_scalar(m.part_sign[:], pidx[:], -2.0, 1.0, ALU.mult, ALU.add)
                v.wait_ge(turned, 2 * groups + 4)
                n = 0
                for to, scale in ((m.wqT, s.dim ** -0.5), (m.wkT, 1.0)):
                    for g in range(groups):
                        v.tensor_scalar(to[:, g, :], turn_ps[0:D, n, 0:P], scale, None, ALU.mult)
                        n += 1
                for to in (m.wq1T, m.wk1T, m.wv1T):
                    v.tensor_copy(to[:], turn_ps[0:D, n, 0:D])
                    n += 1
                v.tensor_copy(m.tok[:], turn_ps[:, n, 0:s.cols])


def embed_and_sort(core, s, m, w):
    nc = core.nc
    D = s.dim
    parts = 125
    per = s.vocab // parts
    smooth = core.dram("smooth", [s.vocab, D])
    m.keys = core.dram("keys", [s.edges // 32, 32], I32)
    m.keys_before = core.dram("keys_before", [s.edges + P], I32)
    m.pivot_row = core.dram("pivot_row", [1, P], I32)
    m.pivots = core.dram("pivots", [P, 64], I32)
    m.h = core.sb("h", [P, s.cols, D])
    m.pivot1 = core.sb("pivot1", [P, P], I32)
    F = s.per_part
    table_in = core.sem("table_in")
    pair_summed = core.sem("pair_summed")
    smoothed = core.sem("smoothed")
    smooth_out = core.sem("smooth_out")
    tokens_in = core.sem("tokens_in")
    edges_in = core.sem("edges_in")
    stored = core.sem("stored")
    turn_wanted = core.sem("turn_wanted")
    turn_made = core.sem("turn_made")
    half_copied = core.sem("half_copied")
    ready_to_turn = core.sem("ready_to_turn")
    sorted_ = core.sem("sorted")
    keys_out = core.sem("keys_out")
    pivot_in = core.sem("pivot_in")
    TURNS = 14
    with ExitStack() as ctx:
        halo = core.sb("halo", [parts, per + 4, D], F32, ctx)
        pair = core.sb("pair", [parts, per, D], F32, ctx)
        acc = core.sb("acc", [parts, per, D], F32, ctx)
        ends = core.sb("ends", [P, 2, F], I32, ctx)
        buf = [core.sb(f"sort{i}", [P, F], F32, ctx) for i in range(2)]
        ibuf = [b[:].bitcast(I32) for b in buf]
        first = core.sb("first", [P, 64], F32, ctx)
        sentinel = core.sb("sentinel", [1, 1], I32, ctx)
        turn_ps = core.ps("sort_ps", [P, 4, 512], ctx)

        with nc.Block() as block:
            @block.sync
            def _(sp):
                sp.dma_start(ends[:], w["L1_ffn_edge_index"].rearrange("i (p f) -> p i f", p=P)).then_inc(edges_in, 16)
                rows = w["L0_tok_emb"].rearrange("(p r) d -> p r d", p=parts)
                sp.dma_start(halo[:, 2:per + 2, :], rows).then_inc(table_in, 16)
                sp.dma_start(halo[1:parts, 0:2, :], rows[0:parts - 1, per - 2:per, :]).then_inc(table_in, 16)
                sp.dma_start(halo[0:parts - 1, per + 2:per + 4, :], rows[1:parts, 0:2, :]).then_inc(table_in, 16)
                for r in range(2):
                    sp.dma_start(halo[0:1, r, :], w["L0_tok_emb"][0:1, :]).then_inc(table_in, 16)
                    sp.dma_start(halo[parts - 1:parts, per + 2 + r, :], w["L0_tok_emb"][s.vocab - 1:s.vocab, :]).then_inc(table_in, 16)
                sp.wait_ge(smoothed, 1)
                sp.dma_start(smooth.rearrange("(p r) d -> p r d", p=parts), acc[:]).then_inc(smooth_out, 16)
                sp.wait_ge(sorted_, 1)
                sp.dma_start(m.keys.rearrange("(p b) f -> p (b f)", p=P), ibuf[0]).then_inc(keys_out, 16)
                sp.dma_start(m.keys_before[1:s.edges + 1].rearrange("(p f) -> p f", p=P), ibuf[0]).then_inc(keys_out, 16)
                sp.dma_start(m.keys_before[0:1].rearrange("(o n) -> o n", o=1), sentinel[:]).then_inc(keys_out, 16)
                sp.dma_start(m.pivots, first[:].bitcast(I32)).then_inc(keys_out, 16)
                with nc.allow_non_contiguous_dma(reason="one key a partition"):
                    sp.dma_start(m.pivot_row.rearrange("o p -> p o"), first[:, 0:1].bitcast(I32)).then_inc(pivot_in, 16)
                sp.wait_ge(pivot_in, 16)
                sp.dma_start(m.pivot1[:], m.pivot_row.to_broadcast([P, P])).then_inc(pivot_in, 16)
                sp.wait_ge(pivot_in, 32)
                sp.wait_ge(keys_out, 64)

            @block.gpsimd
            def _(pool):
                pool.wait_ge(table_in, 16 * 7)
                pool.tensor_tensor(pair[:], halo[:, 1:per + 1, :], halo[:, 3:per + 3, :], ALU.add).then_inc(pair_summed, 1)
                pool.wait_ge(smooth_out, 16)
                for c in range(s.cols):
                    gather(pool, m.h[:, c, :], smooth, m.tok[:, c:c + 1]).then_inc(tokens_in, 16)
                pool.wait_ge(tokens_in, 16 * s.cols)

            @block.tensor
            def _(pe):
                cur = 1
                for t in range(TURNS):
                    pe.wait_ge(ready_to_turn, t + 1)
                    if t:
                        pe.wait_ge(half_copied, 2 * t)
                    src = m.turn_src[t]
                    for k in range(16):
                        last = pe.transpose(turn_ps[:, k // 4, (k % 4) * P:(k % 4 + 1) * P],
                                            buf[src][:, k * P:(k + 1) * P], m.ident[:])
                    last.then_inc(turn_made, 1)

            @block.scalar
            def _(act):
                for t in range(TURNS):
                    act.wait_ge(turn_made, t + 1)
                    act.copy(buf[1 - m.turn_src[t]][:, F // 2:F], turn_ps[:, 2:4, :].rearrange("p a b -> p (a b)")).then_inc(half_copied, 1)

            @block.vector
            def _(v):
                v.memset(sentinel[:], 0)
                v.wait_ge(edges_in, 16)
                src, dst = ends[:, 0, :], ends[:, 1, :]
                v.tensor_scalar(ibuf[0], src, s.nodes - 1, None, ALU.is_ge)
                v.tensor_scalar(ibuf[1], dst, s.nodes, NODE_BITS + 1, ALU.bitwise_and, ALU.logical_shift_left)
                v.drain()
                v.tensor_scalar(ibuf[0], ibuf[0], 2 * NODE_BITS, KEY_BASE, ALU.logical_shift_left, ALU.bitwise_or)
                v.tensor_scalar(dst, dst, s.nodes - 1, NODE_BITS, ALU.bitwise_and, ALU.logical_shift_left)
                v.tensor_scalar(src, src, s.nodes - 1, None, ALU.bitwise_and)
                v.drain()
                v.tensor_tensor(ibuf[0], ibuf[0], ibuf[1], ALU.bitwise_or)
                v.tensor_tensor(dst, dst, src, ALU.bitwise_or)
                v.drain()
                v.tensor_tensor(ibuf[0], ibuf[0], dst, ALU.bitwise_or)
                v.wait_ge(table_in, 16 * 7)
                v.tensor_tensor(acc[:], halo[:, 0:per, :], halo[:, 4:per + 4, :], ALU.add)
                v.drain()
                v.tensor_scalar(acc[:], acc[:], 0.1, None, ALU.mult)
                v.drain()
                v.wait_ge(pair_summed, 1)
                v.scalar_tensor_tensor(acc[:], pair[:], 0.2, acc[:], ALU.mult, ALU.add)
                v.drain()
                v.scalar_tensor_tensor(acc[:], halo[:, 2:per + 2, :], 0.4, acc[:], ALU.mult, ALU.add).then_inc(smoothed, 1)

                state = {"cur": 0, "turn": 0}

                def negate(part):
                    v.tensor_scalar(part, part, -1.0, None, ALU.mult)
                    v.drain()

                def compare(stride):
                    a, b = (buf[state["cur"] ^ i][:].rearrange("p (a two s) -> p a two s", two=2, s=stride) for i in (0, 1))
                    v.tensor_tensor(b[:, :, 0, :], a[:, :, 0, :], a[:, :, 1, :], ALU.min)
                    v.tensor_tensor(b[:, :, 1, :], a[:, :, 0, :], a[:, :, 1, :], ALU.max)
                    v.drain()
                    state["cur"] ^= 1

                def turn():
                    t = state["turn"]
                    v.nop().then_inc(ready_to_turn, 1)
                    v.wait_ge(turn_made, t + 1)
                    v.tensor_copy(buf[1 - state["cur"]][:, 0:F // 2], turn_ps[:, 0:2, :].rearrange("p a b -> p (a b)")).then_inc(half_copied, 1)
                    v.wait_ge(half_copied, 2 * t + 2)
                    state["cur"] ^= 1
                    state["turn"] += 1

                free_bits = F.bit_length() - 1
                part_bits = 7
                for k in range(1, free_bits + part_bits + 1):
                    cur = lambda: buf[state["cur"]][:]
                    if k == 1:
                        negate(cur().rearrange("p (a two s) -> p a two s", two=2, s=2)[:, :, 1, :])
                    elif k < free_bits:
                        negate(cur().rearrange("p (a four s) -> p a four s", four=4, s=1 << (k - 1))[:, :, 1:3, :])
                    elif k == free_bits:
                        negate(cur()[:, F // 2:F])
                        v.tensor_scalar(cur(), cur(), m.part_sign[:, 0:1], None, ALU.mult)
                        v.drain()
                    else:
                        assert m.turn_src[state["turn"]] == state["cur"]
                        turn()
                        if k < free_bits + part_bits:
                            negate(cur().rearrange("p (a four s) -> p a four s", four=4, s=1 << (k - 1 - free_bits))[:, :, 1:3, :])
                        else:
                            negate(cur().rearrange("p (a two s) -> p a two s", two=2, s=64)[:, :, 1, :])
                        for j in range(k - 1, free_bits - 1, -1):
                            compare(1 << (j - free_bits))
                        assert m.turn_src[state["turn"]] == state["cur"]
                        turn()
                    for j in range(min(k, free_bits) - 1, -1, -1):
                        compare(1 << j)
                if state["cur"]:
                    v.tensor_copy(buf[0][:], buf[1][:])
                    v.drain()
                v.tensor_copy(first[:], buf[0][:].rearrange("p (a s) -> p a s", s=32)[:, :, 0])
                v.drain()
                v.nop().then_inc(sorted_, 1)


def turn_sources(s):
    free_bits, part_bits, cur, out = s.per_part.bit_length() - 1, 7, 0, []
    for k in range(1, free_bits + part_bits + 1):
        if k > free_bits:
            out.append(cur)
            cur ^= 1
            cur ^= (k - free_bits) & 1
            out.append(cur)
            cur ^= 1
        cur ^= min(k, free_bits) & 1
    return out


class Attention:

    def __init__(self, core, s, tag, heads, rank, mem, ps):
        self.s, self.heads, self.rank, self.mem, self.ps = s, heads, rank, mem, ps
        sem = core.sem
        self.max_scored = sem(f"{tag}_max_scored")
        self.max_taken = sem(f"{tag}_max_taken")
        self.shift_ready = sem(f"{tag}_shift_ready")
        self.shift_turned = sem(f"{tag}_shift_turned")
        self.shift_placed = sem(f"{tag}_shift_placed")
        self.scored = sem(f"{tag}_scored")
        self.exped = sem(f"{tag}_exped")
        self.weighted = sem(f"{tag}_weighted")
        self.head_added = sem(f"{tag}_head_added")
        self.sems = [self.max_scored, self.max_taken, self.shift_ready, self.shift_turned, self.shift_placed,
                     self.scored, self.exped, self.weighted, self.head_added]

    def tensor(self, pe, qb, kb, qT, kT, values):
        s, T = self.s, self.s.tiles
        K = self.rank + 1
        half = s.steps // 2
        n_max = [0]

        def max_tile(h, c):
            for u in range(2):
                n = n_max[0]
                if n >= 2:
                    pe.wait_ge(self.max_taken, n - 1)
                pe.matmul(self.ps.lo[:, n % 2, :], qb(h)[:, c * P:(c + 1) * P], kb(h)[:, u * half:(u + 1) * half],
                          start=True, stop=True).then_inc(self.max_scored, 1)
                n_max[0] += 1

        def shift_row(h):
            pe.wait_ge(self.shift_ready, h + 1)
            for c in range(T):
                last = pe.matmul(self.ps.lo[0:1, c // 4, (c % 4) * P:(c % 4 + 1) * P], self.mem.shift[:, h % 2, c:c + 1],
                                 self.mem.ident[:], start=True, stop=True)
            last.then_inc(self.shift_turned, 1)

        def score(h, c):
            n = h * T + c
            if c == 0:
                pe.wait_ge(self.shift_placed, h + 1)
            if n >= 2:
                pe.wait_ge(self.exped, n - 1)
            for u in range(2):
                last = pe.matmul(self.ps.mid[:, n % 2, u * half:(u + 1) * half], kT(h)[0:K, c * P:(c + 1) * P],
                                 qT(h)[0:K, u * half:(u + 1) * half], start=True, stop=True)
            last.then_inc(self.scored, 1)

        def weigh(h, c):
            n = h * T + c
            pe.wait_ge(self.exped, n + 1)
            if c == 0 and h:
                pe.wait_ge(self.head_added, h)
            for i in range(T):
                last = pe.matmul(self.ps.hi[:, i // 4, (i % 4) * 65:(i % 4 + 1) * 65],
                                 self.mem.probs[:, n % 3, i * P:(i + 1) * P], values(h, c),
                                 start=(c == 0 and i % 4 == 0), stop=(c == T - 1), skip_group_check=True)
            last.then_inc(self.weighted, 1)

        for c in range(T):
            max_tile(0, c)
        shift_row(0)
        for h in range(self.heads):
            for c in range(T):
                score(h, c)
                if h + 1 < self.heads:
                    max_tile(h + 1, c)
                if h or c:
                    weigh(*divmod(h * T + c - 1, T))
            if h + 1 < self.heads:
                pe.wait_ge(self.shift_placed, h + 1)
                shift_row(h + 1)
        weigh(self.heads - 1, T - 1)

    def scalar(self, act):
        for n in range(self.heads * self.s.tiles):
            act.wait_ge(self.scored, n + 1)
            if n >= 3:
                act.wait_ge(self.weighted, n - 2)
            act.activation(self.mem.probs[:, n % 3, :], self.ps.mid[:, n % 2, :], ACT.Exp).then_inc(self.exped, 1)

    def vector(self, v, qT, residual, scale):
        s, T = self.s, self.s.tiles
        mem = self.mem

        def maxima(h):
            for c in range(T):
                for u in range(2):
                    n = (h * T + c) * 2 + u
                    v.wait_ge(self.max_scored, n + 1)
                    v.tensor_reduce(mem.maxima[:, h % 2, c, u:u + 1], self.ps.lo[:, n % 2, :], X, ALU.max).then_inc(self.max_taken, 1)
            v.drain()
            v.tensor_reduce(mem.shift[:, h % 2, :], mem.maxima[:, h % 2, :, :], X, ALU.max, negate=True).then_inc(self.shift_ready, 1)
            v.wait_ge(self.shift_turned, h + 1)
            v.tensor_copy(qT(h)[self.rank:self.rank + 1, :], self.ps.lo[0:1, :, :].rearrange("p a b -> p (a b)")).then_inc(self.shift_placed, 1)

        def add(h):
            v.wait_ge(self.weighted, (h + 1) * T)
            for b in range(2):
                ctx = self.ps.hi[:, b, 0:4 * 65].rearrange("p (i e) -> p i e", e=65)
                v.reciprocal(mem.recip[:, b, :], ctx[:, :, 64])
            v.drain()
            if scale != 1.0:
                v.tensor_scalar(mem.recip[:], mem.recip[:], scale, None, ALU.mult)
                v.drain()
            for b in range(2):
                ctx = self.ps.hi[:, b, 0:4 * 65].rearrange("p (i e) -> p i e", e=65)
                v.tensor_tensor(mem.part[:, 4 * b:4 * b + 4, :], ctx[:, :, 0:64],
                                mem.recip[:, b, :, None].to_broadcast([P, 4, 64]), ALU.mult)
            v.drain()
            v.nop().then_inc(self.head_added, 1)
            v.tensor_tensor(residual, residual, mem.part[:], ALU.add)
            v.drain()

        maxima(0)
        for h in range(self.heads):
            if h + 1 < self.heads:
                maxima(h + 1)
            add(h)


def tower(core, s, m, w):
    nc = core.nc
    T, D, H, R = s.tiles, s.dim, s.heads, s.rank
    half = s.steps // 2
    per = P // R
    groups = H // per
    hc = s.hidden // P
    NE = s.experts0
    QC = s.query_cols
    m.x4T = core.sb("x4T", [D, s.nodes])
    m.node = core.sb("node", [P, s.cols, 24])
    m.starts = core.sb("starts", [P, s.rows, QC])
    sem = core.sem
    names = ("lnd", "powed", "normed", "turned", "taken", "logits_ready", "projected", "staged", "a_took", "v_took", "v_scored", "v_placed",
             "values_set", "hidden_scored", "hidden_taken", "gate_scored", "routed_scored", "routed_taken",
             "nodes_scored", "turn_taken", "row_done", "piv_ready", "blk_ready")
    q = {n: sem("tw_" + n) for n in names}
    piv_in = sem("tw_piv_in")
    blk_in = sem("tw_blk_in")

    with ExitStack() as ctx:
        sb = lambda name, shape, dt=F32: core.sb("tw_" + name, shape, dt, ctx)
        xln = sb("xln", [P, T, D])
        sq = sb("sq", [P, T, D])
        stat = sb("stat", [P, 4, T])
        xT = sb("xT", [D, s.steps])
        qT = sb("qT", [P, H, s.steps])
        probs = sb("probs", [P, 3, s.steps])
        staged = probs[:, 0:2, :]
        kT = sb("kT", [R + 1, H, s.steps])
        qb = sb("qb", [P, groups, s.steps], BF16)
        kb = sb("kb", [P, groups, s.steps], BF16)
        V = sb("V", [P, T, H, 65])
        q1T = qT[:, 0, :]
        k1T = qT[:, 1, :]
        HT = qT[:, 2:2 + hc, :]
        logit = sb("logit", [P, T, NE])
        gate = sb("gate", [P, T, NE])
        small = sb("small", [P, 4, T])
        mixed = sb("mixed", [P, 2, NE, D])
        picked = sb("picked", [P, 2, D])
        piv2 = sb("piv2", [P, QC, 64], I32)
        blk = sb("blk", [P, QC, 32], I32)
        cmp = sb("cmp", [P, QC, P])
        where = sb("where", [P, 3, QC])
        row_i = sb("row_i", [P, QC], I32)
        blk_i = sb("blk_i", [P, QC], I32)
        mem = Store()
        mem.ident, mem.probs = m.ident, probs
        mem.maxima = sb("maxima", [P, 2, T, 2])
        mem.shift = sb("shift", [P, 2, T])
        mem.recip = sb("recip", [P, 2, 4])
        mem.part = sb("part", [P, T, D])
        ps = Store()
        ps.lo = core.ps("lo", [P, 2, 512], ctx)
        ps.mid = core.ps("mid", [P, 2, 1024], ctx)
        ps.hi = core.ps("hi", [P, 2, 512], ctx)
        a0 = Attention(core, s, "a0", H, R, mem, ps)
        a1 = Attention(core, s, "a1", 1, D, mem, ps)

        with nc.Block() as block:
            @block.vector
            def _(v):
                v.memset(kT[R:R + 1, :, :], 1.0)
                v.memset(k1T[D:D + 1, :], 1.0)
                v.memset(V[:, :, :, 64:65], 1.0)

        with nc.Fori(0, s.rows) as b:
            cols = bass.ts(b, T)
            with nc.Block() as block:
                @block.gpsimd
                def _(pool):
                    def inverse_root(n):
                        pool.wait_ge(q["lnd"], n)
                        pool.drain()
                        pool.tensor_scalar(stat[:, 2, :], stat[:, 1, :], 1.0 / D, 1e-5, ALU.mult, ALU.add)
                        pool.drain()
                        pool.tensor_tensor(stat[:, 3, :], stat[:, 2, :], m.minus_half[:, 0:T], ALU.pow).then_inc(q["powed"], 1)

                    inverse_root(1)
                    pool.wait_ge(q["piv_ready"], 1)
                    for j in range(QC):
                        gather(pool, piv2[:, j, :], m.pivots, row_i[:, j:j + 1]).then_inc(piv_in, 16)
                    pool.wait_ge(q["blk_ready"], 1)
                    for j in range(QC):
                        gather(pool, blk[:, j, :], m.keys, blk_i[:, j:j + 1]).then_inc(blk_in, 16)
                    pool.wait_ge(piv_in, 16 * QC)
                    pool.wait_ge(blk_in, 16 * QC)
                    for n in range(2, 5):
                        inverse_root(n)

                @block.tensor
                def _(pe):
                    def turn(n, slot, free):
                        pe.wait_ge(q["normed"], n)
                        for sem_, value in free:
                            pe.wait_ge(sem_, value)
                        for c in range(T):
                            last = pe.transpose(ps.mid[0:D, slot, c * P:(c + 1) * P], xln[:, c, :], m.ident[:])
                        last.then_inc(q["turned"], 1)

                    def wide(out, left, right):
                        for u in range(2):
                            last = pe.matmul(out[:, u * half:(u + 1) * half], left, right[:, u * half:(u + 1) * half],
                                             start=True, stop=True)
                        return last

                    turn(1, 0, ())
                    pe.wait_ge(q["turn_taken"], 1)
                    for g in range(groups):
                        for i, wT in enumerate((m.wqT, m.wkT)):
                            n = 2 * g + i
                            if n >= 2:
                                pe.wait_ge(q["staged"], n - 1)
                            wide(ps.mid[:, n % 2, :], wT[:, g, :], xT).then_inc(q["projected"], 1)
                    for c in range(T):
                        if c >= 2:
                            pe.wait_ge(q["v_placed"], c - 1)
                        pe.matmul(ps.hi[:, c % 2, :], xT[:, c * P:(c + 1) * P], m.vo[:].rearrange("d h e -> d (h e)"),
                                  start=True, stop=True).then_inc(q["v_scored"], 1)
                    pe.wait_ge(q["a_took"], 2 * groups)
                    pe.wait_ge(q["v_took"], 2 * groups)
                    pe.wait_ge(q["v_placed"], T)
                    a0.tensor(pe, lambda h: qb[R * (h % per):R * (h % per) + R, h // per, :],
                              lambda h: kb[R * (h % per):R * (h % per) + R, h // per, :],
                              lambda h: qT[:, h, :], lambda h: kT[:, h, :], lambda h, c: V[:, c, h, :])

                    turn(2, 0, ())
                    pe.wait_ge(q["turn_taken"], 2)
                    for c in range(hc):
                        wide(ps.mid[:, c % 2, :], m.w1[:, c * P:(c + 1) * P], xT).then_inc(q["hidden_scored"], 1)
                    pe.wait_ge(q["hidden_taken"], hc)
                    for c in range(T):
                        for k in range(hc):
                            last = pe.matmul(ps.lo[:, 0, c * NE:(c + 1) * NE], HT[:, k, c * P:(c + 1) * P], m.wg[:, k, :],
                                             start=(k == 0), stop=(k == hc - 1))
                    last.then_inc(q["gate_scored"], 1)
                    for c in range(T):
                        if c >= 2:
                            pe.wait_ge(q["routed_taken"], c - 1)
                        for k in range(hc):
                            last = pe.matmul(ps.hi[:, c % 2, :], HT[:, k, c * P:(c + 1) * P],
                                             m.wd[:, k, :, :].rearrange("p e d -> p (e d)"), start=(k == 0), stop=(k == hc - 1))
                        last.then_inc(q["routed_scored"], 1)

                    turn(3, 0, ())
                    pe.wait_ge(q["turn_taken"], 3)
                    wide(ps.mid[0:D, 1, :], m.wq1T[:], xT).then_inc(q["projected"], 1)
                    wide(ps.mid[0:D, 0, :], m.wk1T[:], xT).then_inc(q["projected"], 1)
                    for c in range(T):
                        last = pe.matmul(ps.hi[:, 0, c * D:(c + 1) * D], xT[:, c * P:(c + 1) * P], m.wv1T[:], start=True, stop=True)
                    last.then_inc(q["v_scored"], 1)
                    pe.wait_ge(q["v_took"], 2 * groups + 2)
                    pe.wait_ge(q["v_placed"], T + 1)
                    a1.tensor(pe, lambda h: qb[0:D, 0, :], lambda h: kb[0:D, 0, :], lambda h: q1T, lambda h: k1T,
                              lambda h, c: V[:, c, 0, :])

                    turn(4, 0, ())
                    pe.wait_ge(q["turn_taken"], 4)
                    for c in range(T):
                        last = pe.matmul(ps.hi[:, 0, c * 24:(c + 1) * 24], xT[:, c * P:(c + 1) * P], m.wnode[:], start=True, stop=True)
                    last.then_inc(q["nodes_scored"], 1)

                @block.scalar
                def _(act):
                    def take_turn(n):
                        act.wait_ge(q["turned"], n)
                        act.copy(xT[:], ps.mid[0:D, 0, :]).then_inc(q["turn_taken"], 1)

                    take_turn(1)
                    for n in range(2 * groups):
                        act.wait_ge(q["projected"], n + 1)
                        to = kT if n % 2 else qT
                        if n >= 2:
                            act.wait_ge(q["v_took"], n - 1)
                        act.copy(staged[:, n % 2, :], ps.mid[:, n % 2, :]).then_inc(q["staged"], 1)
                        act.drain()
                        for j in range(per // 2):
                            last = act.copy(to[0:R, per * (n // 2) + j, :], staged[R * j:R * j + R, n % 2, :])
                        last.then_inc(q["a_took"], 1)
                    act.wait_ge(q["v_scored"], T)
                    a0.scalar(act)

                    take_turn(2)
                    for c in range(hc):
                        act.wait_ge(q["hidden_scored"], c + 1)
                        act.activation(HT[:, c, :], ps.mid[:, c % 2, :], ACT.Gelu, bias=m.b1[:, c:c + 1]).then_inc(q["hidden_taken"], 1)
                    act.wait_ge(q["logits_ready"], 1)
                    act.activation(logit[:], logit[:], ACT.Exp).then_inc(q["taken"], 1)

                    take_turn(3)
                    for n, to in enumerate((q1T, k1T)):
                        act.wait_ge(q["projected"], 2 * groups + n + 1)
                        act.copy(to[0:D, :], ps.mid[0:D, 1 - n, :]).then_inc(q["staged"], 1)
                    a1.scalar(act)

                    take_turn(4)
                    act.drain()
                    act.copy(m.x4T[:, bass.ts(b, s.steps)], xT[:])

                @block.vector
                def _(v):
                    res = m.h[:, cols, :]

                    def norm(n):
                        v.tensor_reduce(stat[:, 0, :], res, X, ALU.add)
                        v.drain()
                        v.tensor_scalar(stat[:, 0, :], stat[:, 0, :], 1.0 / D, None, ALU.mult)
                        v.drain()
                        v.tensor_tensor(xln[:], res, stat[:, 0, :, None].to_broadcast([P, T, D]), ALU.subtract)
                        v.drain()
                        v.tensor_tensor(sq[:], xln[:], xln[:], ALU.mult)
                        v.drain()
                        v.tensor_reduce(stat[:, 1, :], sq[:], X, ALU.add)
                        v.drain()
                        v.nop().then_inc(q["lnd"], 1)
                        v.wait_ge(q["powed"], n)
                        v.tensor_tensor(xln[:], xln[:], stat[:, 3, :, None].to_broadcast([P, T, D]), ALU.mult).then_inc(q["normed"], 1)

                    query = m.query[:, bass.ts(b, 1), :].rearrange("p a b -> p (a b)")
                    v.tensor_tensor(cmp[:], m.pivot1[:].bitcast(F32)[:, None, :].to_broadcast([P, QC, P]),
                                    query.bitcast(F32)[:, :, None].to_broadcast([P, QC, P]), ALU.is_lt)
                    v.drain()
                    v.tensor_reduce(where[:, 0, :], cmp[:], X, ALU.add)
                    v.drain()
                    v.tensor_scalar(where[:, 0, :], where[:, 0, :], 1.0, 0.0, ALU.subtract, ALU.max)
                    v.drain()
                    v.tensor_copy(row_i[:], where[:, 0, :]).then_inc(q["piv_ready"], 1)
                    norm(1)

                    for n in range(2 * groups):
                        v.wait_ge(q["staged"], n + 1)
                        to = kT if n % 2 else qT
                        v.tensor_copy((kb if n % 2 else qb)[:, n // 2, :], staged[:, n % 2, :])
                        for j in range(per // 2, per):
                            last = v.tensor_copy(to[0:R, per * (n // 2) + j, :], staged[R * j:R * j + R, n % 2, :])
                        last.then_inc(q["v_took"], 1)
                    for c in range(T):
                        v.wait_ge(q["v_scored"], c + 1)
                        v.tensor_copy(V[:, c, :, 0:64], ps.hi[:, c % 2, :].rearrange("p (h e) -> p h e", e=D)).then_inc(q["v_placed"], 1)
                    v.wait_ge(piv_in, 16 * QC)
                    v.tensor_tensor(cmp[:, :, 0:64], piv2[:].bitcast(F32), query.bitcast(F32)[:, :, None].to_broadcast([P, QC, 64]), ALU.is_lt)
                    v.drain()
                    v.tensor_reduce(where[:, 1, :], cmp[:, :, 0:64], X, ALU.add)
                    v.drain()
                    v.tensor_scalar(where[:, 1, :], where[:, 1, :], 1.0, 0.0, ALU.subtract, ALU.max)
                    v.drain()
                    v.scalar_tensor_tensor(where[:, 1, :], where[:, 0, :], 64.0, where[:, 1, :], ALU.mult, ALU.add)
                    v.drain()
                    v.tensor_copy(blk_i[:], where[:, 1, :]).then_inc(q["blk_ready"], 1)

                    a0.vector(v, lambda h: qT[:, h, :], res, 1.0)
                    v.wait_ge(blk_in, 16 * QC)
                    v.tensor_tensor(cmp[:, :, 0:32], blk[:].bitcast(F32), query.bitcast(F32)[:, :, None].to_broadcast([P, QC, 32]), ALU.is_lt)
                    v.drain()
                    v.tensor_reduce(where[:, 2, :], cmp[:, :, 0:32], X, ALU.add)
                    v.drain()
                    v.scalar_tensor_tensor(m.starts[:, bass.ts(b, 1), :].rearrange("p a b -> p (a b)"), where[:, 1, :], 32.0,
                                           where[:, 2, :], ALU.mult, ALU.add)

                    norm(2)
                    v.wait_ge(q["gate_scored"], 1)
                    v.tensor_tensor(logit[:], ps.lo[:, 0, 0:T * NE].rearrange("p (c e) -> p c e", e=NE),
                                    m.bg[:, None, :].to_broadcast([P, T, NE]), ALU.add)
                    v.drain()
                    v.tensor_reduce(small[:, 0, :], logit[:], X, ALU.max)
                    v.drain()
                    v.tensor_tensor(logit[:], logit[:], small[:, 0, :, None].to_broadcast([P, T, NE]), ALU.subtract)
                    v.drain()
                    v.nop().then_inc(q["logits_ready"], 1)
                    v.wait_ge(q["taken"], 1)
                    v.tensor_reduce(small[:, 1, :], logit[:], X, ALU.add)
                    v.drain()
                    v.reciprocal(small[:, 1, :], small[:, 1, :])
                    v.drain()
                    v.tensor_tensor(logit[:], logit[:], small[:, 1, :, None].to_broadcast([P, T, NE]), ALU.mult)
                    v.drain()
                    v.tensor_reduce(small[:, 2, :], logit[:], X, ALU.max)
                    v.drain()
                    v.tensor_tensor(gate[:], logit[:], small[:, 2, :, None].to_broadcast([P, T, NE]), ALU.is_equal)
                    v.drain()
                    v.tensor_tensor(gate[:], gate[:], m.first_slot[:, None, 0:NE].to_broadcast([P, T, NE]), ALU.mult)
                    v.drain()
                    v.tensor_reduce(small[:, 3, :], gate[:], X, ALU.max)
                    v.drain()
                    v.tensor_tensor(gate[:], gate[:], small[:, 3, :, None].to_broadcast([P, T, NE]), ALU.is_equal)
                    v.drain()
                    v.tensor_tensor(gate[:], gate[:], logit[:], ALU.mult)
                    v.drain()
                    for c in range(T):
                        v.wait_ge(q["routed_scored"], c + 1)
                        v.tensor_tensor(mixed[:, c % 2, :, :], ps.hi[:, c % 2, :].rearrange("p (e d) -> p e d", d=D), m.bd[:], ALU.add).then_inc(q["routed_taken"], 1)
                        v.drain()
                        v.tensor_tensor(mixed[:, c % 2, :, :], mixed[:, c % 2, :, :], gate[:, c, :, None].to_broadcast([P, NE, D]), ALU.mult)
                        v.drain()
                        v.tensor_reduce(mem.part[:, c, :], mixed[:, c % 2, :, :].rearrange("p e d -> p d e"), X, ALU.add)
                    v.drain()
                    v.tensor_tensor(res, res, mem.part[:], ALU.add)
                    v.drain()

                    norm(3)
                    for n, (to, of) in enumerate(((qb, q1T), (kb, k1T))):
                        v.wait_ge(q["staged"], 2 * groups + n + 1)
                        v.tensor_copy(to[0:D, 0, :], of[0:D, :]).then_inc(q["v_took"], 1)
                    v.wait_ge(q["v_scored"], T + 1)
                    v.tensor_copy(V[:, :, 0, 0:64], ps.hi[:, 0, :].rearrange("p (c e) -> p c e", e=D)).then_inc(q["v_placed"], 1)
                    a1.vector(v, lambda h: q1T, res, D ** -0.5)

                    norm(4)
                    v.wait_ge(q["nodes_scored"], 1)
                    v.tensor_copy(m.node[:, cols, :], ps.hi[:, 0, 0:T * 24].rearrange("p (c f) -> p c f", f=24))

            core.clear(list(q.values()) + a0.sems + a1.sems, (piv_in, blk_in))


def node_tables(core, s, m):
    nc = core.nc
    C = s.cols
    m.table = core.dram("table", [s.nodes, 24])
    m.dst_table = core.dram("dst_table", [s.nodes, 4])
    start_line = core.dram("start_line", [s.rows * s.query_cols * P])
    m.dst_line = core.dram("dst_line", [s.edges, 4])
    m.begin = core.sb("begin", [P, 2, C])
    m.after = core.sb("after", [P, 2, C])
    m.last_row = core.sb("last_row", [P, 24])
    sem = core.sem
    rows_built = sem("rows_built")
    written = sem("tables_written")
    zeroed = sem("line_zeroed")
    starts_turned = sem("starts_turned")
    starts_placed = sem("starts_placed")
    starts_written = sem("starts_written")
    starts_read = sem("starts_read")
    runs_turned = sem("runs_turned")
    place_ready = sem("place_ready")
    scattered = sem("scattered")
    NQ = s.rows * s.query_cols
    with ExitStack() as ctx:
        sb = lambda name, shape, dt=F32: core.sb("nt_" + name, shape, dt, ctx)
        rows = sb("rows", [P, C, 24])
        zeros = sb("zeros", [P, 1024])
        startsT = sb("startsT", [P, 2, P])
        line = sb("line", [2 * C, 2, P])
        place = sb("place", [P, C])
        place_i = sb("place_i", [P, C], I32)
        empty = sb("empty", [P, C])
        ps = core.ps("nt_ps", [P, 4, 512], ctx)
        with nc.Block() as block:
            @block.vector
            def _(v):
                v.memset(zeros[:], 0.0).then_inc(rows_built, 1)
                heads = rows[:, :, 0:20].rearrange("p c (h f) -> p c h f", f=5)
                for h in range(4):
                    v.tensor_copy(rows[:, :, 5 * h:5 * h + 4], m.node[:, :, 4 * h:4 * h + 4])
                    v.memset(rows[:, :, 5 * h + 4:5 * h + 5], 1.0)
                v.tensor_copy(rows[:, :, 20:24], m.node[:, :, 16:20])
                v.drain()
                v.nop().then_inc(rows_built, 1)
                v.wait_ge(starts_turned, 1)
                v.tensor_copy(startsT[:, 0, :], ps[:, 0, 0:P])
                v.tensor_copy(startsT[0:NQ - P, 1, :], ps[0:NQ - P, 0, P:2 * P]).then_inc(starts_placed, 1)
                v.wait_ge(runs_turned, 1)
                v.tensor_copy(m.begin[:].rearrange("p i c -> p (i c)"), ps[:, 1, 0:2 * C])
                v.tensor_copy(m.after[:].rearrange("p i c -> p (i c)"), ps[:, 1, 2 * C:4 * C])
                v.drain()
                v.tensor_tensor(empty[:], m.begin[:, 0, :], m.after[:, 0, :], ALU.is_equal)
                v.drain()
                v.scalar_tensor_tensor(place[:], empty[:], 2.0 * s.edges, m.begin[:, 0, :], ALU.mult, ALU.add)
                v.drain()
                v.tensor_copy(place_i[:], place[:]).then_inc(place_ready, 1)

            @block.tensor
            def _(pe):
                flat = m.starts[:].rearrange("p b j -> p (b j)")
                pe.transpose(ps[:, 0, 0:P], flat[:, 0:P], m.ident[:])
                pe.transpose(ps[0:NQ - P, 0, P:2 * P], flat[:, P:NQ], m.ident[:]).then_inc(starts_turned, 1)
                pe.wait_ge(starts_read, 32)
                pe.transpose(ps[:, 1, 0:2 * C], line[:, 0, :], m.ident[:])
                pe.transpose(ps[:, 1, 2 * C:4 * C], line[:, 1, :], m.ident[:]).then_inc(runs_turned, 1)

            @block.sync
            def _(sp):
                sp.wait_ge(rows_built, 1)
                for i in range(8):
                    sp.dma_start(m.dst_line.rearrange("(i p r) f -> i p (r f)", i=8, p=P)[i], zeros[:]).then_inc(zeroed, 16)
                sp.wait_ge(rows_built, 2)
                sp.dma_start(m.table.rearrange("(c p) f -> p c f", p=P), rows[:]).then_inc(written, 16)
                sp.dma_start(m.dst_table.rearrange("(c p) f -> p c f", p=P), m.node[:, :, 20:24]).then_inc(written, 16)
                sp.wait_ge(starts_placed, 1)
                sp.dma_start(start_line[0:P * P].rearrange("(c p) -> c p", p=P), startsT[:, 0, :]).then_inc(starts_written, 16)
                sp.dma_start(start_line[P * P:NQ * P].rearrange("(c p) -> c p", p=P), startsT[0:NQ - P, 1, :]).then_inc(starts_written, 16)
                sp.wait_ge(starts_written, 32)
                sp.dma_start(line[:, 0, :], start_line[0:2 * s.nodes].rearrange("(c p) -> c p", p=P)).then_inc(starts_read, 16)
                sp.dma_start(line[:, 1, :], start_line[1:2 * s.nodes + 1].rearrange("(c p) -> c p", p=P)).then_inc(starts_read, 16)
                sp.wait_ge(written, 32)
                sp.dma_start(m.last_row[:], m.table[s.nodes - 1:s.nodes, :].to_broadcast([P, 24])).then_inc(written, 16)
                sp.wait_ge(written, 48)

            @block.gpsimd
            def _(pool):
                pool.wait_ge(place_ready, 1)
                pool.wait_ge(zeroed, 16 * 8)
                for c in range(C):
                    pool.indirect_dma_start(out=m.dst_line, out_offset=bass.IndirectOffsetOnAxis(ap=place_i[:, c:c + 1], axis=0),
                                            in_=m.node[:, c, 20:24], in_offset=None, bounds_check=s.edges - 1,
                                            oob_is_err=False).then_inc(scattered, 16)
                pool.wait_ge(scattered, 16 * C)


def edges(core, s, m, w):
    nc = core.nc
    TT, G = s.group_t, s.groups
    NX = s.experts1
    D = s.dim
    m.results = core.dram("results", [s.edges, 24])
    m.row_sum = core.sb("row_sum", [P, G, 20])
    m.row_max = core.sb("row_max", [P, G, 4])
    m.row_open = core.sb("row_open", [P, G])
    m.expert = core.sb("expert", [P, s.cols, NX, D])
    sem = core.sem
    keys_in = sem("ed_keys_in")
    fills_in = sem("ed_fills_in")
    stored = sem("ed_stored")
    src_ready = sem("ed_src_ready")
    gathered = sem("ed_gathered")
    row_dst_in = sem("ed_row_dst_in")
    logits_ready = sem("ed_logits_ready")
    exped = sem("ed_exped")
    row_built = sem("ed_row_built")
    hid_scored = sem("ed_hid_scored")
    hid_taken = sem("ed_hid_taken")
    exp_scored = sem("ed_exp_scored")
    tokens_copied = sem("ed_tokens_copied")
    CPG = s.cols // G
    with ExitStack() as ctx:
        sb = lambda name, shape, dt=F32: core.sb("ed_" + name, shape, dt, ctx)
        key = sb("key", [P, TT], I32)
        before = sb("before", [P, TT], I32)
        src = sb("src", [P, TT], I32)
        run = sb("run", [P, 2, TT], I32)
        row_dst = sb("row_dst", [P, 1], I32)
        row_fill = sb("row_fill", [P, 4])
        fill = sb("fill", [P, TT, 4])
        got = sb("got", [P, TT, 24])
        start = sb("start", [P, TT])
        carry = sb("carry", [P, TT])
        reset = sb("reset", [P, 4, TT])
        carry4 = sb("carry4", [P, 4, TT])
        fillT = sb("fillT", [P, 4, TT])
        dstT = sb("dstT", [P, 4, TT])
        z = sb("z", [P, 4, TT])
        e = sb("e", [P, 4, TT])
        mx = sb("mx", [P, 4, TT])
        arg = sb("arg", [P, 2, 4, TT])
        weight = sb("weight", [P, 4, TT])
        decay = sb("decay", [P, 20, TT])
        msg = sb("msg", [P, 20, TT])
        acc = sb("acc", [P, 20, TT])
        rowout = sb("rowout", [P, TT, 24])
        one = sb("one", [P, 4])
        hidden_in = sb("hidden_in", [D, CPG * P])
        hid = sb("hid", [P, NX, CPG * P])
        ps_h = core.ps("ed_ps_h", [P, NX, 512], ctx)
        ps_y = core.ps("ed_ps_y", [P, 2, 512], ctx)

        with nc.Fori(0, G) as g:
            with nc.Block() as block:
                @block.sync
                def _(sp):
                    sp.dma_start(key[:], m.keys.rearrange("(g p a) f -> g p (a f)", g=G, p=P)[bass.ts(g, 1)].rearrange("o p t -> (o p) t")).then_inc(keys_in, 16)
                    sp.dma_start(before[:], m.keys_before[0:s.edges].rearrange("(g p t) -> g p t", g=G, p=P)[bass.ts(g, 1)].rearrange("o p t -> (o p) t")).then_inc(keys_in, 16)
                    sp.dma_start(fill[:], m.dst_line.rearrange("(g p t) f -> g p t f", g=G, p=P)[bass.ts(g, 1)].rearrange("o p t f -> (o p) t f")).then_inc(fills_in, 16)
                    sp.wait_ge(row_built, 1)
                    sp.dma_start(m.results.rearrange("(g p t) f -> g p t f", g=G, p=P)[bass.ts(g, 1)].rearrange("o p t f -> (o p) t f"), rowout[:]).then_inc(stored, 16)
                    sp.wait_ge(stored, 16)

                @block.gpsimd
                def _(pool):
                    pool.wait_ge(src_ready, 1)
                    gather(pool, row_fill[:], m.dst_table, row_dst[:]).then_inc(row_dst_in, 16)
                    for t in range(TT):
                        gather(pool, got[:, t, :], m.table, src[:, t:t + 1]).then_inc(gathered, 16)
                    pool.wait_ge(row_dst_in, 16)
                    pool.wait_ge(gathered, 16 * TT)

                @block.tensor
                def _(pe):
                    pe.wait_ge(tokens_copied, 1)
                    for k in range(NX):
                        last = pe.matmul(ps_h[:, k, 0:CPG * P], m.w1x[:, k, :], hidden_in[:], start=True, stop=True)
                    last.then_inc(hid_scored, 1)
                    pe.wait_ge(hid_taken, 1)
                    for c in range(CPG):
                        for k in range(NX):
                            last = pe.matmul(ps_y[:, c, k * D:(k + 1) * D], hid[:, k, c * P:(c + 1) * P], m.w2x[:, k, :],
                                             start=True, stop=True)
                    last.then_inc(exp_scored, 1)

                @block.scalar
                def _(act):
                    act.copy(hidden_in[:], m.x4T[:, bass.ts(g, CPG * P)]).then_inc(tokens_copied, 1)
                    act.wait_ge(hid_scored, 1)
                    for k in range(NX):
                        last = act.activation(hid[:, k, :], ps_h[:, k, 0:CPG * P], ACT.Gelu, bias=m.b1x[:, k:k + 1])
                    last.then_inc(hid_taken, 1)
                    act.wait_ge(logits_ready, 1)
                    act.activation(weight[:], arg[:, 0], ACT.Exp)
                    act.activation(decay[:].rearrange("p (h f) t -> p h f t", f=5),
                                   arg[:, 1, :, None, :].to_broadcast([P, 4, 5, TT]), ACT.Exp).then_inc(exped, 1)

                @block.vector
                def _(v):
                    v.wait_ge(keys_in, 32)
                    v.tensor_scalar(src[:], key[:], s.nodes - 1, None, ALU.bitwise_and)
                    v.tensor_scalar(run[:, 0, :], key[:], NODE_BITS, None, ALU.logical_shift_right)
                    v.tensor_scalar(run[:, 1, :], before[:], NODE_BITS, None, ALU.logical_shift_right)
                    v.drain()
                    v.tensor_scalar(row_dst[:], run[:, 0, 0:1], s.nodes - 1, None, ALU.bitwise_and)
                    v.drain()
                    v.nop().then_inc(src_ready, 1)
                    v.tensor_tensor(start[:], run[:, 0, :], run[:, 1, :], ALU.not_equal)
                    v.drain()
                    v.tensor_scalar(carry[:], start[:], -1.0, 1.0, ALU.mult, ALU.add)
                    v.tensor_reduce(one[:, 0:1], start[:], X, ALU.max)
                    v.drain()
                    v.tensor_scalar(m.row_open[:, bass.ts(g, 1)], one[:, 0:1], -BIG, None, ALU.mult)
                    v.tensor_copy(one[:, 1:2], carry[:, 0:1])
                    v.drain()
                    v.memset(carry[:, 0:1], 0.0)
                    v.drain()
                    v.tensor_copy(carry4[:], carry[:, None, :].to_broadcast([P, 4, TT]))
                    v.wait_ge(fills_in, 16)
                    v.tensor_copy(fillT[:], fill[:].rearrange("p t f -> p f t"))
                    v.drain()
                    v.tensor_scalar(reset[:], carry4[:], BIG, -BIG, ALU.mult, ALU.add)
                    v.wait_ge(row_dst_in, 16)
                    v.scalar_tensor_tensor(fillT[:, :, 0], row_fill[:], one[:, 1:2], fillT[:, :, 0], ALU.mult, ALU.add)
                    v.drain()
                    flat = lambda a: a[:].rearrange("p h t -> p (h t)")
                    v.tensor_tensor_scan(flat(dstT), flat(carry4), flat(fillT), 0.0, ALU.mult, ALU.add)
                    v.wait_ge(exp_scored, 1)
                    v.tensor_tensor(m.expert[:, bass.ts(g, CPG), :, :].rearrange("p c e d -> p c (e d)"), ps_y[:, :, 0:NX * D],
                                    m.b2x[:].rearrange("p e d -> p (e d)")[:, None, :].to_broadcast([P, CPG, NX * D]), ALU.add)
                    v.drain()
                    v.wait_ge(gathered, 16 * TT)
                    v.tensor_tensor(z[:], dstT[:], got[:, :, 20:24].rearrange("p t f -> p f t"), ALU.add)
                    v.drain()
                    v.scalar_tensor_tensor(flat(e), flat(z), 0.2, flat(z), ALU.mult, ALU.max)
                    v.drain()
                    v.tensor_tensor_scan(flat(mx), flat(reset), flat(e), 0.0, ALU.add, ALU.max)
                    v.drain()
                    v.tensor_tensor(arg[:, 0], e[:], mx[:], ALU.subtract)
                    v.tensor_copy(arg[:, 1, :, 0:1], reset[:, :, 0:1])
                    v.tensor_tensor(z[:, :, 1:TT], mx[:, :, 0:TT - 1], mx[:, :, 1:TT], ALU.subtract)
                    v.drain()
                    v.tensor_tensor(arg[:, 1, :, 1:TT], z[:, :, 1:TT], reset[:, :, 1:TT], ALU.add)
                    v.drain()
                    v.nop().then_inc(logits_ready, 1)
                    v.wait_ge(exped, 1)
                    v.tensor_tensor(msg[:].rearrange("p (h f) t -> p h f t", f=5),
                                    got[:, :, 0:20].rearrange("p t (h f) -> p h f t", f=5),
                                    weight[:, :, None, :].to_broadcast([P, 4, 5, TT]), ALU.mult)
                    v.drain()
                    v.tensor_tensor_scan(flat(acc), flat(decay), flat(msg), 0.0, ALU.mult, ALU.add)
                    v.drain()
                    v.tensor_copy(rowout[:, :, 0:20], acc[:].rearrange("p f t -> p t f"))
                    v.tensor_copy(rowout[:, :, 20:24], mx[:].rearrange("p f t -> p t f"))
                    v.tensor_copy(m.row_sum[:, bass.ts(g, 1), :], acc[:, :, TT - 1:TT].rearrange("p f o -> p o f"))
                    v.tensor_copy(m.row_max[:, bass.ts(g, 1), :], mx[:, :, TT - 1:TT].rearrange("p f o -> p o f"))
                    v.drain()
                    v.nop().then_inc(row_built, 1)

            core.clear([keys_in, fills_in, stored, src_ready, logits_ready, exped, row_built, hid_scored,
                        hid_taken, exp_scored, tokens_copied], (row_dst_in, gathered))


def finish(core, s, m, w, out):
    nc = core.nc
    G, C, D, NX, TT = s.groups, s.cols, s.dim, s.experts1, s.group_t
    rows = G * P
    carried = core.dram("carried", [rows + 1, 24])
    sem = core.sem
    packed = sem("fi_packed")
    turned = sem("fi_turned")
    v_taken = sem("fi_v_taken")
    a_taken = sem("fi_a_taken")
    exp_wanted = sem("fi_exp_wanted")
    exped = sem("fi_exped")
    chained = sem("fi_chained")
    turned_back = sem("fi_turned_back")
    carry_built = sem("fi_carry_built")
    carry_out = sem("fi_carry_out")
    place_ready = sem("fi_place_ready")
    runs_in = sem("fi_runs_in")
    carries_in = sem("fi_carries_in")
    variance = sem("fi_variance")
    powed = sem("fi_powed")
    out_ready = sem("fi_out_ready")
    out_stored = sem("fi_out_stored")
    with ExitStack() as ctx:
        sb = lambda name, shape, dt=F32: core.sb("fi_" + name, shape, dt, ctx)
        value = [sb(f"value{i}", [P, C, 24]) for i in range(2)]
        place = sb("place", [P, 3, C])
        place_i = sb("place_i", [P, 3, C], I32)
        with ExitStack() as ctx2:
            sb2 = lambda name, shape, dt=F32: core.sb("fi_" + name, shape, dt, ctx2)
            pack = sb2("pack", [P, G, 96])
            sums = m.x4T[0:20, 0:rows]
            maxs = m.x4T[0:20, rows:2 * rows]
            decay = sb2("decay", [20, rows])
            chain = sb2("chain", [20, rows])
            carry = sb2("carry", [P, G, 24])
            zero = sb2("zero", [1, 24])
            ps = core.ps("fi_ps", [P, 4, 512], ctx2)
            ps_back = core.ps("fi_back", [P, 4, 512], ctx2)
            per_round = 8
            rounds = G // per_round
            with nc.Block() as block:
                @block.sync
                def _(sp):
                    sp.wait_ge(carry_built, 1)
                    sp.dma_start(carried[0:1, :], zero[:]).then_inc(carry_out, 16)
                    sp.dma_start(carried[1:rows + 1, :].rearrange("(g p) f -> p g f", p=P), carry[:]).then_inc(carry_out, 16)
                    sp.wait_ge(carry_out, 32)

                @block.gpsimd
                def _(pool):
                    pool.wait_ge(place_ready, 1)
                    for c in range(C):
                        gather(pool, value[0][:, c, :], m.results, place_i[:, 0, c:c + 1]).then_inc(runs_in, 16)
                    pool.wait_ge(carry_out, 32)
                    for c in range(C):
                        gather(pool, value[1][:, c, :], carried, place_i[:, 1, c:c + 1]).then_inc(carries_in, 16)
                    pool.wait_ge(runs_in, 16 * C)
                    pool.wait_ge(carries_in, 16 * C)

                @block.tensor
                def _(pe):
                    pe.wait_ge(packed, 1)
                    for r in range(rounds):
                        if r >= 2:
                            pe.wait_ge(v_taken, r - 1)
                            pe.wait_ge(a_taken, r - 1)
                        for i in range(per_round):
                            last = pe.transpose(ps[0:96, 2 * (r % 2) + i // 4, (i % 4) * P:(i % 4 + 1) * P],
                                                pack[:, r * per_round + i, :], m.ident[:])
                        last.then_inc(turned, 1)
                    pe.wait_ge(chained, 1)
                    for i, of in enumerate((sums, chain)):
                        for g in range(G):
                            last = pe.transpose(ps_back[:, 2 * i + g // 16, (g % 16) * 20:(g % 16 + 1) * 20],
                                                of[:, g * P:(g + 1) * P], m.ident[0:20, 0:20])
                    last.then_inc(turned_back, 1)

                @block.scalar
                def _(act):
                    for r in range(rounds):
                        act.wait_ge(turned, r + 1)
                        act.wait_ge(v_taken, r + 1)
                        span = slice(r * per_round * P, (r + 1) * per_round * P)
                        bank = ps[:, 2 * (r % 2):2 * (r % 2) + 2, :].rearrange("p a b -> p (a b)")
                        act.copy(sums[:, span], bank[0:20, :]).then_inc(a_taken, 1)
                    act.wait_ge(exp_wanted, 1)
                    act.activation(maxs, maxs, ACT.Exp)
                    act.activation(decay[:], decay[:], ACT.Exp).then_inc(exped, 1)

                @block.vector
                def _(v):
                    v.memset(zero[:], 0.0)
                    v.tensor_scalar(place[:, 0, :], m.after[:, 0, :], 1.0, 0.0, ALU.subtract, ALU.max)
                    v.memset(pack[:], 0.0)
                    v.drain()
                    v.tensor_copy(place_i[:, 0, :], place[:, 0, :])
                    v.tensor_copy(pack[:, :, 0:20], m.row_sum[:])
                    v.tensor_copy(pack[:, :, 32:52].rearrange("p g (h f) -> p g h f", f=5), m.row_max[:, :, :, None].to_broadcast([P, G, 4, 5]))
                    v.tensor_copy(pack[:, :, 64:84], m.row_open[:, :, None].to_broadcast([P, G, 20]))
                    v.drain()
                    v.nop().then_inc(packed, 1)
                    v.tensor_scalar(place_i[:, 1, :], place_i[:, 0, :], TT.bit_length() - 1, None, ALU.logical_shift_right)
                    v.drain()
                    v.tensor_scalar(place_i[:, 2, :], place_i[:, 1, :], TT.bit_length() - 1, None, ALU.logical_shift_left)
                    v.nop().then_inc(place_ready, 1)
                    v.drain()
                    v.tensor_copy(place[:, 2, :], place_i[:, 2, :])
                    for r in range(rounds):
                        v.wait_ge(turned, r + 1)
                        span = slice(r * per_round * P, (r + 1) * per_round * P)
                        bank = ps[:, 2 * (r % 2):2 * (r % 2) + 2, :].rearrange("p a b -> p (a b)")
                        v.tensor_copy(maxs[:, span], bank[32:52, :])
                        v.tensor_copy(decay[:, span], bank[64:84, :]).then_inc(v_taken, 1)
                    v.drain()
                    v.tensor_tensor_scan(chain[:], decay[:], maxs, -BIG, ALU.add, ALU.max)
                    v.drain()
                    v.tensor_tensor(maxs, maxs, chain[:], ALU.subtract)
                    v.tensor_tensor(decay[:, 1:rows], decay[:, 1:rows], chain[:, 0:rows - 1], ALU.add)
                    v.drain()
                    v.tensor_tensor(decay[:, 1:rows], decay[:, 1:rows], chain[:, 1:rows], ALU.subtract)
                    v.drain()
                    v.nop().then_inc(exp_wanted, 1)
                    v.wait_ge(exped, 1)
                    v.wait_ge(a_taken, rounds)
                    v.tensor_tensor(maxs, maxs, sums, ALU.mult)
                    v.drain()
                    v.tensor_tensor_scan(sums, decay[:], maxs, 0.0, ALU.mult, ALU.add)
                    v.drain()
                    v.nop().then_inc(chained, 1)
                    v.wait_ge(turned_back, 1)
                    back = lambda i: ps_back[:, 2 * i:2 * i + 2, 0:320].rearrange("p a (g f) -> p a g f", f=20)
                    both = carry[:].rearrange("p (a g) f -> p a g f", a=2)
                    v.tensor_copy(both[:, :, :, 0:20], back(0))
                    v.tensor_copy(both[:, :, :, 20:24], back(1).rearrange("p a g (h f) -> p a g h f", f=5)[:, :, :, :, 0])
                    v.drain()
                    v.nop().then_inc(carry_built, 1)

        logit = sb("logit", [P, 4, C, 4])
        mask = sb("mask", [P, 3, C])
        count = sb("count", [P, C])
        top = sb("top", [P, C, 4])
        term = [sb(f"term{i}", [P, C, 4, 5]) for i in range(2)]
        agg = sb("agg", [P, C, 4, 4])
        sq = sb("sq", [P, C, 4, 4])
        stat = sb("stat", [P, 4, C])
        score = sb("score", [P, C, 4])
        hot = sb("hot", [P, 2, C, 4])
        gate = sb("gate", [P, C, 4])
        best = sb("best", [P, 4, C])
        one = sb("one", [P, C, 4, 5])
        last = sb("last", [P, 4, 5])
        chunk = 8
        mix = sb("mix", [P, chunk, D])
        with nc.Block() as block:
            @block.gpsimd
            def _(pool):
                pool.wait_ge(variance, 1)
                pool.drain()
                pool.tensor_scalar(stat[:, 2, :], stat[:, 1, :], 1.0 / 16, 1e-5, ALU.mult, ALU.add)
                pool.drain()
                pool.tensor_tensor(stat[:, 3, :], stat[:, 2, :], m.minus_half[:, 0:C], ALU.pow).then_inc(powed, 1)

            @block.scalar
            def _(act):
                act.wait_ge(exp_wanted, 2)
                act.activation(logit[:], logit[:], ACT.Exp).then_inc(exped, 1)
                act.wait_ge(exp_wanted, 3)
                act.activation(best[:, 2, :], best[:, 1, :], ACT.Exp).then_inc(exped, 1)

            @block.sync
            def _(sp):
                n_out = C // chunk
                rows_out = out.rearrange("b t d -> (b t) d").rearrange("(c p) d -> p c d", p=P)
                for i in range(n_out):
                    sp.wait_ge(out_ready, i + 1)
                    sp.dma_start(rows_out[:, i * chunk:(i + 1) * chunk, :], m.h[:, i * chunk:(i + 1) * chunk, :]).then_inc(out_stored, 16)
                sp.wait_ge(out_stored, 16 * n_out)

            @block.vector
            def _(v):
                wide = lambda a: a[:, :, None].to_broadcast([P, C, 4])
                v.tensor_tensor(count[:], m.after[:, 1, :], m.begin[:, 1, :], ALU.subtract)
                v.tensor_tensor(mask[:, 0, :], m.after[:, 0, :], m.begin[:, 0, :], ALU.is_gt)
                v.tensor_tensor(mask[:, 1, :], place[:, 2, :], m.begin[:, 0, :], ALU.is_gt)
                v.tensor_tensor(mask[:, 2, :], m.after[:, 1, :], m.begin[:, 1, :], ALU.is_gt)
                v.tensor_tensor(logit[:, 2], m.node[:, :, 16:20], m.node[:, :, 20:24], ALU.add)
                v.tensor_tensor(logit[:, 3], m.node[:, :, 20:24], m.last_row[:, None, 20:24].to_broadcast([P, C, 4]), ALU.add)
                v.tensor_copy(one[:, :, :, 0:4], m.node[:, :, 0:16].rearrange("p c (h f) -> p c h f", h=4))
                v.memset(one[:, :, :, 4:5], 1.0)
                v.tensor_copy(last[:], m.last_row[:, 0:20].rearrange("p (h f) -> p h f", h=4))
                v.drain()
                v.tensor_tensor(mask[:, 1, :], mask[:, 1, :], mask[:, 0, :], ALU.mult)
                v.scalar_tensor_tensor(logit[:, 2:4], logit[:, 2:4], 0.2, logit[:, 2:4], ALU.mult, ALU.max)
                v.drain()
                v.tensor_tensor(logit[:, 0], value[0][:, :, 20:24], wide(mask[:, 0, :]), ALU.mult)
                v.tensor_tensor(logit[:, 1], value[1][:, :, 20:24], wide(mask[:, 1, :]), ALU.mult)
                v.tensor_tensor(logit[:, 3], logit[:, 3], wide(mask[:, 2, :]), ALU.mult)
                v.drain()
                v.tensor_scalar(mask[:], mask[:], BIG, -BIG, ALU.mult, ALU.add)
                v.drain()
                for i, k in ((0, 0), (1, 1), (3, 2)):
                    v.tensor_tensor(logit[:, i], logit[:, i], wide(mask[:, k, :]), ALU.add)
                v.drain()
                v.tensor_reduce(top[:], logit[:].rearrange("p i c h -> p c h i"), X, ALU.max)
                v.drain()
                v.tensor_tensor(logit[:], logit[:], top[:, None, :, :].to_broadcast([P, 4, C, 4]), ALU.subtract)
                v.drain()
                v.nop().then_inc(exp_wanted, 1)
                v.wait_ge(exped, 2)
                v.tensor_tensor(logit[:, 3], logit[:, 3], wide(count[:]), ALU.mult)
                v.drain()
                weight = lambda i: logit[:, i, :, :, None].to_broadcast([P, C, 4, 5])
                rows = lambda a: a[:, :, 0:20].rearrange("p c (h f) -> p c h f", h=4)
                v.tensor_tensor(term[0][:], rows(value[0][:]), weight(0), ALU.mult)
                v.tensor_tensor(term[1][:], rows(value[1][:]), weight(1), ALU.mult)
                v.tensor_tensor(one[:], one[:], weight(2), ALU.mult)
                v.drain()
                v.tensor_tensor(term[0][:], term[0][:], term[1][:], ALU.add)
                v.drain()
                v.tensor_tensor(term[1][:], last[:, None, :, :].to_broadcast([P, C, 4, 5]), weight(3), ALU.mult)
                v.tensor_tensor(term[0][:], term[0][:], one[:], ALU.add)
                v.drain()
                v.tensor_tensor(term[0][:], term[0][:], term[1][:], ALU.add)
                v.drain()
                v.tensor_scalar(top[:], term[0][:, :, :, 4], 1e-16, None, ALU.add)
                v.drain()
                v.reciprocal(top[:], top[:])
                v.drain()
                v.tensor_tensor(agg[:], term[0][:, :, :, 0:4], top[:, :, :, None].to_broadcast([P, C, 4, 4]), ALU.mult)
                v.drain()
                flat = lambda a: a[:].rearrange("p c h f -> p c (h f)")
                row16 = lambda a: a[:, None, :].to_broadcast([P, C, 16])
                v.tensor_tensor(flat(agg), flat(agg), row16(m.bgat), ALU.add)
                v.drain()
                v.tensor_reduce(stat[:, 0, :], flat(agg), X, ALU.add)
                v.drain()
                v.tensor_scalar(stat[:, 0, :], stat[:, 0, :], 1.0 / 16, None, ALU.mult)
                v.drain()
                v.tensor_tensor(flat(agg), flat(agg), stat[:, 0, :, None].to_broadcast([P, C, 16]), ALU.subtract)
                v.drain()
                v.tensor_tensor(sq[:], agg[:], agg[:], ALU.mult)
                v.drain()
                v.tensor_reduce(stat[:, 1, :], flat(sq), X, ALU.add)
                v.drain()
                v.nop().then_inc(variance, 1)
                v.wait_ge(powed, 1)
                v.tensor_tensor(flat(agg), flat(agg), stat[:, 3, :, None].to_broadcast([P, C, 16]), ALU.mult)
                v.drain()
                v.tensor_tensor(flat(agg), flat(agg), row16(m.gamma), ALU.mult)
                v.drain()
                v.tensor_tensor(flat(agg), flat(agg), row16(m.beta), ALU.add)
                v.drain()
                v.tensor_reduce(score[:], agg[:].rearrange("p c h f -> p c f h"), X, ALU.add)
                v.drain()
                v.tensor_scalar(score[:], score[:], 0.25, None, ALU.mult)
                v.drain()
                for k in range(2):
                    v.tensor_reduce(best[:, k, :], score[:], X, ALU.max)
                    v.drain()
                    v.tensor_tensor(hot[:, k], score[:], wide(best[:, k, :]), ALU.is_equal)
                    v.drain()
                    v.tensor_tensor(hot[:, k], hot[:, k], m.first_slot[:, None, 0:4].to_broadcast([P, C, 4]), ALU.mult)
                    v.drain()
                    v.tensor_reduce(best[:, 3, :], hot[:, k], X, ALU.max)
                    v.drain()
                    v.tensor_tensor(hot[:, k], hot[:, k], wide(best[:, 3, :]), ALU.is_equal)
                    v.drain()
                    if k == 0:
                        v.scalar_tensor_tensor(score[:], hot[:, 0], -BIG, score[:], ALU.mult, ALU.add)
                        v.drain()
                v.tensor_tensor(best[:, 1, :], best[:, 1, :], best[:, 0, :], ALU.subtract)
                v.drain()
                v.nop().then_inc(exp_wanted, 1)
                v.wait_ge(exped, 3)
                v.tensor_scalar(best[:, 0, :], best[:, 2, :], 1.0, None, ALU.add)
                v.drain()
                v.reciprocal(best[:, 0, :], best[:, 0, :])
                v.drain()
                v.tensor_tensor(hot[:, 1], hot[:, 1], wide(best[:, 2, :]), ALU.mult)
                v.drain()
                v.tensor_tensor(gate[:], hot[:, 0], hot[:, 1], ALU.add)
                v.drain()
                v.tensor_tensor(gate[:], gate[:], wide(best[:, 0, :]), ALU.mult)
                v.drain()
                for i in range(C // chunk):
                    cols = slice(i * chunk, (i + 1) * chunk)
                    part = m.expert[:, cols, :, :]
                    v.tensor_tensor(part, part, gate[:, cols, :, None].to_broadcast([P, chunk, NX, D]), ALU.mult)
                    v.drain()
                    v.tensor_reduce(mix[:], part.rearrange("p c e d -> p c d e"), X, ALU.add)
                    v.drain()
                    v.tensor_tensor(m.h[:, cols, :], m.h[:, cols, :], mix[:], ALU.add).then_inc(out_ready, 1)


def build(nc, w, out):
    with ExitStack() as ctx:
        core = Core(nc, ctx)
        s = Shapes(w["x"], w["L0_tok_emb"], w["L0_attn_Q"], w["L0_ffn_W1"], w["L0_ffn_Wd"], w["L1_ffn_W1"], w["L1_ffn_edge_index"])
        m = Store()
        m.turn_src = turn_sources(s)
        load_weights(core, s, m, w)
        embed_and_sort(core, s, m, w)
        tower(core, s, m, w)
        node_tables(core, s, m)
        edges(core, s, m, w)
        finish(core, s, m, w, out)


def kernel(**inputs):
    import numpy as _np
    import concourse.bacc as _bacc
    from concourse import mybir as _mybir
    from concourse.bass_utils import run_bass_kernel_spmd as _run

    nc = _bacc.Bacc("TRN2", target_bir_lowering=False, num_devices=1)
    arrays, aps = {}, {}
    for name, value in inputs.items():
        a = _np.ascontiguousarray(value)
        arrays[f"in_{name}_dram"] = a
        aps[name] = nc.dram_tensor(f"in_{name}_dram", a.shape, _mybir.dt.from_np(a.dtype), kind="ExternalInput").ap()
    shape = tuple(inputs["x"].shape) + (inputs["L0_tok_emb"].shape[1],)
    out = nc.dram_tensor("out_0_dram", shape, _mybir.dt.float32, kind="ExternalOutput").ap()
    build(nc, aps, out)
    r = _run(nc, [arrays], core_ids=[0])
    return r.results[0]["out_0_dram"]
```

```python
from contextlib import ExitStack

import concourse.bass as bass
from concourse import mybir

F32 = mybir.dt.float32
F16 = mybir.dt.float16
I32 = mybir.dt.int32
ALU = mybir.AluOpType
ACT = mybir.ActivationFunctionType
X = mybir.AxisListType.X

P = 128
BIG = 1.0e30

NODE_BITS = 13
KEY_BASE = 0x40000000


class Store:
    pass


class Shapes:

    def __init__(self, x, emb, q, w1, wd, w1x, edge_index):
        self.rows, self.steps = x.shape
        self.vocab, self.dim = emb.shape
        self.heads, self.rank, _ = q.shape
        self.hidden = w1.shape[1]
        self.experts0 = wd.shape[0]
        self.experts1, _, self.hidden1 = w1x.shape
        self.edges = edge_index.shape[1]
        self.nodes = self.rows * self.steps
        self.cols = self.nodes // P
        self.tiles = self.steps // P
        self.per_part = self.edges // P
        self.group_t = 64
        self.groups = self.edges // (P * self.group_t)
        self.query_cols = 17
        assert self.nodes == 1 << NODE_BITS and self.edges == 1 << 18
        assert self.rows * self.query_cols * P > 2 * self.nodes


class Core:

    def __init__(self, nc, ctx):
        self.nc, self.ctx = nc, ctx
        self.sems = {}

    def sb(self, name, shape, dt=F32, ctx=None):
        return (ctx or self.ctx).enter_context(self.nc.sbuf_tensor(name, shape, dt))

    def ps(self, name, shape, ctx):
        return ctx.enter_context(self.nc.psum_tensor(name, shape, F32))

    def sem(self, name):
        assert name not in self.sems
        self.sems[name] = self.ctx.enter_context(self.nc.semaphore(name))
        return self.sems[name]

    def dram(self, name, shape, dt=F32):
        return self.nc.dram_tensor(name, shape, dt, kind="Internal").ap()

    def clear(self, sems, gathers=()):
        with self.nc.Block() as block:
            @block.sync
            def _(sp):
                for s in sems:
                    sp.sem_clear(s)

            @block.gpsimd
            def _(pool):
                for s in gathers:
                    pool.dma_reset(range(s.num, s.num + 1))
                    pool.sem_clear(s)


def gather(pool, out, table, index):
    return pool.indirect_dma_start(out=out, out_offset=None, in_=table,
                                   in_offset=bass.IndirectOffsetOnAxis(ap=index, axis=0))


def load_weights(core, s, m, w):
    nc = core.nc
    H, R, D = s.heads, s.rank, s.dim
    per = P // R
    groups = H // per
    hc = s.hidden // P
    n1 = s.experts1
    sb = core.sb
    m.ident = sb("ident", [P, P])
    m.wqT = sb("wqT", [D, H, 3, R])
    m.wkT = sb("wkT", [D, H, 3, R])
    m.vo = sb("vo", [D, H, D])
    m.w1 = sb("w1", [D, s.hidden])
    m.b1 = sb("b1", [P, hc])
    m.wg = sb("wg", [P, hc, s.experts0])
    m.bg = sb("bg", [P, s.experts0])
    m.wd = sb("wd", [P, hc, s.experts0, D])
    m.bd = sb("bd", [P, s.experts0, D])
    m.wq1T = sb("wq1T", [D, 2, D])
    m.wk1T = sb("wk1T", [D, 2, D])
    m.wv1T = sb("wv1T", [D, D])
    m.wnode = sb("wnode", [D, 24])
    m.bgat = sb("bgat", [P, 16])
    m.gamma = sb("gamma", [P, 16])
    m.beta = sb("beta", [P, 16])
    m.w1x = sb("w1x", [D, n1, s.hidden1])
    m.b1x = sb("b1x", [P, n1])
    m.w2x = sb("w2x", [P, n1, D])
    m.b2x = sb("b2x", [P, n1, D])
    m.first_slot = sb("first_slot", [P, 8])
    m.minus_half = sb("minus_half", [P, s.cols])
    m.iota_t = sb("iota_t", [P, 8], I32)
    m.part_sign = sb("part_sign", [P, 1])
    m.query = sb("query", [P, s.rows, s.query_cols], I32)
    m.tok = sb("tok", [P, s.cols], I32)

    weights_in = core.sem("weights_in")
    raw_in = core.sem("raw_in")
    ident_made = core.sem("ident_made")
    turned = core.sem("turned")
    unturned = core.sem("unturned")
    toks_float = core.sem("toks_float")
    with ExitStack() as ctx:
        qraw = sb("qraw", [P, 2, groups, D], F32, ctx)
        raw1 = sb("raw1", [D, 3, D], F32, ctx)
        att = sb("att", [D, 2, 4, 4], F32, ctx)
        prod = sb("prod", [D, 2, 4, 4], F32, ctx)
        tok_in = sb("tok_in", [s.cols, P], I32, ctx)
        tok_f = sb("tok_f", [s.cols, P], F32, ctx)
        pidx = sb("pidx", [P, 1], I32, ctx)
        turn_ps = core.ps("turn_ps", [P, 8, 512], ctx)
        with nc.Block() as block:
            @block.sync
            def _(sp):
                for g in range(groups):
                    for i, a in enumerate((w["L0_attn_Q"], w["L0_attn_K"])):
                        sp.dma_start(qraw[:, i, g, :], a.rearrange("(g h) r d -> g (h r) d", g=groups)[g]).then_inc(raw_in, 16)
                for i, a in enumerate((w["L1_attn_Wq"], w["L1_attn_Wk"], w["L1_attn_Wv"])):
                    sp.dma_start(raw1[:, i, :], a).then_inc(raw_in, 16)
                sp.dma_start(tok_in[:], w["x"].rearrange("b (c p) -> (b c) p", p=P)).then_inc(raw_in, 16)
                sp.dma_start(m.wnode[:, 0:16], w["L1_ffn_W_gat"]).then_inc(raw_in, 16)
                for i, a in enumerate((w["L1_ffn_att_src"], w["L1_ffn_att_dst"])):
                    sp.dma_start(att[:, i, :, :].rearrange("p a b -> p (a b)"),
                                 a.rearrange("(o h) e -> o (h e)", o=1).to_broadcast([D, 16])).then_inc(raw_in, 16)
                sp.dma_start(m.vo[:], w["L0_attn_VO"].rearrange("h d e -> d h e")).then_inc(weights_in, 16)
                sp.dma_start(m.w1[:], w["L0_ffn_W1"]).then_inc(weights_in, 16)
                sp.dma_start(m.wg[:], w["L0_ffn_Wg"].rearrange("(c p) e -> p c e", p=P)).then_inc(weights_in, 16)
                for c in range(hc):
                    sp.dma_start(m.wd[:, c, :, :], w["L0_ffn_Wd"].rearrange("e (c p) d -> c p e d", p=P)[c]).then_inc(weights_in, 16)
                sp.dma_start(m.w1x[:], w["L1_ffn_W1"].rearrange("e d f -> d e f")).then_inc(weights_in, 16)
                sp.dma_start(m.w2x[:], w["L1_ffn_W2"].rearrange("e f d -> f e d")).then_inc(weights_in, 16)
                rows = ((m.bg[:], w["L0_ffn_bg"]), (m.bgat[:], w["L1_ffn_b_gat"]), (m.gamma[:], w["L1_ffn_ln_gamma"]),
                        (m.beta[:], w["L1_ffn_ln_beta"]))
                for to, a in rows:
                    sp.dma_start(to, a.rearrange("(o n) -> o n", o=1).to_broadcast([P, a.shape[0]])).then_inc(weights_in, 16)
                for to, a in ((m.bd, w["L0_ffn_bd"]), (m.b2x, w["L1_ffn_b2"])):
                    sp.dma_start(to[:].rearrange("p e d -> p (e d)"),
                                 a.rearrange("(o e) d -> o (e d)", o=1).to_broadcast([P, a.shape[0] * D])).then_inc(weights_in, 16)
                with nc.allow_non_contiguous_dma(reason="bias columns, a few hundred elements"):
                    sp.dma_start(m.b1[:], w["L0_ffn_b1"].rearrange("(c p) -> p c", p=P)).then_inc(weights_in, 16)
                    sp.dma_start(m.b1x[:], w["L1_ffn_b1"].rearrange("e p -> p e")).then_inc(weights_in, 16)
                sp.wait_ge(weights_in, 16 * (6 + hc + 4 + 2 + 2 - 1))

            @block.gpsimd
            def _(pool):
                pool.memset(m.ident[:], 0.0)
                pool.memset(m.minus_half[:], -0.5)
                pool.iota(m.iota_t[:], [[-1, 8]], base=8, channel_multiplier=0)
                pool.iota(pidx[:], [[0, 1]], base=0, channel_multiplier=1)
                pool.iota(m.query[:], [[P * s.query_cols, s.rows], [P, s.query_cols]], base=0, channel_multiplier=1)
                pool.drain()
                pool.affine_select(out=m.ident[:], in_=m.ident[:], compare_op=ALU.not_equal, fill=1.0, base=0,
                                   pattern=[[-1, P]], channel_multiplier=1).then_inc(ident_made, 1)

            @block.tensor
            def _(pe):
                pe.wait_ge(ident_made, 1)
                pe.wait_ge(toks_float, 1)
                pe.wait_ge(raw_in, 16 * (2 * groups + 7))
                n = 0
                for i in range(2):
                    for g in range(groups):
                        pe.transpose(turn_ps[0:D, n, 0:P], qraw[:, i, g, :], m.ident[:]).then_inc(turned, 1)
                        n += 1
                for i in range(3):
                    pe.transpose(turn_ps[0:D, n, 0:D], raw1[:, i, :], m.ident[0:D, 0:D]).then_inc(turned, 1)
                    n += 1
                pe.transpose(turn_ps[:, n, 0:s.cols], tok_f[:], m.ident[0:s.cols, 0:s.cols]).then_inc(turned, 1)

            @block.vector
            def _(v):
                v.wait_ge(raw_in, 16 * (2 * groups + 7))
                v.tensor_copy(tok_f[:], tok_in[:]).then_inc(toks_float, 1)
                v.tensor_tensor(prod[:], att[:], m.wnode[:, 0:16].rearrange("p (h e) -> p h e", h=4)[:, None, :, :].to_broadcast([D, 2, 4, 4]), ALU.mult)
                v.drain()
                v.tensor_reduce(m.wnode[:, 16:24].rearrange("p (i h) -> p i h", i=2), prod[:], X, ALU.add)
                v.wait_ge(ident_made, 1)
                v.tensor_copy(m.first_slot[:], m.iota_t[:])
                v.tensor_scalar(pidx[:], pidx[:], 1, None, ALU.bitwise_and)
                v.tensor_scalar(m.query[:], m.query[:], NODE_BITS, KEY_BASE, ALU.logical_shift_left, ALU.bitwise_or)
                v.drain()
                v.tensor_scalar(m.part_sign[:], pidx[:], -2.0, 1.0, ALU.mult, ALU.add)
                v.wait_ge(turned, 2 * groups + 4)
                n = 0
                for to, scale in ((m.wqT, s.dim ** -0.5), (m.wkT, 1.0)):
                    for g in range(groups):
                        v.tensor_scalar(to[:, g * per:(g + 1) * per, :, :],
                                        turn_ps[0:D, n, 0:P].rearrange("d (h r) -> d h r", r=R)[:, :, None, :].to_broadcast([D, per, 3, R]),
                                        scale, None, ALU.mult)
                        n += 1
                for to, copies in ((m.wq1T, 2), (m.wk1T, 2), (m.wv1T, 1)):
                    for i in range(copies):
                        v.tensor_copy(to[:, i, :] if copies > 1 else to[:], turn_ps[0:D, n, 0:D])
                    n += 1
                v.tensor_copy(m.tok[:], turn_ps[:, n, 0:s.cols])


def embed_and_sort(core, s, m, w):
    nc = core.nc
    D = s.dim
    parts = 125
    per = s.vocab // parts
    smooth = core.dram("smooth", [s.vocab, D])
    m.keys = core.dram("keys", [s.edges // 32, 32], I32)
    m.keys_before = core.dram("keys_before", [s.edges + P], I32)
    m.pivot_row = core.dram("pivot_row", [1, P], I32)
    m.pivots = core.dram("pivots", [P, 64], I32)
    m.results = core.dram("results", [s.edges, 24])
    m.dst_line = core.dram("dst_line", [s.edges, 4])
    blank = [a.rearrange("(p r) f -> p (r f)", p=P) for a in (m.results, m.dst_line)]
    piece = 2048
    zero_made = core.sem("zero_made")
    blanked = core.sem("blanked")
    m.h = core.sb("h", [P, s.cols, D])
    m.pivot1 = core.sb("pivot1", [P, P], I32)
    F = s.per_part
    table_in = core.sem("table_in")
    pair_summed = core.sem("pair_summed")
    smoothed = core.sem("smoothed")
    smooth_out = core.sem("smooth_out")
    tokens_in = core.sem("tokens_in")
    edges_in = core.sem("edges_in")
    stored = core.sem("stored")
    turn_wanted = core.sem("turn_wanted")
    turn_made = core.sem("turn_made")
    half_copied = core.sem("half_copied")
    ready_to_turn = core.sem("ready_to_turn")
    sorted_ = core.sem("sorted")
    keys_out = core.sem("keys_out")
    pivot_in = core.sem("pivot_in")
    TURNS = 14
    with ExitStack() as ctx:
        halo = core.sb("halo", [parts, per + 4, D], F32, ctx)
        pair = core.sb("pair", [parts, per, D], F32, ctx)
        acc = core.sb("acc", [parts, per, D], F32, ctx)
        ends = core.sb("ends", [P, 2, F], I32, ctx)
        buf = [core.sb(f"sort{i}", [P, F], F32, ctx) for i in range(2)]
        ibuf = [b[:].bitcast(I32) for b in buf]
        first = core.sb("first", [P, 64], F32, ctx)
        zeros = core.sb("zeros", [P, piece], F32, ctx)
        sentinel = core.sb("sentinel", [1, 1], I32, ctx)
        turn_ps = core.ps("sort_ps", [P, 4, 512], ctx)

        with nc.Block() as block:
            @block.sync
            def _(sp):
                sp.dma_start(ends[:], w["L1_ffn_edge_index"].rearrange("i (p f) -> p i f", p=P)).then_inc(edges_in, 16)
                rows = w["L0_tok_emb"].rearrange("(p r) d -> p r d", p=parts)
                sp.dma_start(halo[:, 2:per + 2, :], rows).then_inc(table_in, 16)
                sp.dma_start(halo[1:parts, 0:2, :], rows[0:parts - 1, per - 2:per, :]).then_inc(table_in, 16)
                sp.dma_start(halo[0:parts - 1, per + 2:per + 4, :], rows[1:parts, 0:2, :]).then_inc(table_in, 16)
                for r in range(2):
                    sp.dma_start(halo[0:1, r, :], w["L0_tok_emb"][0:1, :]).then_inc(table_in, 16)
                    sp.dma_start(halo[parts - 1:parts, per + 2 + r, :], w["L0_tok_emb"][s.vocab - 1:s.vocab, :]).then_inc(table_in, 16)
                sp.wait_ge(zero_made, 1)
                for table in blank:
                    for i in range(table.shape[1] // piece):
                        sp.dma_start(table[:, i * piece:(i + 1) * piece], zeros[:]).then_inc(blanked, 16)
                sp.wait_ge(smoothed, 1)
                sp.dma_start(smooth.rearrange("(p r) d -> p r d", p=parts), acc[:]).then_inc(smooth_out, 16)
                sp.wait_ge(sorted_, 1)
                sp.dma_start(m.keys.rearrange("(p b) f -> p (b f)", p=P), ibuf[0]).then_inc(keys_out, 16)
                sp.dma_start(m.keys_before[1:s.edges + 1].rearrange("(p f) -> p f", p=P), ibuf[0]).then_inc(keys_out, 16)
                sp.dma_start(m.keys_before[0:1].rearrange("(o n) -> o n", o=1), sentinel[:]).then_inc(keys_out, 16)
                sp.dma_start(m.pivots, first[:].bitcast(I32)).then_inc(keys_out, 16)
                with nc.allow_non_contiguous_dma(reason="one key a partition"):
                    sp.dma_start(m.pivot_row.rearrange("o p -> p o"), first[:, 0:1].bitcast(I32)).then_inc(pivot_in, 16)
                sp.wait_ge(pivot_in, 16)
                sp.dma_start(m.pivot1[:], m.pivot_row.to_broadcast([P, P])).then_inc(pivot_in, 16)
                sp.wait_ge(pivot_in, 32)
                sp.wait_ge(keys_out, 64)
                sp.wait_ge(blanked, 16 * sum(table.shape[1] // piece for table in blank))

            @block.gpsimd
            def _(pool):
                pool.wait_ge(table_in, 16 * 7)
                pool.tensor_tensor(pair[:], halo[:, 1:per + 1, :], halo[:, 3:per + 3, :], ALU.add).then_inc(pair_summed, 1)
                pool.wait_ge(smooth_out, 16)
                for c in range(s.cols):
                    gather(pool, m.h[:, c, :], smooth, m.tok[:, c:c + 1]).then_inc(tokens_in, 16)
                pool.wait_ge(tokens_in, 16 * s.cols)

            @block.tensor
            def _(pe):
                cur = 1
                for t in range(TURNS):
                    pe.wait_ge(ready_to_turn, t + 1)
                    if t:
                        pe.wait_ge(half_copied, 2 * t)
                    src = m.turn_src[t]
                    for k in range(16):
                        last = pe.transpose(turn_ps[:, k // 4, (k % 4) * P:(k % 4 + 1) * P],
                                            buf[src][:, k * P:(k + 1) * P], m.ident[:])
                    last.then_inc(turn_made, 1)

            @block.scalar
            def _(act):
                for t in range(TURNS):
                    act.wait_ge(turn_made, t + 1)
                    act.copy(buf[1 - m.turn_src[t]][:, F // 2:F], turn_ps[:, 2:4, :].rearrange("p a b -> p (a b)")).then_inc(half_copied, 1)

            @block.vector
            def _(v):
                v.memset(sentinel[:], 0)
                v.memset(zeros[:], 0.0).then_inc(zero_made, 1)
                v.wait_ge(edges_in, 16)
                src, dst = ends[:, 0, :], ends[:, 1, :]
                v.tensor_scalar(ibuf[0], src, s.nodes - 1, None, ALU.is_ge)
                v.tensor_scalar(ibuf[1], dst, s.nodes, NODE_BITS + 1, ALU.bitwise_and, ALU.logical_shift_left)
                v.drain()
                v.tensor_scalar(ibuf[0], ibuf[0], 2 * NODE_BITS, KEY_BASE, ALU.logical_shift_left, ALU.bitwise_or)
                v.tensor_scalar(dst, dst, s.nodes - 1, NODE_BITS, ALU.bitwise_and, ALU.logical_shift_left)
                v.tensor_scalar(src, src, s.nodes - 1, None, ALU.bitwise_and)
                v.drain()
                v.tensor_tensor(ibuf[0], ibuf[0], ibuf[1], ALU.bitwise_or)
                v.tensor_tensor(dst, dst, src, ALU.bitwise_or)
                v.drain()
                v.tensor_tensor(ibuf[0], ibuf[0], dst, ALU.bitwise_or)
                v.wait_ge(table_in, 16 * 7)
                v.tensor_tensor(acc[:], halo[:, 0:per, :], halo[:, 4:per + 4, :], ALU.add)
                v.drain()
                v.tensor_scalar(acc[:], acc[:], 0.1, None, ALU.mult)
                v.drain()
                v.wait_ge(pair_summed, 1)
                v.scalar_tensor_tensor(acc[:], pair[:], 0.2, acc[:], ALU.mult, ALU.add)
                v.drain()
                v.scalar_tensor_tensor(acc[:], halo[:, 2:per + 2, :], 0.4, acc[:], ALU.mult, ALU.add).then_inc(smoothed, 1)

                state = {"cur": 0, "turn": 0}

                def negate(part):
                    v.tensor_scalar(part, part, -1.0, None, ALU.mult)
                    v.drain()

                def compare(stride):
                    a, b = (buf[state["cur"] ^ i][:].rearrange("p (a two s) -> p a two s", two=2, s=stride) for i in (0, 1))
                    v.tensor_tensor(b[:, :, 0, :], a[:, :, 0, :], a[:, :, 1, :], ALU.min)
                    v.tensor_tensor(b[:, :, 1, :], a[:, :, 0, :], a[:, :, 1, :], ALU.max)
                    v.drain()
                    state["cur"] ^= 1

                def turn():
                    t = state["turn"]
                    v.nop().then_inc(ready_to_turn, 1)
                    v.wait_ge(turn_made, t + 1)
                    v.tensor_copy(buf[1 - state["cur"]][:, 0:F // 2], turn_ps[:, 0:2, :].rearrange("p a b -> p (a b)")).then_inc(half_copied, 1)
                    v.wait_ge(half_copied, 2 * t + 2)
                    state["cur"] ^= 1
                    state["turn"] += 1

                free_bits = F.bit_length() - 1
                part_bits = 7
                for k in range(1, free_bits + part_bits + 1):
                    cur = lambda: buf[state["cur"]][:]
                    if k == 1:
                        negate(cur().rearrange("p (a two s) -> p a two s", two=2, s=2)[:, :, 1, :])
                    elif k < free_bits:
                        negate(cur().rearrange("p (a four s) -> p a four s", four=4, s=1 << (k - 1))[:, :, 1:3, :])
                    elif k == free_bits:
                        negate(cur()[:, F // 2:F])
                        v.tensor_scalar(cur(), cur(), m.part_sign[:, 0:1], None, ALU.mult)
                        v.drain()
                    else:
                        assert m.turn_src[state["turn"]] == state["cur"]
                        turn()
                        if k < free_bits + part_bits:
                            negate(cur().rearrange("p (a four s) -> p a four s", four=4, s=1 << (k - 1 - free_bits))[:, :, 1:3, :])
                        else:
                            negate(cur().rearrange("p (a two s) -> p a two s", two=2, s=64)[:, :, 1, :])
                        for j in range(k - 1, free_bits - 1, -1):
                            compare(1 << (j - free_bits))
                        assert m.turn_src[state["turn"]] == state["cur"]
                        turn()
                    for j in range(min(k, free_bits) - 1, -1, -1):
                        compare(1 << j)
                if state["cur"]:
                    v.tensor_copy(buf[0][:], buf[1][:])
                    v.drain()
                v.tensor_copy(first[:], buf[0][:].rearrange("p (a s) -> p a s", s=32)[:, :, 0])
                v.drain()
                v.nop().then_inc(sorted_, 1)


def turn_sources(s):
    free_bits, part_bits, cur, out = s.per_part.bit_length() - 1, 7, 0, []
    for k in range(1, free_bits + part_bits + 1):
        if k > free_bits:
            out.append(cur)
            cur ^= 1
            cur ^= (k - free_bits) & 1
            out.append(cur)
            cur ^= 1
        cur ^= min(k, free_bits) & 1
    return out


class Attention:

    LAG = 2
    PROBS = 4

    def __init__(self, core, s, tag, heads, rank, mem, ps):
        self.s, self.heads, self.rank, self.mem, self.ps = s, heads, rank, mem, ps
        sem = core.sem
        self.ring_filled = sem(f"{tag}_ring_filled")
        self.ring_free = sem(f"{tag}_ring_free")
        self.shift_ready = sem(f"{tag}_shift_ready")
        self.scored = sem(f"{tag}_scored")
        self.exped = sem(f"{tag}_exped")
        self.weighted = sem(f"{tag}_weighted")
        self.context_out = sem(f"{tag}_context_out")
        self.sems = [self.ring_filled, self.ring_free, self.shift_ready, self.scored, self.exped, self.weighted,
                     self.context_out]

    def beside(self):
        T = self.s.tiles
        for h in range(self.heads):
            done = 0
            for c in range(T):
                work = []
                if h + 1 < self.heads and c < T - 2:
                    upto = -(-T * (c + 1) // (T - 2))
                    work += [("max", h + 1, t) for t in range(done, upto)]
                    done = upto
                if h and c == 3:
                    work.append(("turn", h - 1, 0))
                if h + 1 < self.heads and c == T - 2:
                    work.append(("shift", h + 1, 0))
                yield h, c, work

    def first(self):
        return [("max", 0, t) for t in range(self.s.tiles)] + [("shift", 0, 0)]

    def tensor(self, pe, qmax, kmax, products, values):
        s, T = self.s, self.s.tiles
        half = s.steps // 2
        ring = [0]
        shift_slot = {}

        def slot(u):
            n = ring[0]
            if n >= 2:
                pe.wait_ge(self.ring_free, n - 1)
            ring[0] += 1
            return n % 2

        def do(kind, h, t):
            for u in range(2):
                if kind == "max":
                    b = slot(u)
                    pe.matmul(self.ps.lo[:, b, :], qmax(h)[:, t * P:(t + 1) * P], kmax(h)[:, u * half:(u + 1) * half],
                              start=True, stop=True).then_inc(self.ring_filled, 1)
                elif kind == "shift":
                    pe.wait_ge(self.shift_ready, h + 1)
                    b = slot(u)
                    for i in range(T // 2):
                        last = pe.matmul(self.ps.lo[0:1, b, i * P:(i + 1) * P],
                                         self.mem.shift[:, h % 2, u * T // 2 + i:u * T // 2 + i + 1],
                                         self.mem.ident[:], start=True, stop=True)
                    last.then_inc(self.ring_filled, 1)
                    shift_slot[h] = ring[0]
                else:
                    pe.wait_ge(self.context_out, h + 1)
                    b = slot(u)
                    for i in range(T // 2):
                        c = u * T // 2 + i
                        last = pe.transpose(self.ps.lo[:, b, i * 65:(i + 1) * 65],
                                            self.mem.context[:, h % 2, c * P:(c + 1) * P], self.mem.ident[0:65, 0:65])
                    last.then_inc(self.ring_filled, 1)

        def score(h, c):
            n = h * T + c
            if c == 0:
                pe.wait_ge(self.ring_free, shift_slot[h])
            if n >= 2:
                pe.wait_ge(self.exped, n - 1)
            pairs = products(h)
            for u in range(2):
                for i, (kside, qside) in enumerate(pairs):
                    last = pe.matmul(self.ps.mid[:, n % 2, u * half:(u + 1) * half], kside[:, c * P:(c + 1) * P],
                                     qside[:, u * half:(u + 1) * half], start=(i == 0), stop=(i == len(pairs) - 1))
            last.then_inc(self.scored, 1)

        def weigh(n):
            h, c = divmod(n, T)
            pe.wait_ge(self.exped, n + 1)
            if c == 0 and h:
                pe.wait_ge(self.context_out, h)
            for u in range(2):
                last = pe.matmul(self.ps.hi[0:65, u, :], values(h, c), self.mem.probs[:, n % self.PROBS, u * half:(u + 1) * half],
                                 start=(c == 0), stop=(c == T - 1))
            last.then_inc(self.weighted, 1)

        for work in self.first():
            do(*work)
        for h, c, beside in self.beside():
            score(h, c)
            for work in beside:
                do(*work)
            if h * T + c >= self.LAG:
                weigh(h * T + c - self.LAG)
        for n in range(self.heads * T - self.LAG, self.heads * T):
            weigh(n)
        do("turn", self.heads - 1, 0)

    def scalar(self, act):
        T = self.s.tiles

        def copy_out(h):
            act.wait_ge(self.weighted, (h + 1) * T)
            act.copy(self.mem.context[:, h % 2, :], self.ps.hi[0:65, :, :].rearrange("p a b -> p (a b)")).then_inc(self.context_out, 1)

        for n in range(self.heads * T):
            act.wait_ge(self.scored, n + 1)
            if n >= self.PROBS:
                act.wait_ge(self.weighted, n - self.PROBS + 1)
            act.activation(self.mem.probs[:, n % self.PROBS, :], self.ps.mid[:, n % 2, :], ACT.Exp).then_inc(self.exped, 1)
            if n >= T and n % T == self.LAG - 1:
                copy_out(n // T - 1)
        copy_out(self.heads - 1)

    def vector(self, v, shift_row, residual, scale):
        T = self.s.tiles
        half = self.s.steps // 2
        mem = self.mem
        ring = [0]

        def do(kind, h, t):
            for u in range(2):
                n = ring[0]
                ring[0] += 1
                if kind == "max":
                    v.wait_ge(self.ring_filled, n + 1)
                    v.tensor_reduce(mem.maxima[:, h % 2, t, u:u + 1], self.ps.lo[:, n % 2, :], X, ALU.max).then_inc(self.ring_free, 1)
                elif kind == "shift":
                    v.wait_ge(self.ring_filled, n + 1)
                    v.tensor_copy(shift_row(h)[:, u * half:(u + 1) * half], self.ps.lo[0:1, n % 2, :]).then_inc(self.ring_free, 1)
                else:
                    v.wait_ge(self.ring_filled, n + 1)
                    context = self.ps.lo[:, n % 2, 0:T // 2 * 65].rearrange("p (i e) -> p i e", e=65)
                    rows = slice(u * T // 2, (u + 1) * T // 2)
                    v.reciprocal(mem.recip[:, u, :], context[:, :, 64])
                    v.drain()
                    if scale != 1.0:
                        v.tensor_scalar(mem.recip[:, u, :], mem.recip[:, u, :], scale, None, ALU.mult)
                        v.drain()
                    v.tensor_tensor(mem.part[:, rows, :], context[:, :, 0:64],
                                    mem.recip[:, u, :, None].to_broadcast([P, T // 2, 64]), ALU.mult).then_inc(self.ring_free, 1)
                    v.drain()
                    v.tensor_tensor(residual[:, rows, :], residual[:, rows, :], mem.part[:, rows, :], ALU.add)
            if kind == "max" and t == T - 1:
                v.drain()
                v.tensor_reduce(mem.shift[:, h % 2, :], mem.maxima[:, h % 2, :, :], X, ALU.max, negate=True).then_inc(self.shift_ready, 1)

        for work in self.first():
            do(*work)
        for h, c, beside in self.beside():
            for work in beside:
                do(*work)
        do("turn", self.heads - 1, 0)
        v.drain()


def tower(core, s, m, w):
    nc = core.nc
    T, D, H, R = s.tiles, s.dim, s.heads, s.rank
    half = s.steps // 2
    hc = s.hidden // P
    NE = s.experts0
    QC = s.query_cols
    m.x4T = core.sb("x4T", [D, s.nodes])
    m.node = core.sb("node", [P, s.cols, 24])
    m.starts = core.sb("starts", [P, s.rows, QC])
    sem = core.sem
    names = ("lnd", "powed", "normed", "turned", "taken", "logits_ready", "projected", "a_took", "v_took", "v_scored", "v_placed",
             "values_set", "hidden_scored", "hidden_taken", "gate_scored", "routed_scored", "routed_taken",
             "nodes_scored", "turn_taken", "row_done", "piv_ready", "blk_ready")
    q = {n: sem("tw_" + n) for n in names}
    piv_in = sem("tw_piv_in")
    blk_in = sem("tw_blk_in")

    with ExitStack() as ctx:
        sb = lambda name, shape, dt=F32: core.sb("tw_" + name, shape, dt, ctx)
        xln = sb("xln", [P, T, D])
        sq = sb("sq", [P, T, D])
        stat = sb("stat", [P, 4, T])
        xT = sb("xT", [D, s.steps])
        q0 = sb("q0", [3 * R + 1, H, s.steps], F16)
        k0 = sb("k0", [3 * R + 1, H, s.steps], F16)
        q1 = sb("q1", [2 * D, s.steps], F16)
        k1 = sb("k1", [2 * D, s.steps], F16)
        q1s = sb("q1s", [D + 1, s.steps], F16)
        k1s = sb("k1s", [D + 1, s.steps], F16)
        V = sb("V", [P, T, H, 65])
        HT = sb("HT", [P, hc, s.steps])
        logit = sb("logit", [P, T, NE])
        gate = sb("gate", [P, T, NE])
        small = sb("small", [P, 4, T])
        mixed = sb("mixed", [P, 2, NE, D])
        picked = sb("picked", [P, 2, D])
        piv2 = sb("piv2", [P, QC, 64], I32)
        blk = sb("blk", [P, QC, 32], I32)
        cmp = sb("cmp", [P, QC, P])
        where = sb("where", [P, 3, QC])
        row_i = sb("row_i", [P, QC], I32)
        blk_i = sb("blk_i", [P, QC], I32)
        mem = Store()
        mem.ident = m.ident
        mem.probs = sb("probs", [P, Attention.PROBS, s.steps])
        mem.context = sb("context", [65, 2, s.steps])
        mem.maxima = sb("maxima", [P, 2, T, 2])
        mem.shift = sb("shift", [P, 2, T])
        mem.recip = sb("recip", [P, 2, 4])
        mem.part = sb("part", [P, T, D])
        ps = Store()
        ps.lo = core.ps("lo", [P, 2, 512], ctx)
        ps.mid = core.ps("mid", [P, 2, 1024], ctx)
        ps.hi = core.ps("hi", [P, 2, 512], ctx)
        a0 = Attention(core, s, "a0", H, R, mem, ps)
        a1 = Attention(core, s, "a1", 1, D, mem, ps)

        with nc.Block() as block:
            @block.vector
            def _(v):
                v.memset(k0[3 * R:3 * R + 1, :, :], 1.0)
                v.memset(k1s[D:D + 1, :], 1.0)
                v.memset(V[:, :, :, 64:65], 1.0)

        with nc.Fori(0, s.rows) as b:
            cols = bass.ts(b, T)
            with nc.Block() as block:
                @block.gpsimd
                def _(pool):
                    def inverse_root(n):
                        pool.wait_ge(q["lnd"], n)
                        pool.drain()
                        pool.tensor_scalar(stat[:, 2, :], stat[:, 1, :], 1.0 / D, 1e-5, ALU.mult, ALU.add)
                        pool.drain()
                        pool.tensor_tensor(stat[:, 3, :], stat[:, 2, :], m.minus_half[:, 0:T], ALU.pow).then_inc(q["powed"], 1)

                    inverse_root(1)
                    pool.wait_ge(q["piv_ready"], 1)
                    for j in range(QC):
                        gather(pool, piv2[:, j, :], m.pivots, row_i[:, j:j + 1]).then_inc(piv_in, 16)
                    pool.wait_ge(q["blk_ready"], 1)
                    for j in range(QC):
                        gather(pool, blk[:, j, :], m.keys, blk_i[:, j:j + 1]).then_inc(blk_in, 16)
                    pool.wait_ge(piv_in, 16 * QC)
                    pool.wait_ge(blk_in, 16 * QC)
                    for n in range(2, 5):
                        inverse_root(n)

                @block.tensor
                def _(pe):
                    def turn(n, slot, free):
                        pe.wait_ge(q["normed"], n)
                        for sem_, value in free:
                            pe.wait_ge(sem_, value)
                        for c in range(T):
                            last = pe.transpose(ps.mid[0:D, slot, c * P:(c + 1) * P], xln[:, c, :], m.ident[:])
                        last.then_inc(q["turned"], 1)

                    def wide(out, left, right):
                        for u in range(2):
                            last = pe.matmul(out[:, u * half:(u + 1) * half], left, right[:, u * half:(u + 1) * half],
                                             start=True, stop=True)
                        return last

                    turn(1, 0, ())
                    pe.wait_ge(q["turn_taken"], 1)
                    for n in range(2 * H):
                        if n >= 2:
                            pe.wait_ge(q["v_took"], n - 1)
                        wT = (m.wqT, m.wkT)[n % 2]
                        wide(ps.mid[0:3 * R, n % 2, :], wT[:, n // 2].rearrange("d a r -> d (a r)"), xT).then_inc(q["projected"], 1)
                    for c in range(T):
                        if c >= 2:
                            pe.wait_ge(q["v_placed"], c - 1)
                        pe.matmul(ps.hi[:, c % 2, :], xT[:, c * P:(c + 1) * P], m.vo[:].rearrange("d h e -> d (h e)"),
                                  start=True, stop=True).then_inc(q["v_scored"], 1)
                    pe.wait_ge(q["v_took"], 2 * H)
                    pe.wait_ge(q["v_placed"], T)
                    a0.tensor(pe, lambda h: q0[0:R, h, :], lambda h: k0[0:R, h, :], lambda h: ((k0[:, h, :], q0[:, h, :]),),
                              lambda h, c: V[:, c, h, :])

                    turn(2, 0, ())
                    pe.wait_ge(q["turn_taken"], 2)
                    for c in range(hc):
                        wide(ps.mid[:, c % 2, :], m.w1[:, c * P:(c + 1) * P], xT).then_inc(q["hidden_scored"], 1)
                    pe.wait_ge(q["hidden_taken"], hc)
                    for c in range(T):
                        for k in range(hc):
                            last = pe.matmul(ps.lo[:, 0, c * NE:(c + 1) * NE], HT[:, k, c * P:(c + 1) * P], m.wg[:, k, :],
                                             start=(k == 0), stop=(k == hc - 1))
                    last.then_inc(q["gate_scored"], 1)
                    for c in range(T):
                        if c >= 2:
                            pe.wait_ge(q["routed_taken"], c - 1)
                        for k in range(hc):
                            last = pe.matmul(ps.hi[:, c % 2, :], HT[:, k, c * P:(c + 1) * P],
                                             m.wd[:, k, :, :].rearrange("p e d -> p (e d)"), start=(k == 0), stop=(k == hc - 1))
                        last.then_inc(q["routed_scored"], 1)

                    turn(3, 0, ())
                    pe.wait_ge(q["turn_taken"], 3)
                    wide(ps.mid[:, 1, :], m.wq1T[:].rearrange("d a e -> d (a e)"), xT).then_inc(q["projected"], 1)
                    wide(ps.mid[:, 0, :], m.wk1T[:].rearrange("d a e -> d (a e)"), xT).then_inc(q["projected"], 1)
                    for c in range(T):
                        last = pe.matmul(ps.hi[:, 0, c * D:(c + 1) * D], xT[:, c * P:(c + 1) * P], m.wv1T[:], start=True, stop=True)
                    last.then_inc(q["v_scored"], 1)
                    pe.wait_ge(q["v_took"], 2 * H + 2)
                    pe.wait_ge(q["v_placed"], T + 1)
                    a1.tensor(pe, lambda h: q1[0:D, :], lambda h: k1[0:D, :], lambda h: ((k1, q1), (k1s, q1s)),
                              lambda h, c: V[:, c, 0, :])

                    turn(4, 0, ())
                    pe.wait_ge(q["turn_taken"], 4)
                    for c in range(T):
                        last = pe.matmul(ps.hi[:, 0, c * 24:(c + 1) * 24], xT[:, c * P:(c + 1) * P], m.wnode[:], start=True, stop=True)
                    last.then_inc(q["nodes_scored"], 1)

                @block.scalar
                def _(act):
                    def take_turn(n):
                        act.wait_ge(q["turned"], n)
                        act.copy(xT[:], ps.mid[0:D, 0, :]).then_inc(q["turn_taken"], 1)

                    take_turn(1)
                    for n in range(2 * H):
                        act.wait_ge(q["projected"], n + 1)
                        act.copy((q0, k0)[n % 2][0:3 * R, n // 2, :], ps.mid[0:3 * R, n % 2, :]).then_inc(q["a_took"], 1)
                    act.wait_ge(q["v_scored"], T)
                    a0.scalar(act)

                    take_turn(2)
                    for c in range(hc):
                        act.wait_ge(q["hidden_scored"], c + 1)
                        act.activation(HT[:, c, :], ps.mid[:, c % 2, :], ACT.Gelu, bias=m.b1[:, c:c + 1]).then_inc(q["hidden_taken"], 1)
                    act.wait_ge(q["logits_ready"], 1)
                    act.activation(logit[:], logit[:], ACT.Exp).then_inc(q["taken"], 1)

                    take_turn(3)
                    for n, to in enumerate((q1, k1)):
                        act.wait_ge(q["projected"], 2 * H + n + 1)
                        act.copy(to[:], ps.mid[:, 1 - n, :]).then_inc(q["a_took"], 1)
                    a1.scalar(act)

                    take_turn(4)
                    act.drain()
                    act.copy(m.x4T[:, bass.ts(b, s.steps)], xT[:])

                @block.vector
                def _(v):
                    res = m.h[:, cols, :]

                    def norm(n):
                        v.tensor_reduce(stat[:, 0, :], res, X, ALU.add)
                        v.drain()
                        v.tensor_scalar(stat[:, 0, :], stat[:, 0, :], 1.0 / D, None, ALU.mult)
                        v.drain()
                        v.tensor_tensor(xln[:], res, stat[:, 0, :, None].to_broadcast([P, T, D]), ALU.subtract)
                        v.drain()
                        v.tensor_tensor(sq[:], xln[:], xln[:], ALU.mult)
                        v.drain()
                        v.tensor_reduce(stat[:, 1, :], sq[:], X, ALU.add)
                        v.drain()
                        v.nop().then_inc(q["lnd"], 1)
                        v.wait_ge(q["powed"], n)
                        v.tensor_tensor(xln[:], xln[:], stat[:, 3, :, None].to_broadcast([P, T, D]), ALU.mult).then_inc(q["normed"], 1)

                    query = m.query[:, bass.ts(b, 1), :].rearrange("p a b -> p (a b)")
                    v.tensor_tensor(cmp[:], m.pivot1[:].bitcast(F32)[:, None, :].to_broadcast([P, QC, P]),
                                    query.bitcast(F32)[:, :, None].to_broadcast([P, QC, P]), ALU.is_lt)
                    v.drain()
                    v.tensor_reduce(where[:, 0, :], cmp[:], X, ALU.add)
                    v.drain()
                    v.tensor_scalar(where[:, 0, :], where[:, 0, :], 1.0, 0.0, ALU.subtract, ALU.max)
                    v.drain()
                    v.tensor_copy(row_i[:], where[:, 0, :]).then_inc(q["piv_ready"], 1)
                    norm(1)

                    for n in range(2 * H):
                        v.wait_ge(q["a_took"], n + 1)
                        low = (q0, k0)[n % 2][(2 - n % 2) * R:(3 - n % 2) * R, n // 2, :]
                        v.tensor_tensor(low, ps.mid[(2 - n % 2) * R:(3 - n % 2) * R, n % 2, :], low, ALU.subtract).then_inc(q["v_took"], 1)
                    for c in range(T):
                        v.wait_ge(q["v_scored"], c + 1)
                        v.tensor_copy(V[:, c, :, 0:64], ps.hi[:, c % 2, :].rearrange("p (h e) -> p h e", e=D)).then_inc(q["v_placed"], 1)
                    v.wait_ge(piv_in, 16 * QC)
                    v.tensor_tensor(cmp[:, :, 0:64], piv2[:].bitcast(F32), query.bitcast(F32)[:, :, None].to_broadcast([P, QC, 64]), ALU.is_lt)
                    v.drain()
                    v.tensor_reduce(where[:, 1, :], cmp[:, :, 0:64], X, ALU.add)
                    v.drain()
                    v.tensor_scalar(where[:, 1, :], where[:, 1, :], 1.0, 0.0, ALU.subtract, ALU.max)
                    v.drain()
                    v.scalar_tensor_tensor(where[:, 1, :], where[:, 0, :], 64.0, where[:, 1, :], ALU.mult, ALU.add)
                    v.drain()
                    v.tensor_copy(blk_i[:], where[:, 1, :]).then_inc(q["blk_ready"], 1)

                    a0.vector(v, lambda h: q0[3 * R:3 * R + 1, h, :], res, 1.0)
                    v.wait_ge(blk_in, 16 * QC)
                    v.tensor_tensor(cmp[:, :, 0:32], blk[:].bitcast(F32), query.bitcast(F32)[:, :, None].to_broadcast([P, QC, 32]), ALU.is_lt)
                    v.drain()
                    v.tensor_reduce(where[:, 2, :], cmp[:, :, 0:32], X, ALU.add)
                    v.drain()
                    v.scalar_tensor_tensor(m.starts[:, bass.ts(b, 1), :].rearrange("p a b -> p (a b)"), where[:, 1, :], 32.0,
                                           where[:, 2, :], ALU.mult, ALU.add)

                    norm(2)
                    v.wait_ge(q["gate_scored"], 1)
                    v.tensor_tensor(logit[:], ps.lo[:, 0, 0:T * NE].rearrange("p (c e) -> p c e", e=NE),
                                    m.bg[:, None, :].to_broadcast([P, T, NE]), ALU.add)
                    v.drain()
                    v.tensor_reduce(small[:, 0, :], logit[:], X, ALU.max)
                    v.drain()
                    v.tensor_tensor(logit[:], logit[:], small[:, 0, :, None].to_broadcast([P, T, NE]), ALU.subtract)
                    v.drain()
                    v.nop().then_inc(q["logits_ready"], 1)
                    v.wait_ge(q["taken"], 1)
                    v.tensor_reduce(small[:, 1, :], logit[:], X, ALU.add)
                    v.drain()
                    v.reciprocal(small[:, 1, :], small[:, 1, :])
                    v.drain()
                    v.tensor_tensor(logit[:], logit[:], small[:, 1, :, None].to_broadcast([P, T, NE]), ALU.mult)
                    v.drain()
                    v.tensor_reduce(small[:, 2, :], logit[:], X, ALU.max)
                    v.drain()
                    v.tensor_tensor(gate[:], logit[:], small[:, 2, :, None].to_broadcast([P, T, NE]), ALU.is_equal)
                    v.drain()
                    v.tensor_tensor(gate[:], gate[:], m.first_slot[:, None, 0:NE].to_broadcast([P, T, NE]), ALU.mult)
                    v.drain()
                    v.tensor_reduce(small[:, 3, :], gate[:], X, ALU.max)
                    v.drain()
                    v.tensor_tensor(gate[:], gate[:], small[:, 3, :, None].to_broadcast([P, T, NE]), ALU.is_equal)
                    v.drain()
                    v.tensor_tensor(gate[:], gate[:], logit[:], ALU.mult)
                    v.drain()
                    for c in range(T):
                        v.wait_ge(q["routed_scored"], c + 1)
                        v.tensor_tensor(mixed[:, c % 2, :, :], ps.hi[:, c % 2, :].rearrange("p (e d) -> p e d", d=D), m.bd[:], ALU.add).then_inc(q["routed_taken"], 1)
                        v.drain()
                        v.tensor_tensor(mixed[:, c % 2, :, :], mixed[:, c % 2, :, :], gate[:, c, :, None].to_broadcast([P, NE, D]), ALU.mult)
                        v.drain()
                        v.tensor_reduce(mem.part[:, c, :], mixed[:, c % 2, :, :].rearrange("p e d -> p d e"), X, ALU.add)
                    v.drain()
                    v.tensor_tensor(res, res, mem.part[:], ALU.add)
                    v.drain()

                    norm(3)
                    v.wait_ge(q["a_took"], 2 * H + 1)
                    v.tensor_copy(q1s[0:D, :], q1[0:D, :])
                    v.tensor_tensor(q1[D:2 * D, :], ps.mid[D:2 * D, 1, :], q1[D:2 * D, :], ALU.subtract).then_inc(q["v_took"], 1)
                    v.wait_ge(q["a_took"], 2 * H + 2)
                    v.tensor_tensor(k1s[0:D, :], ps.mid[0:D, 0, :], k1[0:D, :], ALU.subtract).then_inc(q["v_took"], 1)
                    v.wait_ge(q["v_scored"], T + 1)
                    v.tensor_copy(V[:, :, 0, 0:64], ps.hi[:, 0, :].rearrange("p (c e) -> p c e", e=D)).then_inc(q["v_placed"], 1)
                    a1.vector(v, lambda h: q1s[D:D + 1, :], res, D ** -0.5)

                    norm(4)
                    v.wait_ge(q["nodes_scored"], 1)
                    v.tensor_copy(m.node[:, cols, :], ps.hi[:, 0, 0:T * 24].rearrange("p (c f) -> p c f", f=24))

            core.clear(list(q.values()) + a0.sems + a1.sems, (piv_in, blk_in))


def node_tables(core, s, m):
    nc = core.nc
    C = s.cols
    m.table = core.dram("table", [s.nodes, 24])
    m.dst_table = core.dram("dst_table", [s.nodes, 4])
    start_line = core.dram("start_line", [s.rows * s.query_cols * P])
    m.begin = core.sb("begin", [P, 2, C])
    m.after = core.sb("after", [P, 2, C])
    m.last_row = core.sb("last_row", [P, 24])
    m.active = core.sb("active", [P, 1], I32)
    sem = core.sem
    rows_built = sem("rows_built")
    written = sem("tables_written")
    starts_turned = sem("starts_turned")
    starts_placed = sem("starts_placed")
    starts_written = sem("starts_written")
    starts_read = sem("starts_read")
    runs_turned = sem("runs_turned")
    place_ready = sem("place_ready")
    scattered = sem("scattered")
    NQ = s.rows * s.query_cols
    with ExitStack() as ctx:
        sb = lambda name, shape, dt=F32: core.sb("nt_" + name, shape, dt, ctx)
        rows = sb("rows", [P, C, 24])
        startsT = sb("startsT", [P, 2, P])
        line = sb("line", [2 * C, 2, P])
        place = sb("place", [P, C])
        place_i = sb("place_i", [P, C], I32)
        empty = sb("empty", [P, C])
        ps = core.ps("nt_ps", [P, 4, 512], ctx)
        with nc.Block() as block:
            @block.vector
            def _(v):
                heads = rows[:, :, 0:20].rearrange("p c (h f) -> p c h f", f=5)
                for h in range(4):
                    v.tensor_copy(rows[:, :, 5 * h:5 * h + 4], m.node[:, :, 4 * h:4 * h + 4])
                    v.memset(rows[:, :, 5 * h + 4:5 * h + 5], 1.0)
                v.tensor_copy(rows[:, :, 20:24], m.node[:, :, 16:20])
                v.drain()
                v.nop().then_inc(rows_built, 1)
                v.wait_ge(starts_turned, 1)
                v.tensor_copy(startsT[:, 0, :], ps[:, 0, 0:P])
                v.tensor_copy(startsT[0:NQ - P, 1, :], ps[0:NQ - P, 0, P:2 * P]).then_inc(starts_placed, 1)
                v.wait_ge(runs_turned, 1)
                v.tensor_copy(m.begin[:].rearrange("p i c -> p (i c)"), ps[:, 1, 0:2 * C])
                v.tensor_copy(m.after[:].rearrange("p i c -> p (i c)"), ps[:, 1, 2 * C:4 * C])
                v.drain()
                v.tensor_tensor(empty[:], m.begin[:, 0, :], m.after[:, 0, :], ALU.is_equal)
                v.drain()
                v.scalar_tensor_tensor(place[:], empty[:], 2.0 * s.edges, m.begin[:, 0, :], ALU.mult, ALU.add)
                v.drain()
                v.tensor_copy(place_i[:], place[:]).then_inc(place_ready, 1)
                v.tensor_copy(m.active[:], m.begin[:, 1, 0:1])
                v.drain()
                v.tensor_scalar(m.active[:], m.active[:], P * s.group_t - 1, None, ALU.add)
                v.drain()
                v.tensor_scalar(m.active[:], m.active[:], (P * s.group_t).bit_length() - 1, None, ALU.logical_shift_right)

            @block.tensor
            def _(pe):
                flat = m.starts[:].rearrange("p b j -> p (b j)")
                pe.transpose(ps[:, 0, 0:P], flat[:, 0:P], m.ident[:])
                pe.transpose(ps[0:NQ - P, 0, P:2 * P], flat[:, P:NQ], m.ident[:]).then_inc(starts_turned, 1)
                pe.wait_ge(starts_read, 32)
                pe.transpose(ps[:, 1, 0:2 * C], line[:, 0, :], m.ident[:])
                pe.transpose(ps[:, 1, 2 * C:4 * C], line[:, 1, :], m.ident[:]).then_inc(runs_turned, 1)

            @block.sync
            def _(sp):
                sp.wait_ge(rows_built, 1)
                sp.dma_start(m.table.rearrange("(c p) f -> p c f", p=P), rows[:]).then_inc(written, 16)
                sp.dma_start(m.dst_table.rearrange("(c p) f -> p c f", p=P), m.node[:, :, 20:24]).then_inc(written, 16)
                sp.wait_ge(starts_placed, 1)
                sp.dma_start(start_line[0:P * P].rearrange("(c p) -> c p", p=P), startsT[:, 0, :]).then_inc(starts_written, 16)
                sp.dma_start(start_line[P * P:NQ * P].rearrange("(c p) -> c p", p=P), startsT[0:NQ - P, 1, :]).then_inc(starts_written, 16)
                sp.wait_ge(starts_written, 32)
                sp.dma_start(line[:, 0, :], start_line[0:2 * s.nodes].rearrange("(c p) -> c p", p=P)).then_inc(starts_read, 16)
                sp.dma_start(line[:, 1, :], start_line[1:2 * s.nodes + 1].rearrange("(c p) -> c p", p=P)).then_inc(starts_read, 16)
                sp.wait_ge(written, 32)
                sp.dma_start(m.last_row[:], m.table[s.nodes - 1:s.nodes, :].to_broadcast([P, 24])).then_inc(written, 16)
                sp.wait_ge(written, 48)

            @block.gpsimd
            def _(pool):
                pool.wait_ge(place_ready, 1)
                for c in range(C):
                    pool.indirect_dma_start(out=m.dst_line, out_offset=bass.IndirectOffsetOnAxis(ap=place_i[:, c:c + 1], axis=0),
                                            in_=m.node[:, c, 20:24], in_offset=None, bounds_check=s.edges - 1,
                                            oob_is_err=False).then_inc(scattered, 16)
                pool.wait_ge(scattered, 16 * C)


def edges(core, s, m, w):
    nc = core.nc
    TT, G = s.group_t, s.groups
    NX = s.experts1
    D = s.dim
    m.row_sum = core.sb("row_sum", [P, G, 20])
    m.row_max = core.sb("row_max", [P, G, 4])
    m.row_open = core.sb("row_open", [P, G])
    m.expert = core.sb("expert", [P, s.cols, NX, D])
    sem = core.sem
    keys_in = sem("ed_keys_in")
    fills_in = sem("ed_fills_in")
    stored = sem("ed_stored")
    src_ready = sem("ed_src_ready")
    gathered = sem("ed_gathered")
    row_dst_in = sem("ed_row_dst_in")
    logits_ready = sem("ed_logits_ready")
    exped = sem("ed_exped")
    row_built = sem("ed_row_built")
    hid_scored = sem("ed_hid_scored")
    hid_taken = sem("ed_hid_taken")
    exp_scored = sem("ed_exp_scored")
    tokens_copied = sem("ed_tokens_copied")
    base = 8
    CPG = s.cols // base
    half = CPG // 2
    exp_taken = sem("ed_exp_taken")
    with ExitStack() as ctx:
        sb = lambda name, shape, dt=F32: core.sb("ed_" + name, shape, dt, ctx)
        key = sb("key", [P, TT], I32)
        before = sb("before", [P, TT], I32)
        src = sb("src", [P, TT], I32)
        run = sb("run", [P, 2, TT], I32)
        row_dst = sb("row_dst", [P, 1], I32)
        row_fill = sb("row_fill", [P, 4])
        fill = sb("fill", [P, TT, 4])
        got = sb("got", [P, TT, 24])
        start = sb("start", [P, TT])
        carry = sb("carry", [P, TT])
        reset = sb("reset", [P, 4, TT])
        carry4 = sb("carry4", [P, 4, TT])
        fillT = sb("fillT", [P, 4, TT])
        dstT = sb("dstT", [P, 4, TT])
        z = sb("z", [P, 4, TT])
        e = sb("e", [P, 4, TT])
        mx = sb("mx", [P, 4, TT])
        arg = sb("arg", [P, 2, 4, TT])
        weight = sb("weight", [P, 4, TT])
        decay = sb("decay", [P, 20, TT])
        msg = sb("msg", [P, 20, TT])
        acc = sb("acc", [P, 20, TT])
        rowout = sb("rowout", [P, TT, 24])
        one = sb("one", [P, 4])
        hidden_in = sb("hidden_in", [D, CPG * P])
        hid = sb("hid", [P, 2, NX, half * P])
        ps_h = core.ps("ed_ps_h", [P, NX, 512], ctx)
        ps_y = core.ps("ed_ps_y", [P, half, 512], ctx)

        def round_(g, with_experts):
            with nc.Block() as block:
                @block.sync
                def _(sp):
                    sp.dma_start(key[:], m.keys.rearrange("(g p a) f -> g p (a f)", g=G, p=P)[bass.ts(g, 1)].rearrange("o p t -> (o p) t")).then_inc(keys_in, 16)
                    sp.dma_start(before[:], m.keys_before[0:s.edges].rearrange("(g p t) -> g p t", g=G, p=P)[bass.ts(g, 1)].rearrange("o p t -> (o p) t")).then_inc(keys_in, 16)
                    sp.dma_start(fill[:], m.dst_line.rearrange("(g p t) f -> g p t f", g=G, p=P)[bass.ts(g, 1)].rearrange("o p t f -> (o p) t f")).then_inc(fills_in, 16)
                    sp.wait_ge(row_built, 1)
                    sp.dma_start(m.results.rearrange("(g p t) f -> g p t f", g=G, p=P)[bass.ts(g, 1)].rearrange("o p t f -> (o p) t f"), rowout[:]).then_inc(stored, 16)
                    sp.wait_ge(stored, 16)

                @block.gpsimd
                def _(pool):
                    pool.wait_ge(src_ready, 1)
                    gather(pool, row_fill[:], m.dst_table, row_dst[:]).then_inc(row_dst_in, 16)
                    for t in range(TT):
                        gather(pool, got[:, t, :], m.table, src[:, t:t + 1]).then_inc(gathered, 16)
                    pool.wait_ge(row_dst_in, 16)
                    pool.wait_ge(gathered, 16 * TT)

                if with_experts:
                    @block.tensor
                    def _(pe):
                        pe.wait_ge(tokens_copied, 1)
                        for u in range(2):
                            if u:
                                pe.wait_ge(hid_taken, u)
                            for k in range(NX):
                                last = pe.matmul(ps_h[:, k, :], m.w1x[:, k, :], hidden_in[:, u * half * P:(u + 1) * half * P],
                                                 start=True, stop=True)
                            last.then_inc(hid_scored, 1)
                            pe.wait_ge(hid_taken, u + 1)
                            if u:
                                pe.wait_ge(exp_taken, u)
                            for c in range(half):
                                for k in range(NX):
                                    last = pe.matmul(ps_y[:, c, k * D:(k + 1) * D], hid[:, u, k, c * P:(c + 1) * P], m.w2x[:, k, :],
                                                     start=True, stop=True)
                            last.then_inc(exp_scored, 1)

                else:
                    @block.tensor
                    def _(pe):
                        pe.nop()

                @block.scalar
                def _(act):
                    if with_experts:
                        act.copy(hidden_in[:], m.x4T[:, bass.ts(g, CPG * P)]).then_inc(tokens_copied, 1)
                        for u in range(2):
                            act.wait_ge(hid_scored, u + 1)
                            for k in range(NX):
                                last = act.activation(hid[:, u, k, :], ps_h[:, k, :], ACT.Gelu, bias=m.b1x[:, k:k + 1])
                            last.then_inc(hid_taken, 1)
                    act.wait_ge(logits_ready, 1)
                    act.activation(weight[:], arg[:, 0], ACT.Exp)
                    act.activation(decay[:].rearrange("p (h f) t -> p h f t", f=5),
                                   arg[:, 1, :, None, :].to_broadcast([P, 4, 5, TT]), ACT.Exp).then_inc(exped, 1)

                @block.vector
                def _(v):
                    v.wait_ge(keys_in, 32)
                    v.tensor_scalar(src[:], key[:], s.nodes - 1, None, ALU.bitwise_and)
                    v.tensor_scalar(run[:, 0, :], key[:], NODE_BITS, None, ALU.logical_shift_right)
                    v.tensor_scalar(run[:, 1, :], before[:], NODE_BITS, None, ALU.logical_shift_right)
                    v.drain()
                    v.tensor_scalar(row_dst[:], run[:, 0, 0:1], s.nodes - 1, None, ALU.bitwise_and)
                    v.drain()
                    v.nop().then_inc(src_ready, 1)
                    v.tensor_tensor(start[:], run[:, 0, :], run[:, 1, :], ALU.not_equal)
                    v.drain()
                    v.tensor_scalar(carry[:], start[:], -1.0, 1.0, ALU.mult, ALU.add)
                    v.tensor_reduce(one[:, 0:1], start[:], X, ALU.max)
                    v.drain()
                    v.tensor_scalar(m.row_open[:, bass.ts(g, 1)], one[:, 0:1], -BIG, None, ALU.mult)
                    v.tensor_copy(one[:, 1:2], carry[:, 0:1])
                    v.drain()
                    v.memset(carry[:, 0:1], 0.0)
                    v.drain()
                    v.tensor_copy(carry4[:], carry[:, None, :].to_broadcast([P, 4, TT]))
                    v.wait_ge(fills_in, 16)
                    v.tensor_copy(fillT[:], fill[:].rearrange("p t f -> p f t"))
                    v.drain()
                    v.tensor_scalar(reset[:], carry4[:], BIG, -BIG, ALU.mult, ALU.add)
                    v.wait_ge(row_dst_in, 16)
                    v.scalar_tensor_tensor(fillT[:, :, 0], row_fill[:], one[:, 1:2], fillT[:, :, 0], ALU.mult, ALU.add)
                    v.drain()
                    flat = lambda a: a[:].rearrange("p h t -> p (h t)")
                    v.tensor_tensor_scan(flat(dstT), flat(carry4), flat(fillT), 0.0, ALU.mult, ALU.add)
                    if with_experts:
                        for u in range(2):
                            v.wait_ge(exp_scored, u + 1)
                            v.tensor_tensor(m.expert[:, bass.ds(g * CPG + u * half, half), :, :].rearrange("p c e d -> p c (e d)"),
                                            ps_y[:, :, 0:NX * D],
                                            m.b2x[:].rearrange("p e d -> p (e d)")[:, None, :].to_broadcast([P, half, NX * D]), ALU.add).then_inc(exp_taken, 1)
                    v.drain()
                    v.wait_ge(gathered, 16 * TT)
                    v.tensor_tensor(z[:], dstT[:], got[:, :, 20:24].rearrange("p t f -> p f t"), ALU.add)
                    v.drain()
                    v.scalar_tensor_tensor(flat(e), flat(z), 0.2, flat(z), ALU.mult, ALU.max)
                    v.drain()
                    v.tensor_tensor_scan(flat(mx), flat(reset), flat(e), 0.0, ALU.add, ALU.max)
                    v.drain()
                    v.tensor_tensor(arg[:, 0], e[:], mx[:], ALU.subtract)
                    v.tensor_copy(arg[:, 1, :, 0:1], reset[:, :, 0:1])
                    v.tensor_tensor(z[:, :, 1:TT], mx[:, :, 0:TT - 1], mx[:, :, 1:TT], ALU.subtract)
                    v.drain()
                    v.tensor_tensor(arg[:, 1, :, 1:TT], z[:, :, 1:TT], reset[:, :, 1:TT], ALU.add)
                    v.drain()
                    v.nop().then_inc(logits_ready, 1)
                    v.wait_ge(exped, 1)
                    v.tensor_tensor(msg[:].rearrange("p (h f) t -> p h f t", f=5),
                                    got[:, :, 0:20].rearrange("p t (h f) -> p h f t", f=5),
                                    weight[:, :, None, :].to_broadcast([P, 4, 5, TT]), ALU.mult)
                    v.drain()
                    v.tensor_tensor_scan(flat(acc), flat(decay), flat(msg), 0.0, ALU.mult, ALU.add)
                    v.drain()
                    v.tensor_copy(rowout[:, :, 0:20], acc[:].rearrange("p f t -> p t f"))
                    v.tensor_copy(rowout[:, :, 20:24], mx[:].rearrange("p f t -> p t f"))
                    v.tensor_copy(m.row_sum[:, bass.ts(g, 1), :], acc[:, :, TT - 1:TT].rearrange("p f o -> p o f"))
                    v.tensor_copy(m.row_max[:, bass.ts(g, 1), :], mx[:, :, TT - 1:TT].rearrange("p f o -> p o f"))
                    v.drain()
                    v.nop().then_inc(row_built, 1)

            core.clear([keys_in, fills_in, stored, src_ready, logits_ready, exped, row_built, hid_scored,
                        hid_taken, exp_scored, exp_taken, tokens_copied], (row_dst_in, gathered))

        with nc.Block() as block:
            @block.vector
            def _(v):
                v.memset(m.row_sum[:], 0.0)
                v.memset(m.row_max[:], -BIG)
                v.memset(m.row_open[:], 0.0)
        active = nc.values_load(m.active[0:1, 0:1], min_val=0, max_val=G,
                                skip_runtime_bounds_check_because="a count of edges over the edges of a group")
        with nc.Fori(0, base) as g:
            round_(g, True)
        with nc.Fori(base, G) as g:
            with nc.If(g < active):
                round_(g, False)
            nc.end_ifs()


def finish(core, s, m, w, out):
    nc = core.nc
    G, C, D, NX, TT = s.groups, s.cols, s.dim, s.experts1, s.group_t
    rows = G * P
    carried = core.dram("carried", [rows + 1, 24])
    sem = core.sem
    packed = sem("fi_packed")
    turned = sem("fi_turned")
    v_taken = sem("fi_v_taken")
    a_taken = sem("fi_a_taken")
    exp_wanted = sem("fi_exp_wanted")
    exped = sem("fi_exped")
    chained = sem("fi_chained")
    turned_back = sem("fi_turned_back")
    carry_built = sem("fi_carry_built")
    carry_out = sem("fi_carry_out")
    place_ready = sem("fi_place_ready")
    runs_in = sem("fi_runs_in")
    carries_in = sem("fi_carries_in")
    variance = sem("fi_variance")
    powed = sem("fi_powed")
    out_ready = sem("fi_out_ready")
    out_stored = sem("fi_out_stored")
    with ExitStack() as ctx:
        sb = lambda name, shape, dt=F32: core.sb("fi_" + name, shape, dt, ctx)
        value = [sb(f"value{i}", [P, C, 24]) for i in range(2)]
        place = sb("place", [P, 3, C])
        place_i = sb("place_i", [P, 3, C], I32)
        with ExitStack() as ctx2:
            sb2 = lambda name, shape, dt=F32: core.sb("fi_" + name, shape, dt, ctx2)
            pack = sb2("pack", [P, G, 96])
            sums = m.x4T[0:20, 0:rows]
            maxs = m.x4T[0:20, rows:2 * rows]
            decay = sb2("decay", [20, rows])
            chain = sb2("chain", [20, rows])
            carry = sb2("carry", [P, G, 24])
            zero = sb2("zero", [1, 24])
            ps = core.ps("fi_ps", [P, 4, 512], ctx2)
            ps_back = core.ps("fi_back", [P, 4, 512], ctx2)
            per_round = 8
            rounds = G // per_round
            with nc.Block() as block:
                @block.sync
                def _(sp):
                    sp.wait_ge(carry_built, 1)
                    sp.dma_start(carried[0:1, :], zero[:]).then_inc(carry_out, 16)
                    sp.dma_start(carried[1:rows + 1, :].rearrange("(g p) f -> p g f", p=P), carry[:]).then_inc(carry_out, 16)
                    sp.wait_ge(carry_out, 32)

                @block.gpsimd
                def _(pool):
                    pool.wait_ge(place_ready, 1)
                    for c in range(C):
                        gather(pool, value[0][:, c, :], m.results, place_i[:, 0, c:c + 1]).then_inc(runs_in, 16)
                    pool.wait_ge(carry_out, 32)
                    for c in range(C):
                        gather(pool, value[1][:, c, :], carried, place_i[:, 1, c:c + 1]).then_inc(carries_in, 16)
                    pool.wait_ge(runs_in, 16 * C)
                    pool.wait_ge(carries_in, 16 * C)

                @block.tensor
                def _(pe):
                    pe.wait_ge(packed, 1)
                    for r in range(rounds):
                        if r >= 2:
                            pe.wait_ge(v_taken, r - 1)
                            pe.wait_ge(a_taken, r - 1)
                        for i in range(per_round):
                            last = pe.transpose(ps[0:96, 2 * (r % 2) + i // 4, (i % 4) * P:(i % 4 + 1) * P],
                                                pack[:, r * per_round + i, :], m.ident[:])
                        last.then_inc(turned, 1)
                    pe.wait_ge(chained, 1)
                    for i, of in enumerate((sums, chain)):
                        for g in range(G):
                            last = pe.transpose(ps_back[:, 2 * i + g // 16, (g % 16) * 20:(g % 16 + 1) * 20],
                                                of[:, g * P:(g + 1) * P], m.ident[0:20, 0:20])
                    last.then_inc(turned_back, 1)

                @block.scalar
                def _(act):
                    for r in range(rounds):
                        act.wait_ge(turned, r + 1)
                        act.wait_ge(v_taken, r + 1)
                        span = slice(r * per_round * P, (r + 1) * per_round * P)
                        bank = ps[:, 2 * (r % 2):2 * (r % 2) + 2, :].rearrange("p a b -> p (a b)")
                        act.copy(sums[:, span], bank[0:20, :]).then_inc(a_taken, 1)
                    act.wait_ge(exp_wanted, 1)
                    act.activation(maxs, maxs, ACT.Exp)
                    act.activation(decay[:], decay[:], ACT.Exp).then_inc(exped, 1)

                @block.vector
                def _(v):
                    v.memset(zero[:], 0.0)
                    v.tensor_scalar(place[:, 0, :], m.after[:, 0, :], 1.0, 0.0, ALU.subtract, ALU.max)
                    v.memset(pack[:], 0.0)
                    v.drain()
                    v.tensor_copy(place_i[:, 0, :], place[:, 0, :])
                    v.tensor_copy(pack[:, :, 0:20], m.row_sum[:])
                    v.tensor_copy(pack[:, :, 32:52].rearrange("p g (h f) -> p g h f", f=5), m.row_max[:, :, :, None].to_broadcast([P, G, 4, 5]))
                    v.tensor_copy(pack[:, :, 64:84], m.row_open[:, :, None].to_broadcast([P, G, 20]))
                    v.drain()
                    v.nop().then_inc(packed, 1)
                    v.tensor_scalar(place_i[:, 1, :], place_i[:, 0, :], TT.bit_length() - 1, None, ALU.logical_shift_right)
                    v.drain()
                    v.tensor_scalar(place_i[:, 2, :], place_i[:, 1, :], TT.bit_length() - 1, None, ALU.logical_shift_left)
                    v.nop().then_inc(place_ready, 1)
                    v.drain()
                    v.tensor_copy(place[:, 2, :], place_i[:, 2, :])
                    for r in range(rounds):
                        v.wait_ge(turned, r + 1)
                        span = slice(r * per_round * P, (r + 1) * per_round * P)
                        bank = ps[:, 2 * (r % 2):2 * (r % 2) + 2, :].rearrange("p a b -> p (a b)")
                        v.tensor_copy(maxs[:, span], bank[32:52, :])
                        v.tensor_copy(decay[:, span], bank[64:84, :]).then_inc(v_taken, 1)
                    v.drain()
                    v.tensor_tensor_scan(chain[:], decay[:], maxs, -BIG, ALU.add, ALU.max)
                    v.drain()
                    v.tensor_tensor(maxs, maxs, chain[:], ALU.subtract)
                    v.tensor_tensor(decay[:, 1:rows], decay[:, 1:rows], chain[:, 0:rows - 1], ALU.add)
                    v.drain()
                    v.tensor_tensor(decay[:, 1:rows], decay[:, 1:rows], chain[:, 1:rows], ALU.subtract)
                    v.drain()
                    v.nop().then_inc(exp_wanted, 1)
                    v.wait_ge(exped, 1)
                    v.wait_ge(a_taken, rounds)
                    v.tensor_tensor(maxs, maxs, sums, ALU.mult)
                    v.drain()
                    v.tensor_tensor_scan(sums, decay[:], maxs, 0.0, ALU.mult, ALU.add)
                    v.drain()
                    v.nop().then_inc(chained, 1)
                    v.wait_ge(turned_back, 1)
                    back = lambda i: ps_back[:, 2 * i:2 * i + 2, 0:320].rearrange("p a (g f) -> p a g f", f=20)
                    both = carry[:].rearrange("p (a g) f -> p a g f", a=2)
                    v.tensor_copy(both[:, :, :, 0:20], back(0))
                    v.tensor_copy(both[:, :, :, 20:24], back(1).rearrange("p a g (h f) -> p a g h f", f=5)[:, :, :, :, 0])
                    v.drain()
                    v.nop().then_inc(carry_built, 1)

        logit = sb("logit", [P, 4, C, 4])
        mask = sb("mask", [P, 3, C])
        count = sb("count", [P, C])
        top = sb("top", [P, C, 4])
        term = [sb(f"term{i}", [P, C, 4, 5]) for i in range(2)]
        agg = sb("agg", [P, C, 4, 4])
        sq = sb("sq", [P, C, 4, 4])
        stat = sb("stat", [P, 4, C])
        score = sb("score", [P, C, 4])
        hot = sb("hot", [P, 2, C, 4])
        gate = sb("gate", [P, C, 4])
        best = sb("best", [P, 4, C])
        one = sb("one", [P, C, 4, 5])
        last = sb("last", [P, 4, 5])
        chunk = 8
        mix = sb("mix", [P, chunk, D])
        with nc.Block() as block:
            @block.gpsimd
            def _(pool):
                pool.wait_ge(variance, 1)
                pool.drain()
                pool.tensor_scalar(stat[:, 2, :], stat[:, 1, :], 1.0 / 16, 1e-5, ALU.mult, ALU.add)
                pool.drain()
                pool.tensor_tensor(stat[:, 3, :], stat[:, 2, :], m.minus_half[:, 0:C], ALU.pow).then_inc(powed, 1)

            @block.scalar
            def _(act):
                act.wait_ge(exp_wanted, 2)
                act.activation(logit[:], logit[:], ACT.Exp).then_inc(exped, 1)
                act.wait_ge(exp_wanted, 3)
                act.activation(best[:, 2, :], best[:, 1, :], ACT.Exp).then_inc(exped, 1)

            @block.sync
            def _(sp):
                n_out = C // chunk
                rows_out = out.rearrange("b t d -> (b t) d").rearrange("(c p) d -> p c d", p=P)
                for i in range(n_out):
                    sp.wait_ge(out_ready, i + 1)
                    sp.dma_start(rows_out[:, i * chunk:(i + 1) * chunk, :], m.h[:, i * chunk:(i + 1) * chunk, :]).then_inc(out_stored, 16)
                sp.wait_ge(out_stored, 16 * n_out)

            @block.vector
            def _(v):
                wide = lambda a: a[:, :, None].to_broadcast([P, C, 4])
                v.tensor_tensor(count[:], m.after[:, 1, :], m.begin[:, 1, :], ALU.subtract)
                v.tensor_tensor(mask[:, 0, :], m.after[:, 0, :], m.begin[:, 0, :], ALU.is_gt)
                v.tensor_tensor(mask[:, 1, :], place[:, 2, :], m.begin[:, 0, :], ALU.is_gt)
                v.tensor_tensor(mask[:, 2, :], m.after[:, 1, :], m.begin[:, 1, :], ALU.is_gt)
                v.tensor_tensor(logit[:, 2], m.node[:, :, 16:20], m.node[:, :, 20:24], ALU.add)
                v.tensor_tensor(logit[:, 3], m.node[:, :, 20:24], m.last_row[:, None, 20:24].to_broadcast([P, C, 4]), ALU.add)
                v.tensor_copy(one[:, :, :, 0:4], m.node[:, :, 0:16].rearrange("p c (h f) -> p c h f", h=4))
                v.memset(one[:, :, :, 4:5], 1.0)
                v.tensor_copy(last[:], m.last_row[:, 0:20].rearrange("p (h f) -> p h f", h=4))
                v.drain()
                v.tensor_tensor(mask[:, 1, :], mask[:, 1, :], mask[:, 0, :], ALU.mult)
                v.scalar_tensor_tensor(logit[:, 2:4], logit[:, 2:4], 0.2, logit[:, 2:4], ALU.mult, ALU.max)
                v.drain()
                v.tensor_tensor(logit[:, 0], value[0][:, :, 20:24], wide(mask[:, 0, :]), ALU.mult)
                v.tensor_tensor(logit[:, 1], value[1][:, :, 20:24], wide(mask[:, 1, :]), ALU.mult)
                v.tensor_tensor(logit[:, 3], logit[:, 3], wide(mask[:, 2, :]), ALU.mult)
                v.drain()
                v.tensor_scalar(mask[:], mask[:], BIG, -BIG, ALU.mult, ALU.add)
                v.drain()
                for i, k in ((0, 0), (1, 1), (3, 2)):
                    v.tensor_tensor(logit[:, i], logit[:, i], wide(mask[:, k, :]), ALU.add)
                v.drain()
                v.tensor_reduce(top[:], logit[:].rearrange("p i c h -> p c h i"), X, ALU.max)
                v.drain()
                v.tensor_tensor(logit[:], logit[:], top[:, None, :, :].to_broadcast([P, 4, C, 4]), ALU.subtract)
                v.drain()
                v.nop().then_inc(exp_wanted, 1)
                v.wait_ge(exped, 2)
                v.tensor_tensor(logit[:, 3], logit[:, 3], wide(count[:]), ALU.mult)
                v.drain()
                weight = lambda i: logit[:, i, :, :, None].to_broadcast([P, C, 4, 5])
                rows = lambda a: a[:, :, 0:20].rearrange("p c (h f) -> p c h f", h=4)
                v.tensor_tensor(term[0][:], rows(value[0][:]), weight(0), ALU.mult)
                v.tensor_tensor(term[1][:], rows(value[1][:]), weight(1), ALU.mult)
                v.tensor_tensor(one[:], one[:], weight(2), ALU.mult)
                v.drain()
                v.tensor_tensor(term[0][:], term[0][:], term[1][:], ALU.add)
                v.drain()
                v.tensor_tensor(term[1][:], last[:, None, :, :].to_broadcast([P, C, 4, 5]), weight(3), ALU.mult)
                v.tensor_tensor(term[0][:], term[0][:], one[:], ALU.add)
                v.drain()
                v.tensor_tensor(term[0][:], term[0][:], term[1][:], ALU.add)
                v.drain()
                v.tensor_scalar(top[:], term[0][:, :, :, 4], 1e-16, None, ALU.add)
                v.drain()
                v.reciprocal(top[:], top[:])
                v.drain()
                v.tensor_tensor(agg[:], term[0][:, :, :, 0:4], top[:, :, :, None].to_broadcast([P, C, 4, 4]), ALU.mult)
                v.drain()
                flat = lambda a: a[:].rearrange("p c h f -> p c (h f)")
                row16 = lambda a: a[:, None, :].to_broadcast([P, C, 16])
                v.tensor_tensor(flat(agg), flat(agg), row16(m.bgat), ALU.add)
                v.drain()
                v.tensor_reduce(stat[:, 0, :], flat(agg), X, ALU.add)
                v.drain()
                v.tensor_scalar(stat[:, 0, :], stat[:, 0, :], 1.0 / 16, None, ALU.mult)
                v.drain()
                v.tensor_tensor(flat(agg), flat(agg), stat[:, 0, :, None].to_broadcast([P, C, 16]), ALU.subtract)
                v.drain()
                v.tensor_tensor(sq[:], agg[:], agg[:], ALU.mult)
                v.drain()
                v.tensor_reduce(stat[:, 1, :], flat(sq), X, ALU.add)
                v.drain()
                v.nop().then_inc(variance, 1)
                v.wait_ge(powed, 1)
                v.tensor_tensor(flat(agg), flat(agg), stat[:, 3, :, None].to_broadcast([P, C, 16]), ALU.mult)
                v.drain()
                v.tensor_tensor(flat(agg), flat(agg), row16(m.gamma), ALU.mult)
                v.drain()
                v.tensor_tensor(flat(agg), flat(agg), row16(m.beta), ALU.add)
                v.drain()
                v.tensor_reduce(score[:], agg[:].rearrange("p c h f -> p c f h"), X, ALU.add)
                v.drain()
                v.tensor_scalar(score[:], score[:], 0.25, None, ALU.mult)
                v.drain()
                for k in range(2):
                    v.tensor_reduce(best[:, k, :], score[:], X, ALU.max)
                    v.drain()
                    v.tensor_tensor(hot[:, k], score[:], wide(best[:, k, :]), ALU.is_equal)
                    v.drain()
                    v.tensor_tensor(hot[:, k], hot[:, k], m.first_slot[:, None, 0:4].to_broadcast([P, C, 4]), ALU.mult)
                    v.drain()
                    v.tensor_reduce(best[:, 3, :], hot[:, k], X, ALU.max)
                    v.drain()
                    v.tensor_tensor(hot[:, k], hot[:, k], wide(best[:, 3, :]), ALU.is_equal)
                    v.drain()
                    if k == 0:
                        v.scalar_tensor_tensor(score[:], hot[:, 0], -BIG, score[:], ALU.mult, ALU.add)
                        v.drain()
                v.tensor_tensor(best[:, 1, :], best[:, 1, :], best[:, 0, :], ALU.subtract)
                v.drain()
                v.nop().then_inc(exp_wanted, 1)
                v.wait_ge(exped, 3)
                v.tensor_scalar(best[:, 0, :], best[:, 2, :], 1.0, None, ALU.add)
                v.drain()
                v.reciprocal(best[:, 0, :], best[:, 0, :])
                v.drain()
                v.tensor_tensor(hot[:, 1], hot[:, 1], wide(best[:, 2, :]), ALU.mult)
                v.drain()
                v.tensor_tensor(gate[:], hot[:, 0], hot[:, 1], ALU.add)
                v.drain()
                v.tensor_tensor(gate[:], gate[:], wide(best[:, 0, :]), ALU.mult)
                v.drain()
                for i in range(C // chunk):
                    cols = slice(i * chunk, (i + 1) * chunk)
                    part = m.expert[:, cols, :, :]
                    v.tensor_tensor(part, part, gate[:, cols, :, None].to_broadcast([P, chunk, NX, D]), ALU.mult)
                    v.drain()
                    v.tensor_reduce(mix[:], part.rearrange("p c e d -> p c d e"), X, ALU.add)
                    v.drain()
                    v.tensor_tensor(m.h[:, cols, :], m.h[:, cols, :], mix[:], ALU.add).then_inc(out_ready, 1)


def build(nc, w, out):
    with ExitStack() as ctx:
        core = Core(nc, ctx)
        s = Shapes(w["x"], w["L0_tok_emb"], w["L0_attn_Q"], w["L0_ffn_W1"], w["L0_ffn_Wd"], w["L1_ffn_W1"], w["L1_ffn_edge_index"])
        m = Store()
        m.turn_src = turn_sources(s)
        load_weights(core, s, m, w)
        embed_and_sort(core, s, m, w)
        tower(core, s, m, w)
        node_tables(core, s, m)
        edges(core, s, m, w)
        finish(core, s, m, w, out)


def kernel(**inputs):
    import numpy as _np
    import concourse.bacc as _bacc
    from concourse import mybir as _mybir
    from concourse.bass_utils import run_bass_kernel_spmd as _run

    nc = _bacc.Bacc("TRN2", target_bir_lowering=False, num_devices=1)
    arrays, aps = {}, {}
    for name, value in inputs.items():
        a = _np.ascontiguousarray(value)
        arrays[f"in_{name}_dram"] = a
        aps[name] = nc.dram_tensor(f"in_{name}_dram", a.shape, _mybir.dt.from_np(a.dtype), kind="ExternalInput").ap()
    shape = tuple(inputs["x"].shape) + (inputs["L0_tok_emb"].shape[1],)
    out = nc.dram_tensor("out_0_dram", shape, _mybir.dt.float32, kind="ExternalOutput").ap()
    build(nc, aps, out)
    r = _run(nc, [arrays], core_ids=[0])
    return r.results[0]["out_0_dram"]
```

```python
from contextlib import ExitStack

import concourse.bass as bass
from concourse import mybir

F32 = mybir.dt.float32
F16 = mybir.dt.float16
I32 = mybir.dt.int32
ALU = mybir.AluOpType
ACT = mybir.ActivationFunctionType
X = mybir.AxisListType.X

P = 128
BIG = 1.0e30

NODE_BITS = 13
KEY_BASE = 0x40000000


WEIGHT_SCALE = 64.0


class Store:
    pass


class Shapes:

    def __init__(self, x, emb, q, w1, wd, w1x, edge_index):
        self.rows, self.steps = x.shape
        self.vocab, self.dim = emb.shape
        self.heads, self.rank, _ = q.shape
        self.hidden = w1.shape[1]
        self.experts0 = wd.shape[0]
        self.experts1, _, self.hidden1 = w1x.shape
        self.edges = edge_index.shape[1]
        self.nodes = self.rows * self.steps
        self.cols = self.nodes // P
        self.tiles = self.steps // P
        self.per_part = self.edges // P
        self.group_t = 64
        self.groups = self.edges // (P * self.group_t)
        self.query_cols = 17
        assert self.nodes == 1 << NODE_BITS and self.edges == 1 << 18
        assert self.rows * self.query_cols * P > 2 * self.nodes


class Core:

    def __init__(self, nc, ctx):
        self.nc, self.ctx = nc, ctx
        self.sems = {}

    def sb(self, name, shape, dt=F32, ctx=None):
        return (ctx or self.ctx).enter_context(self.nc.sbuf_tensor(name, shape, dt))

    def ps(self, name, shape, ctx):
        return ctx.enter_context(self.nc.psum_tensor(name, shape, F32))

    def sem(self, name):
        assert name not in self.sems
        self.sems[name] = self.ctx.enter_context(self.nc.semaphore(name))
        return self.sems[name]

    def dram(self, name, shape, dt=F32):
        return self.nc.dram_tensor(name, shape, dt, kind="Internal").ap()

    def clear(self, sems, gathers=()):
        with self.nc.Block() as block:
            @block.sync
            def _(sp):
                for s in sems:
                    sp.sem_clear(s)

            @block.gpsimd
            def _(pool):
                for s in gathers:
                    pool.dma_reset(range(s.num, s.num + 1))
                    pool.sem_clear(s)


def gather(pool, out, table, index):
    return pool.indirect_dma_start(out=out, out_offset=None, in_=table,
                                   in_offset=bass.IndirectOffsetOnAxis(ap=index, axis=0))


def load_weights(core, s, m, w):
    nc = core.nc
    H, R, D = s.heads, s.rank, s.dim
    per = P // R
    groups = H // per
    hc = s.hidden // P
    n1 = s.experts1
    sb = core.sb
    m.ident = sb("ident", [P, P])
    m.qk_high = sb("qk_high", [P, 2, H, 3, R], F16)
    m.qk_low = sb("qk_low", [D, 2, H, 3, R], F16)
    m.vo_high = sb("vo_high", [P, H, D], F16)
    m.vo_low = sb("vo_low", [D, H, D], F16)
    m.w1 = sb("w1", [D, s.hidden])
    m.b1 = sb("b1", [P, hc])
    m.wg = sb("wg", [P, hc, s.experts0])
    m.bg = sb("bg", [P, s.experts0])
    m.wd = sb("wd", [P, hc, s.experts0, D])
    m.bd = sb("bd", [P, s.experts0, D])
    m.wq1T = sb("wq1T", [D, 2, D])
    m.wk1T = sb("wk1T", [D, 2, D])
    m.wv1T = sb("wv1T", [D, D])
    m.wnode = sb("wnode", [D, 24])
    m.bgat = sb("bgat", [P, 16])
    m.gamma = sb("gamma", [P, 16])
    m.beta = sb("beta", [P, 16])
    m.w1x = sb("w1x", [D, n1, s.hidden1])
    m.b1x = sb("b1x", [P, n1])
    m.w2x = sb("w2x", [P, n1, D])
    m.b2x = sb("b2x", [P, n1, D])
    m.first_slot = sb("first_slot", [P, 8])
    m.minus_half = sb("minus_half", [P, s.cols])
    m.iota_t = sb("iota_t", [P, 8], I32)
    m.part_sign = sb("part_sign", [P, 1])
    m.query = sb("query", [P, s.rows, s.query_cols], I32)
    m.tok = sb("tok", [P, s.cols], I32)

    weights_in = core.sem("weights_in")
    raw_in = core.sem("raw_in")
    ident_made = core.sem("ident_made")
    turned = core.sem("turned")
    toks_float = core.sem("toks_float")
    highs_made = core.sem("highs_made")
    highs_doubled = core.sem("highs_doubled")
    with ExitStack() as ctx:
        vo = sb("vo", [D, H, D], F32, ctx)
        qk = sb("qk", [D, 2, H, 3, R], F32, ctx)
        qraw = sb("qraw", [P, 2, groups, D], F32, ctx)
        raw1 = sb("raw1", [D, 3, D], F32, ctx)
        att = sb("att", [D, 2, 4, 4], F32, ctx)
        prod = sb("prod", [D, 2, 4, 4], F32, ctx)
        tok_in = sb("tok_in", [s.cols, P], I32, ctx)
        tok_f = sb("tok_f", [s.cols, P], F32, ctx)
        pidx = sb("pidx", [P, 1], I32, ctx)
        turn_ps = core.ps("turn_ps", [P, 8, 512], ctx)
        with nc.Block() as block:
            @block.sync
            def _(sp):
                for g in range(groups):
                    for i, a in enumerate((w["L0_attn_Q"], w["L0_attn_K"])):
                        sp.dma_start(qraw[:, i, g, :], a.rearrange("(g h) r d -> g (h r) d", g=groups)[g]).then_inc(raw_in, 16)
                for i, a in enumerate((w["L1_attn_Wq"], w["L1_attn_Wk"], w["L1_attn_Wv"])):
                    sp.dma_start(raw1[:, i, :], a).then_inc(raw_in, 16)
                sp.dma_start(tok_in[:], w["x"].rearrange("b (c p) -> (b c) p", p=P)).then_inc(raw_in, 16)
                sp.dma_start(m.wnode[:, 0:16], w["L1_ffn_W_gat"]).then_inc(raw_in, 16)
                for i, a in enumerate((w["L1_ffn_att_src"], w["L1_ffn_att_dst"])):
                    sp.dma_start(att[:, i, :, :].rearrange("p a b -> p (a b)"),
                                 a.rearrange("(o h) e -> o (h e)", o=1).to_broadcast([D, 16])).then_inc(raw_in, 16)
                sp.dma_start(vo[:], w["L0_attn_VO"].rearrange("h d e -> d h e")).then_inc(weights_in, 16)
                sp.dma_start(m.w1[:], w["L0_ffn_W1"]).then_inc(weights_in, 16)
                sp.dma_start(m.wg[:], w["L0_ffn_Wg"].rearrange("(c p) e -> p c e", p=P)).then_inc(weights_in, 16)
                for c in range(hc):
                    sp.dma_start(m.wd[:, c, :, :], w["L0_ffn_Wd"].rearrange("e (c p) d -> c p e d", p=P)[c]).then_inc(weights_in, 16)
                sp.dma_start(m.w1x[:], w["L1_ffn_W1"].rearrange("e d f -> d e f")).then_inc(weights_in, 16)
                sp.dma_start(m.w2x[:], w["L1_ffn_W2"].rearrange("e f d -> f e d")).then_inc(weights_in, 16)
                rows = ((m.bg[:], w["L0_ffn_bg"]), (m.bgat[:], w["L1_ffn_b_gat"]), (m.gamma[:], w["L1_ffn_ln_gamma"]),
                        (m.beta[:], w["L1_ffn_ln_beta"]))
                for to, a in rows:
                    sp.dma_start(to, a.rearrange("(o n) -> o n", o=1).to_broadcast([P, a.shape[0]])).then_inc(weights_in, 16)
                for to, a in ((m.bd, w["L0_ffn_bd"]), (m.b2x, w["L1_ffn_b2"])):
                    sp.dma_start(to[:].rearrange("p e d -> p (e d)"),
                                 a.rearrange("(o e) d -> o (e d)", o=1).to_broadcast([P, a.shape[0] * D])).then_inc(weights_in, 16)
                with nc.allow_non_contiguous_dma(reason="bias columns, a few hundred elements"):
                    sp.dma_start(m.b1[:], w["L0_ffn_b1"].rearrange("(c p) -> p c", p=P)).then_inc(weights_in, 16)
                    sp.dma_start(m.b1x[:], w["L1_ffn_b1"].rearrange("e p -> p e")).then_inc(weights_in, 16)
                sp.wait_ge(weights_in, 16 * (6 + hc + 4 + 2 + 2 - 1))
                sp.wait_ge(highs_made, 1)
                sp.dma_start(m.qk_high[D:P].rearrange("p i h a r -> p (i h a r)"),
                             m.qk_high[0:D].rearrange("p i h a r -> p (i h a r)")).then_inc(highs_doubled, 16)
                sp.dma_start(m.vo_high[D:P].rearrange("p h d -> p (h d)"),
                             m.vo_high[0:D].rearrange("p h d -> p (h d)")).then_inc(highs_doubled, 16)
                sp.wait_ge(highs_doubled, 32)

            @block.gpsimd
            def _(pool):
                pool.memset(m.ident[:], 0.0)
                pool.memset(m.minus_half[:], -0.5)
                pool.iota(m.iota_t[:], [[-1, 8]], base=8, channel_multiplier=0)
                pool.iota(pidx[:], [[0, 1]], base=0, channel_multiplier=1)
                pool.iota(m.query[:], [[P * s.query_cols, s.rows], [P, s.query_cols]], base=0, channel_multiplier=1)
                pool.drain()
                pool.affine_select(out=m.ident[:], in_=m.ident[:], compare_op=ALU.not_equal, fill=1.0, base=0,
                                   pattern=[[-1, P]], channel_multiplier=1).then_inc(ident_made, 1)

            @block.tensor
            def _(pe):
                pe.wait_ge(ident_made, 1)
                pe.wait_ge(toks_float, 1)
                pe.wait_ge(raw_in, 16 * (2 * groups + 7))
                n = 0
                for i in range(2):
                    for g in range(groups):
                        pe.transpose(turn_ps[0:D, n, 0:P], qraw[:, i, g, :], m.ident[:]).then_inc(turned, 1)
                        n += 1
                for i in range(3):
                    pe.transpose(turn_ps[0:D, n, 0:D], raw1[:, i, :], m.ident[0:D, 0:D]).then_inc(turned, 1)
                    n += 1
                pe.transpose(turn_ps[:, n, 0:s.cols], tok_f[:], m.ident[0:s.cols, 0:s.cols]).then_inc(turned, 1)

            @block.vector
            def _(v):
                v.wait_ge(raw_in, 16 * (2 * groups + 7))
                v.tensor_copy(tok_f[:], tok_in[:]).then_inc(toks_float, 1)
                v.tensor_tensor(prod[:], att[:], m.wnode[:, 0:16].rearrange("p (h e) -> p h e", h=4)[:, None, :, :].to_broadcast([D, 2, 4, 4]), ALU.mult)
                v.drain()
                v.tensor_reduce(m.wnode[:, 16:24].rearrange("p (i h) -> p i h", i=2), prod[:], X, ALU.add)
                v.wait_ge(ident_made, 1)
                v.tensor_copy(m.first_slot[:], m.iota_t[:])
                v.tensor_scalar(pidx[:], pidx[:], 1, None, ALU.bitwise_and)
                v.tensor_scalar(m.query[:], m.query[:], NODE_BITS, KEY_BASE, ALU.logical_shift_left, ALU.bitwise_or)
                v.drain()
                v.tensor_scalar(m.part_sign[:], pidx[:], -2.0, 1.0, ALU.mult, ALU.add)
                v.wait_ge(turned, 2 * groups + 4)
                n = 0
                for to, scale in ((qk[:, 0], WEIGHT_SCALE * s.dim ** -0.5), (qk[:, 1], WEIGHT_SCALE)):
                    for g in range(groups):
                        v.tensor_scalar(to[:, g * per:(g + 1) * per, :, :],
                                        turn_ps[0:D, n, 0:P].rearrange("d (h r) -> d h r", r=R)[:, :, None, :].to_broadcast([D, per, 3, R]),
                                        scale, None, ALU.mult)
                        n += 1
                for to, copies in ((m.wq1T, 2), (m.wk1T, 2), (m.wv1T, 1)):
                    for i in range(copies):
                        v.tensor_copy(to[:, i, :] if copies > 1 else to[:], turn_ps[0:D, n, 0:D])
                    n += 1
                v.tensor_copy(m.tok[:], turn_ps[:, n, 0:s.cols])
                v.wait_ge(weights_in, 16 * (6 + hc + 4 + 2 + 2 - 1))
                v.tensor_scalar(vo[:], vo[:], WEIGHT_SCALE, None, ALU.mult)
                v.drain()
                for whole, high, low in ((vo, m.vo_high, m.vo_low), (qk, m.qk_high, m.qk_low)):
                    v.tensor_copy(high[0:D], whole[:])
                    v.drain()
                    v.tensor_tensor(low[:], whole[:], high[0:D], ALU.subtract)
                    v.drain()
                v.nop().then_inc(highs_made, 1)


def embed_and_sort(core, s, m, w):
    nc = core.nc
    D = s.dim
    parts = 125
    per = s.vocab // parts
    smooth = core.dram("smooth", [s.vocab, D])
    m.keys = core.dram("keys", [s.edges // 32, 32], I32)
    m.keys_before = core.dram("keys_before", [s.edges + P], I32)
    m.pivot_row = core.dram("pivot_row", [1, P], I32)
    m.pivots = core.dram("pivots", [P, 64], I32)
    m.results = core.dram("results", [s.edges, 24])
    m.dst_line = core.dram("dst_line", [s.edges, 4])
    blank = [a.rearrange("(p r) f -> p (r f)", p=P) for a in (m.results, m.dst_line)]
    piece = 2048
    zero_made = core.sem("zero_made")
    blanked = core.sem("blanked")
    m.h = core.sb("h", [P, s.cols, D])
    m.pivot1 = core.sb("pivot1", [P, P], I32)
    F = s.per_part
    table_in = core.sem("table_in")
    pair_summed = core.sem("pair_summed")
    smoothed = core.sem("smoothed")
    smooth_out = core.sem("smooth_out")
    tokens_in = core.sem("tokens_in")
    edges_in = core.sem("edges_in")
    stored = core.sem("stored")
    turn_wanted = core.sem("turn_wanted")
    turn_made = core.sem("turn_made")
    half_copied = core.sem("half_copied")
    ready_to_turn = core.sem("ready_to_turn")
    sorted_ = core.sem("sorted")
    keys_out = core.sem("keys_out")
    pivot_in = core.sem("pivot_in")
    TURNS = 14
    with ExitStack() as ctx:
        halo = core.sb("halo", [parts, per + 4, D], F32, ctx)
        pair = core.sb("pair", [parts, per, D], F32, ctx)
        acc = core.sb("acc", [parts, per, D], F32, ctx)
        ends = core.sb("ends", [P, 2, F], I32, ctx)
        buf = [core.sb(f"sort{i}", [P, F], F32, ctx) for i in range(2)]
        ibuf = [b[:].bitcast(I32) for b in buf]
        first = core.sb("first", [P, 64], F32, ctx)
        zeros = core.sb("zeros", [P, piece], F32, ctx)
        sentinel = core.sb("sentinel", [1, 1], I32, ctx)
        turn_ps = core.ps("sort_ps", [P, 4, 512], ctx)

        half_cols = lambda h: slice(h * (F // 2), (h + 1) * (F // 2))
        with nc.Block() as block:
            @block.sync
            def _(sp):
                sp.dma_start(ends[:], w["L1_ffn_edge_index"].rearrange("i (p f) -> p i f", p=P)).then_inc(edges_in, 16)
                rows = w["L0_tok_emb"].rearrange("(p r) d -> p r d", p=parts)
                sp.dma_start(halo[:, 2:per + 2, :], rows).then_inc(table_in, 16)
                sp.dma_start(halo[1:parts, 0:2, :], rows[0:parts - 1, per - 2:per, :]).then_inc(table_in, 16)
                sp.dma_start(halo[0:parts - 1, per + 2:per + 4, :], rows[1:parts, 0:2, :]).then_inc(table_in, 16)
                for r in range(2):
                    sp.dma_start(halo[0:1, r, :], w["L0_tok_emb"][0:1, :]).then_inc(table_in, 16)
                    sp.dma_start(halo[parts - 1:parts, per + 2 + r, :], w["L0_tok_emb"][s.vocab - 1:s.vocab, :]).then_inc(table_in, 16)
                sp.wait_ge(zero_made, 1)
                for table in blank:
                    for i in range(table.shape[1] // piece):
                        sp.dma_start(table[:, i * piece:(i + 1) * piece], zeros[:]).then_inc(blanked, 16)
                sp.wait_ge(smoothed, 1)
                sp.dma_start(smooth.rearrange("(p r) d -> p r d", p=parts), acc[:]).then_inc(smooth_out, 16)
                sp.wait_ge(sorted_, 1)
                sp.dma_start(m.keys.rearrange("(p b) f -> p (b f)", p=P), ibuf[0]).then_inc(keys_out, 16)
                sp.dma_start(m.keys_before[1:s.edges + 1].rearrange("(p f) -> p f", p=P), ibuf[0]).then_inc(keys_out, 16)
                sp.dma_start(m.keys_before[0:1].rearrange("(o n) -> o n", o=1), sentinel[:]).then_inc(keys_out, 16)
                sp.dma_start(m.pivots, first[:].bitcast(I32)).then_inc(keys_out, 16)
                with nc.allow_non_contiguous_dma(reason="one key a partition"):
                    sp.dma_start(m.pivot_row.rearrange("o p -> p o"), first[:, 0:1].bitcast(I32)).then_inc(pivot_in, 16)
                sp.wait_ge(pivot_in, 16)
                sp.dma_start(m.pivot1[:], m.pivot_row.to_broadcast([P, P])).then_inc(pivot_in, 16)
                sp.wait_ge(pivot_in, 32)
                sp.wait_ge(keys_out, 64)
                sp.wait_ge(blanked, 16 * sum(table.shape[1] // piece for table in blank))

            @block.gpsimd
            def _(pool):
                pool.wait_ge(table_in, 16 * 7)
                pool.tensor_tensor(pair[:], halo[:, 1:per + 1, :], halo[:, 3:per + 3, :], ALU.add).then_inc(pair_summed, 1)
                pool.wait_ge(smooth_out, 16)
                for c in range(s.cols):
                    gather(pool, m.h[:, c, :], smooth, m.tok[:, c:c + 1]).then_inc(tokens_in, 16)
                pool.wait_ge(tokens_in, 16 * s.cols)

            @block.tensor
            def _(pe):
                for t in range(2 * TURNS):
                    pe.wait_ge(ready_to_turn, t + 1)
                    if t >= 2:
                        pe.wait_ge(half_copied, t - 1)
                    of = buf[m.turn_src[t // 2]][:, half_cols(t % 2)]
                    for k in range(8):
                        last = pe.transpose(turn_ps[:, 2 * (t % 2) + k // 4, (k % 4) * P:(k % 4 + 1) * P],
                                            of[:, k * P:(k + 1) * P], m.ident[:])
                    last.then_inc(turn_made, 1)

            @block.scalar
            def _(act):
                for t in range(2 * TURNS):
                    act.wait_ge(turn_made, t + 1)
                    act.copy(buf[1 - m.turn_src[t // 2]][:, half_cols(t % 2)],
                             turn_ps[:, 2 * (t % 2):2 * (t % 2) + 2, :].rearrange("p a b -> p (a b)")).then_inc(half_copied, 1)

            @block.vector
            def _(v):
                v.memset(sentinel[:], 0)
                v.memset(zeros[:], 0.0).then_inc(zero_made, 1)
                v.wait_ge(edges_in, 16)
                src, dst = ends[:, 0, :], ends[:, 1, :]
                v.tensor_scalar(ibuf[0], src, s.nodes - 1, None, ALU.is_ge)
                v.tensor_scalar(ibuf[1], dst, s.nodes, NODE_BITS + 1, ALU.bitwise_and, ALU.logical_shift_left)
                v.drain()
                v.tensor_scalar(ibuf[0], ibuf[0], 2 * NODE_BITS, KEY_BASE, ALU.logical_shift_left, ALU.bitwise_or)
                v.tensor_scalar(dst, dst, s.nodes - 1, NODE_BITS, ALU.bitwise_and, ALU.logical_shift_left)
                v.tensor_scalar(src, src, s.nodes - 1, None, ALU.bitwise_and)
                v.drain()
                v.tensor_tensor(ibuf[0], ibuf[0], ibuf[1], ALU.bitwise_or)
                v.tensor_tensor(dst, dst, src, ALU.bitwise_or)
                v.drain()
                v.tensor_tensor(ibuf[0], ibuf[0], dst, ALU.bitwise_or)
                v.wait_ge(table_in, 16 * 7)
                v.tensor_tensor(acc[:], halo[:, 0:per, :], halo[:, 4:per + 4, :], ALU.add)
                v.drain()
                v.tensor_scalar(acc[:], acc[:], 0.1, None, ALU.mult)
                v.drain()
                v.wait_ge(pair_summed, 1)
                v.scalar_tensor_tensor(acc[:], pair[:], 0.2, acc[:], ALU.mult, ALU.add)
                v.drain()
                v.scalar_tensor_tensor(acc[:], halo[:, 2:per + 2, :], 0.4, acc[:], ALU.mult, ALU.add).then_inc(smoothed, 1)

                state = {"cur": 0, "turn": 0}

                def negate(part):
                    v.tensor_scalar(part, part, -1.0, None, ALU.mult)
                    v.drain()

                def compare(stride, cols=slice(0, F), cur=None):
                    of = state["cur"] if cur is None else cur
                    a, b = (buf[of ^ i][:, cols].rearrange("p (a two s) -> p a two s", two=2, s=stride) for i in (0, 1))
                    v.tensor_tensor(b[:, :, 0, :], a[:, :, 0, :], a[:, :, 1, :], ALU.min)
                    v.tensor_tensor(b[:, :, 1, :], a[:, :, 0, :], a[:, :, 1, :], ALU.max)
                    v.drain()
                    if cur is None:
                        state["cur"] ^= 1

                free_bits = F.bit_length() - 1
                part_bits = 7
                phases = free_bits + part_bits
                for k in range(1, phases + 1):
                    cur = lambda: buf[state["cur"]][:]
                    if k == 1:
                        negate(cur().rearrange("p (a two s) -> p a two s", two=2, s=2)[:, :, 1, :])
                    elif k < free_bits:
                        negate(cur().rearrange("p (a four s) -> p a four s", four=4, s=1 << (k - 1))[:, :, 1:3, :])
                    elif k == free_bits:
                        negate(cur()[:, F // 2:F])
                        v.tensor_scalar(cur(), cur(), m.part_sign[:, 0:1], None, ALU.mult)
                        v.drain()
                    else:
                        turned = state["cur"] ^ 1
                        for h in range(2):
                            now = turned
                            v.wait_ge(half_copied, state["turn"] + h + 1)
                            mine = buf[now][:, half_cols(h)]
                            if k < phases:
                                negate(mine.rearrange("p (a four s) -> p a four s", four=4, s=1 << (k - 1 - free_bits))[:, :, 1:3, :])
                            else:
                                negate(mine.rearrange("p (a two s) -> p a two s", two=2, s=64)[:, :, 1, :])
                            for j in range(k - 1, free_bits - 1, -1):
                                compare(1 << (j - free_bits), half_cols(h), now)
                                now ^= 1
                            assert m.turn_src[state["turn"] // 2 + 1] == now
                            v.nop().then_inc(ready_to_turn, 1)
                        state["turn"] += 4
                        state["cur"] = now ^ 1
                        v.wait_ge(half_copied, state["turn"])
                    for j in range(min(k, free_bits) - 1, -1, -1):
                        if j == 0 and free_bits <= k < phases:
                            assert m.turn_src[state["turn"] // 2] == state["cur"] ^ 1
                            for h in range(2):
                                compare(1, half_cols(h), state["cur"])
                                v.nop().then_inc(ready_to_turn, 1)
                            state["cur"] ^= 1
                        else:
                            compare(1 << j)
                if state["cur"]:
                    v.tensor_copy(buf[0][:], buf[1][:])
                    v.drain()
                v.tensor_copy(first[:], buf[0][:].rearrange("p (a s) -> p a s", s=32)[:, :, 0])
                v.drain()
                v.nop().then_inc(sorted_, 1)


def turn_sources(s):
    free_bits, part_bits, cur, out = s.per_part.bit_length() - 1, 7, 0, []
    for k in range(1, free_bits + part_bits + 1):
        if k > free_bits:
            out.append(cur)
            cur ^= 1
            cur ^= (k - free_bits) & 1
            out.append(cur)
            cur ^= 1
        cur ^= min(k, free_bits) & 1
    return out


class Side:

    def __init__(self, order):
        self.filled, self.took, self.before = {}, {}, {}
        counts = {"a": 0, "v": 0}
        holder = {}
        for n, (item, banks, by) in enumerate(order):
            self.filled[item] = n + 1
            self.before[item] = [holder[b] for b in banks if b in holder]
            counts[by] += 1
            self.took[item] = (by, counts[by])
            for b in banks:
                holder[b] = item


def schedule(s, kind):
    T, H = s.tiles, s.heads
    own = kind in ("first", "middle", "last")
    tail = kind in ("middle", "last", "end")
    prep = kind in ("start", "first", "middle")
    early = H - EARLY_LEFT
    slots = [("a0", h) for h in range(H)] if own else []
    if tail:
        slots.insert(early if own else 0, ("a1", 0))
    steps = {}
    LATE = T * (early + 1) + 5

    def at(step, *events):
        steps.setdefault(step, []).extend(events)

    def norm(step, k):
        for part in range(4):
            at(step + part, ("norm", k, part))

    if own:
        for c in range(T):
            at(c // 2, ("values", c))
        ready = STARTED if kind == "first" else early
        for i in range(2 * (H - ready)):
            at(4 + i, ("project", ready + i // 2, i % 2, 0))
        for i, step in enumerate((36, 37, 49, 50, 62)):
            at(step, ("search", i))
    if tail:
        norm(3, 2)
        at(8, ("turn", 2))
        at(9, ("hidden", 0))
        at(10, ("hidden", 1))
        at(12, ("gate", 0))
        at(13, ("gate", 1))
        at(14, ("gate", 2))
        for c in range(T):
            at(15 + c, ("routed", c), ("mix", c))
        norm(25, 3)
        at(30, ("turn", 3))
        at(31, ("project1", 0))
        at(32, ("project1", 1))
        at(33, ("values1",))
        norm(LATE, 4)
        at(LATE + 5, ("turn", 4))
        at(LATE + 6, ("nodes",))
    if prep:
        norm(30, 1)
        at(35, ("turn", 1))
        for h in range(early if own else STARTED):
            first = max(37 + 2 * h, T * (h + 1))
            at(first, ("project", h, 0, 1))
            at(first + 1, ("project", h, 1, 1))

    def whole_shift(j):
        return [("max", j, t, u) for t in range(T) for u in range(2)] + [("shift", j, u) for u in range(2)]

    events = []
    if kind == "end":
        events += [("context", -1, u) for u in range(2)]
    if not own:
        for step in sorted(steps):
            if step < LATE:
                events += steps[step]
    n = 0
    if slots and not own:
        events += whole_shift(0)
    for j in range(len(slots)):
        follows = j + 1 < len(slots) or (own and prep)
        maxima = [("max", j + 1, t, u) for t in range(T) for u in range(2)] if follows else []
        for c in range(T):
            kept = (0, 1) if own and tail and j == 0 else (3, 4)
            ring = [maxima.pop(0) if maxima and c < T - 2 and not (place == 1 and c in kept) else None for place in range(3)]
            if j and c in (3, 4):
                ring[1] = ("context", j - 1, c - 3)
            if own and tail and j == 0 and c < 2:
                ring[1] = ("context", -1, c)
            if follows and c == T - 2:
                ring[1:3] = [("shift", j + 1, 0), ("shift", j + 1, 1)]
            weigh = [("weigh", *divmod(n - LAG, T), u) for u in range(2)] if n >= LAG else [None, None]
            now = steps.get(n, []) if own else []
            alone = [e for e in now if e[0] in ("norm", "mix", "search") or e in (("gate", 1), ("gate", 2))]
            events += [("score", j, c), ring[0], *(e for e in now if e not in alone), weigh[0], ring[1], weigh[1], ring[2], *alone]
            n += 1
        assert not maxima
    for i in range(max(0, n - LAG), n):
        events += [("weigh", *divmod(i, T), u) for u in range(2)]
    if slots:
        if not own:
            events += [("context", len(slots) - 1, u) for u in range(2)]
        for step in sorted(steps):
            if step >= (n if own else LATE):
                events += steps[step]
    elif prep:
        events += whole_shift(0)
    return slots, [e for e in events if e]


EARLY_LEFT = 2
STARTED = 2
LAG = 2
PROBS = 4


def tower(core, s, m, w):
    nc = core.nc
    T, D, H, R = s.tiles, s.dim, s.heads, s.rank
    half = s.steps // 2
    hc = s.hidden // P
    NE = s.experts0
    QC = s.query_cols
    m.x4T = core.sb("x4T", [D, s.nodes])
    m.node = core.sb("node", [P, s.cols, 24])
    m.starts = core.sb("starts", [P, s.rows, QC])
    m.begin = core.sb("begin", [P, 2, s.cols])
    m.after = core.sb("after", [P, 2, s.cols])
    m.active = core.sb("active", [P, 1], I32)
    m.place_i = core.sb("place_i", [P, s.cols], I32)
    sem = core.sem
    filled = sem("tw_filled")
    a_took = sem("tw_a_took")
    v_took = sem("tw_v_took")
    high_taken = sem("tw_high_taken")
    varied = sem("tw_varied")
    rooted = sem("tw_rooted")
    normed = sem("tw_normed")
    gated = sem("tw_gated")
    gate_exped = sem("tw_gate_exped")
    ring_filled = sem("tw_ring_filled")
    ring_free = sem("tw_ring_free")
    shift_turned = sem("tw_shift_turned")
    shift_placed = sem("tw_shift_placed")
    shift_ready = sem("tw_shift_ready")
    scored = sem("tw_scored")
    exped = sem("tw_exped")
    weighted = sem("tw_weighted")
    context_out = sem("tw_context_out")
    where_ready = sem("tw_where_ready")
    early_scattered = sem("tw_early_scattered")
    piv_in = sem("tw_piv_in")
    blk_in = sem("tw_blk_in")
    counted = [filled, a_took, v_took, high_taken, varied, rooted, normed, gated, gate_exped, ring_filled, ring_free,
               shift_turned, shift_placed, shift_ready, scored, exped, weighted, context_out, where_ready]

    with ExitStack() as ctx:
        sb = lambda name, shape, dt=F32: core.sb("tw_" + name, shape, dt, ctx)
        xln = [sb("xln0", [P, T, 2, D]), sb("xln1", [P, T, D])]
        sq = sb("sq", [P, T, D])
        stat = sb("stat", [P, 4, T])
        pairT = sb("pairT", [P, s.steps], F16)
        xT = sb("xT", [D, s.steps])
        q0 = sb("q0", [3 * R + 1, H, s.steps], F16)
        k0 = sb("k0", [3 * R + 1, H, s.steps], F16)
        q1 = sb("q1", [2 * D, s.steps], F16)
        k1 = sb("k1", [2 * D, s.steps], F16)
        q1s = sb("q1s", [D + 1, s.steps], F16)
        k1s = sb("k1s", [D + 1, s.steps], F16)
        V0 = sb("V0", [P, T, H, 65])
        V1 = sb("V1", [P, T, 65])
        HT = sb("HT", [P, hc, s.steps])
        probs = sb("probs", [P, PROBS, s.steps])
        context = sb("context", [65, 2, s.steps])
        maxima = sb("maxima", [P, 2, T, 2])
        shift = sb("shift", [P, 2, T], F16)
        ident16 = sb("ident16", [P, P], F16)
        recip = sb("recip", [P, T // 2])
        part = sb("part", [P, T, D])
        routed_sum = sb("routed_sum", [P, T, D])
        logit = sb("logit", [P, T, NE])
        gate = sb("gate", [P, T, NE])
        small = sb("small", [P, 4, T])
        mixed = sb("mixed", [P, NE, D])
        piv2 = sb("piv2", [P, QC, 64], I32)
        blk = sb("blk", [P, QC, 32], I32)
        cmp = sb("cmp", [P, QC, P])
        where = sb("where", [P, 3, QC])
        row_i = sb("row_i", [P, QC], I32)
        blk_i = sb("blk_i", [P, QC], I32)
        ring = core.ps("ring", [P, 2, 512], ctx)
        score = core.ps("score", [P, 2, 512], ctx)
        sums = core.ps("sums", [65, 2, 512], ctx)
        side = core.ps("side", [P, 2, 512], ctx)

        with nc.Block() as block:
            @block.vector
            def _(v):
                v.memset(k0[3 * R:3 * R + 1, :, :], 1.0)
                v.memset(k1s[D:D + 1, :], 1.0)
                v.memset(V0[:, :, :, 64:65], 1.0)
                v.memset(V1[:, :, 64:65], 1.0)
                v.tensor_copy(ident16[:], m.ident[:])

        banks = {"turn": (0, 1), "project": (0, 1), "project1": (0, 1), "hidden": (0, 1), "gate": (0,), "values1": (0,), "nodes": (0,)}
        taker = {"turn": "a", "project": "v", "project1": "v", "hidden": "a", "gate": "v", "values1": "v", "nodes": "v",
                 "routed": "v"}

        def run(kind, row):
            slots, events = schedule(s, kind)
            own = kind in ("first", "middle", "last")
            order = []
            for e in events:
                if e[0] in ("values", "routed"):
                    order.append((e, (e[1] % 2,), "a" if e[0] == "values" else "v"))
                elif e[0] in banks and e not in (("gate", 1), ("gate", 2)):
                    order.append((e, banks[e[0]], "v" if e == ("turn", 1) else taker[e[0]]))
            items = Side(order)
            took_sem = {"a": a_took, "v": v_took}

            def wait_taken(eng, item):
                if item in items.took:
                    by, count = items.took[item]
                    eng.wait_ge(took_sem[by], count)

            def cols_of(which):
                return bass.ts(row + which, T) if which else bass.ts(row, T)

            norm_number = {k: i + 1 for i, k in enumerate(x[1] for x in events if x[0] == "norm" and x[2] == 0)}

            def buffer(j):
                return 0 if j < 0 else (len(slots) - 1 - j) % 2

            norm_row = {1: 1, 2: -1, 3: -1, 4: -1}

            def operands(j):
                if j < 0:
                    return (None, None, (), None, None, -1, 1.0)
                name, h = slots[j] if j < len(slots) else ("a0", 0)
                if name == "a0":
                    return (q0[0:R, h, :], k0[0:R, h, :], ((k0[:, h, :], q0[:, h, :]),), lambda c: V0[:, c, h, :],
                            q0[3 * R:3 * R + 1, h, :], 0, 1.0)
                return (q1[0:D, :], k1[0:D, :], ((k1[:], q1[:]), (k1s[:], q1s[:])), lambda c: V1[:, c, :],
                        q1s[D:D + 1, :], -1, D ** -0.5)

            def operand_items(j):
                if j == len(slots):
                    return [("project", 0, i, 1) for i in range(2)]
                name, h = slots[j]
                if name == "a1":
                    return [("project1", i) for i in range(2)]
                return [("project", h, i, 0) for i in range(2)]

            def value_item(j, c):
                return ("values", c) if slots[j][0] == "a0" else ("values1",)

            with nc.Block() as block:
                @block.gpsimd
                def _(pool):
                    norms = searches = columns = 0

                    def scatter(count):
                        nonlocal columns
                        for _ in range(count if kind == "end" else 0):
                            scatter_scores(pool, s, m, columns, early_scattered)
                            columns += 1

                    for e in events:
                        if e[0] == "norm" and e[2] == 2:
                            norms += 1
                            pool.wait_ge(varied, norms)
                            pool.tensor_scalar(stat[:, 2, :], stat[:, 1, :], 1.0 / D, 1e-5, ALU.mult, ALU.add)
                            pool.drain()
                            pool.tensor_tensor(stat[:, 3, :], stat[:, 2, :], m.minus_half[:, 0:T], ALU.pow).then_inc(rooted, 1)
                            scatter(2 * T)
                        elif e == ("search", 1):
                            pool.wait_ge(where_ready, 1)
                            for j in range(QC):
                                gather(pool, piv2[:, j, :], m.pivots, row_i[:, j:j + 1]).then_inc(piv_in, 16)
                            searches += 1
                        elif e == ("search", 3):
                            pool.wait_ge(where_ready, 2)
                            for j in range(QC):
                                gather(pool, blk[:, j, :], m.keys, blk_i[:, j:j + 1]).then_inc(blk_in, 16)
                    if kind == "end":
                        scatter((s.rows - 1) * T - columns)
                        pool.wait_ge(early_scattered, 16 * (s.rows - 1) * T)
                    if searches:
                        pool.wait_ge(piv_in, 16 * QC)
                        pool.wait_ge(blk_in, 16 * QC)

                @block.tensor
                def _(pe):
                    shifts = 0
                    emptied = []
                    counts = {"v": 0, "a": 0}

                    def ring_slot(by):
                        if len(emptied) >= 2:
                            pe.wait_ge(*emptied[-2])
                        counts[by] += 1
                        emptied.append((ring_free if by == "v" else shift_placed, counts[by]))
                        return (len(emptied) - 1) % 2

                    def wide(left, right):
                        for u in range(2):
                            last = pe.matmul(side[0:left.shape[1], u, :], left, right[:, u * half:(u + 1) * half], start=True, stop=True)
                        return last

                    for e in events:
                        name = e[0]
                        if e in items.filled:
                            for old in items.before[e]:
                                wait_taken(pe, old)
                        if name == "max":
                            _, j, t, u = e
                            qm, km = operands(j)[0:2]
                            if (t, u) == (0, 0):
                                for i in operand_items(j):
                                    wait_taken(pe, i)
                            pe.matmul(ring[:, ring_slot("v"), :], qm[:, t * P:(t + 1) * P], km[:, u * half:(u + 1) * half],
                                      start=True, stop=True).then_inc(ring_filled, 1)
                        elif name == "shift":
                            _, j, u = e
                            if u == 0:
                                shifts += 1
                                pe.wait_ge(shift_ready, shifts)
                            b = ring_slot("a")
                            for i in range(T // 2):
                                c = u * T // 2 + i
                                last = pe.matmul(ring[0:1, b, i * P:(i + 1) * P], shift[:, j % 2, c:c + 1], ident16[:],
                                                 start=True, stop=True)
                            last.then_inc(shift_turned, 1)
                        elif name == "context":
                            _, j, u = e
                            if j >= 0:
                                pe.wait_ge(context_out, j + 1)
                            b = ring_slot("v")
                            for i in range(T // 2):
                                c = u * T // 2 + i
                                last = pe.transpose(ring[:, b, i * 65:(i + 1) * 65], context[:, buffer(j), c * P:(c + 1) * P],
                                                    m.ident[0:65, 0:65])
                            last.then_inc(ring_filled, 1)
                        elif name == "score":
                            _, j, c = e
                            n = j * T + c
                            if c == 0 and shifts:
                                pe.wait_ge(shift_placed, 2 * shifts)
                            pairs = operands(j)[2]
                            for u in range(2):
                                if n:
                                    pe.wait_ge(exped, 2 * n - 1 + u)
                                for i, (kside, qside) in enumerate(pairs):
                                    last = pe.matmul(score[:, u, :], kside[:, c * P:(c + 1) * P], qside[:, u * half:(u + 1) * half],
                                                     start=(i == 0), stop=(i == len(pairs) - 1))
                                last.then_inc(scored, 1)
                        elif name == "weigh":
                            _, j, c, u = e
                            if u == 0:
                                pe.wait_ge(exped, 2 * (j * T + c) + 2)
                                wait_taken(pe, value_item(j, c))
                                if c == 0 and j:
                                    pe.wait_ge(context_out, j)
                            last = pe.matmul(sums[:, u, :], operands(j)[3](c), probs[:, (j * T + c) % PROBS, u * half:(u + 1) * half],
                                             start=(c == 0), stop=(c == T - 1))
                            if u:
                                last.then_inc(weighted, 1)
                        elif name == "turn":
                            pe.wait_ge(normed, norm_number[e[1]])
                            for c in range(T):
                                of = xln[0][:, c].rearrange("p i d -> p (i d)") if e[1] == 1 else xln[1][:, c, :]
                                last = pe.transpose(side[0:of.shape[1], c // 4, (c % 4) * P:(c % 4 + 1) * P], of, m.ident[:])
                            last.then_inc(filled, 1)
                        elif name == "project":
                            if e[3]:
                                wait_taken(pe, ("turn", 1))
                            high, low = (a[:, e[2], e[1]].rearrange("d a r -> d (a r)") for a in (m.qk_high, m.qk_low))
                            for u in range(2):
                                tokens = slice(u * half, (u + 1) * half)
                                pe.matmul(side[0:3 * R, u, :], high, pairT[:, tokens], start=True, stop=False)
                                last = pe.matmul(side[0:3 * R, u, :], low, pairT[0:D, tokens], start=False, stop=True)
                            last.then_inc(filled, 1)
                        elif name == "values":
                            tile = slice(e[1] * P, (e[1] + 1) * P)
                            pe.matmul(side[:, e[1] % 2, :], pairT[:, tile], m.vo_high[:].rearrange("d h e -> d (h e)"),
                                      start=True, stop=False)
                            pe.matmul(side[:, e[1] % 2, :], pairT[0:D, tile], m.vo_low[:].rearrange("d h e -> d (h e)"),
                                      start=False, stop=True).then_inc(filled, 1)
                        elif name == "hidden":
                            wait_taken(pe, ("turn", 2))
                            wide(m.w1[:, e[1] * P:(e[1] + 1) * P], xT).then_inc(filled, 1)
                        elif e == ("gate", 0):
                            wait_taken(pe, ("hidden", hc - 1))
                            for c in range(T):
                                for k in range(hc):
                                    last = pe.matmul(side[:, 0, c * NE:(c + 1) * NE], HT[:, k, c * P:(c + 1) * P], m.wg[:, k, :],
                                                     start=(k == 0), stop=(k == hc - 1))
                            last.then_inc(filled, 1)
                        elif name == "routed":
                            for k in range(hc):
                                last = pe.matmul(side[:, e[1] % 2, :], HT[:, k, e[1] * P:(e[1] + 1) * P],
                                                 m.wd[:, k, :, :].rearrange("p e d -> p (e d)"), start=(k == 0), stop=(k == hc - 1))
                            last.then_inc(filled, 1)
                        elif name == "project1":
                            wait_taken(pe, ("turn", 3))
                            wide((m.wq1T, m.wk1T)[e[1]][:].rearrange("d a e -> d (a e)"), xT).then_inc(filled, 1)
                        elif name == "values1":
                            for c in range(T):
                                last = pe.matmul(side[:, 0, c * D:(c + 1) * D], xT[:, c * P:(c + 1) * P], m.wv1T[:], start=True, stop=True)
                            last.then_inc(filled, 1)
                        elif name == "nodes":
                            wait_taken(pe, ("turn", 4))
                            for c in range(T):
                                last = pe.matmul(side[:, 0, c * 24:(c + 1) * 24], xT[:, c * P:(c + 1) * P], m.wnode[:], start=True, stop=True)
                            last.then_inc(filled, 1)

                @block.scalar
                def _(act):
                    def copy_out(j):
                        act.wait_ge(weighted, (j + 1) * T)
                        act.copy(context[:, buffer(j), :], sums[:].rearrange("p a b -> p (a b)")).then_inc(context_out, 1)

                    both = side[:].rearrange("p a b -> p (a b)")
                    slots_turned, ring_n = 0, -1
                    for e in events:
                        name = e[0]
                        ring_n += name in ("max", "shift", "context")
                        if e in items.filled and name not in ("routed", "values1", "nodes", "gate"):
                            act.wait_ge(filled, items.filled[e])
                        if name == "score":
                            _, j, c = e
                            n = j * T + c
                            for u in range(2):
                                act.wait_ge(scored, 2 * n + u + 1)
                                if u == 0 and n >= PROBS:
                                    act.wait_ge(weighted, n - PROBS + 1)
                                act.activation(probs[:, n % PROBS, u * half:(u + 1) * half], score[:, u, :], ACT.Exp).then_inc(exped, 1)
                        elif name == "shift":
                            slots_turned += 1
                            act.wait_ge(shift_turned, slots_turned)
                            act.copy(operands(e[1])[4][:, e[2] * half:(e[2] + 1) * half], ring[0:1, ring_n % 2, :]).then_inc(shift_placed, 1)
                        elif name == "weigh":
                            if e[2:] == (T - 1, 1):
                                copy_out(e[1])
                        elif name == "turn":
                            if e[1] == 1:
                                act.copy(pairT[:], both).then_inc(high_taken, 1)
                            else:
                                act.copy(xT[:], both[0:D, :]).then_inc(a_took, 1)
                            if e[1] == 4:
                                act.drain()
                                act.copy(m.x4T[:, bass.ts(row - 1, s.steps)], xT[:])
                        elif name == "project":
                            act.activation((q0, k0)[e[2]][0:3 * R, e[1], :], both[0:3 * R, :], ACT.Copy,
                                           scale=1 / WEIGHT_SCALE).then_inc(high_taken, 1)
                        elif name == "project1":
                            act.copy((q1, k1)[e[1]][:], both).then_inc(high_taken, 1)
                        elif name == "values":
                            act.activation(V0[:, e[1], :, 0:64], side[:, e[1] % 2, :].rearrange("p (h e) -> p h e", e=D), ACT.Copy,
                                           scale=1 / WEIGHT_SCALE).then_inc(a_took, 1)
                        elif name == "hidden":
                            act.activation(HT[:, e[1], :], both, ACT.Gelu, bias=m.b1[:, e[1]:e[1] + 1]).then_inc(a_took, 1)
                        elif e == ("gate", 0):
                            act.wait_ge(gated, 1)
                            act.activation(logit[:], logit[:], ACT.Exp).then_inc(gate_exped, 1)

                @block.vector
                def _(v):
                    if own:
                        query = m.query[:, bass.ts(row, 1), :].rearrange("p a b -> p (a b)")
                        queries = lambda width: query.bitcast(F32)[:, :, None].to_broadcast([P, QC, width])
                    ring_n = highs = mine = 0
                    both = side[:].rearrange("p a b -> p (a b)")
                    for e in events:
                        name = e[0]
                        if e in items.filled and name in ("routed", "values1", "nodes", "gate"):
                            v.wait_ge(filled, items.filled[e])
                        if name == "max":
                            mine += 1
                            v.wait_ge(ring_filled, mine)
                            v.tensor_reduce(maxima[:, e[1] % 2, e[2], e[3]:e[3] + 1], ring[:, ring_n % 2, :], X, ALU.max).then_inc(ring_free, 1)
                            ring_n += 1
                            if e[2:] == (T - 1, 1):
                                v.drain()
                                v.tensor_reduce(shift[:, e[1] % 2, :], maxima[:, e[1] % 2, :, :], X, ALU.max, negate=True).then_inc(shift_ready, 1)
                        elif name == "shift":
                            ring_n += 1
                        elif name == "context":
                            which, scale = operands(e[1])[5:7]
                            u = e[2]
                            mine += 1
                            v.wait_ge(ring_filled, mine)
                            ctx_ps = ring[:, ring_n % 2, 0:T // 2 * 65].rearrange("p (i e) -> p i e", e=65)
                            tiles = slice(u * T // 2, (u + 1) * T // 2)
                            v.reciprocal(recip[:], ctx_ps[:, :, 64])
                            v.drain()
                            if scale != 1.0:
                                v.tensor_scalar(recip[:], recip[:], scale, None, ALU.mult)
                                v.drain()
                            v.tensor_tensor(part[:, tiles, :], ctx_ps[:, :, 0:64], recip[:, :, None].to_broadcast([P, T // 2, 64]),
                                            ALU.mult).then_inc(ring_free, 1)
                            v.drain()
                            ring_n += 1
                            if u:
                                res = m.h[:, cols_of(which), :]
                                v.tensor_tensor(res, res, part[:], ALU.add)
                                v.drain()
                        elif name == "norm":
                            res = m.h[:, cols_of(norm_row[e[1]]), :]
                            doubled = e[1] == 1
                            centred = xln[0][:, :, 0, :] if doubled else xln[1][:]
                            v.drain()
                            if e[2] == 0:
                                v.tensor_reduce(stat[:, 0, :], res, X, ALU.add)
                                v.drain()
                                v.tensor_scalar(stat[:, 0, :], stat[:, 0, :], 1.0 / D, None, ALU.mult)
                            elif e[2] == 1:
                                v.tensor_tensor(centred, res, stat[:, 0, :, None].to_broadcast([P, T, D]), ALU.subtract)
                                v.drain()
                                v.tensor_tensor(sq[:], centred, centred, ALU.mult)
                            elif e[2] == 2:
                                v.tensor_reduce(stat[:, 1, :], sq[:], X, ALU.add).then_inc(varied, 1)
                            else:
                                v.wait_ge(rooted, norm_number[e[1]])
                                root = stat[:, 3, :, None].to_broadcast([P, T, D])
                                if doubled:
                                    v.tensor_tensor(xln[0][:, :, 1, :], centred, root, ALU.mult)
                                    v.drain()
                                v.tensor_tensor(centred, centred, root, ALU.mult).then_inc(normed, 1)
                        elif e == ("turn", 1):
                            highs += 1
                            v.wait_ge(high_taken, highs)
                            v.tensor_tensor(pairT[D:P, :], both[D:P, :], pairT[D:P, :], ALU.subtract).then_inc(v_took, 1)
                        elif name == "project":
                            highs += 1
                            v.wait_ge(high_taken, highs)
                            at_ = (2 - e[2]) * R
                            low = (q0, k0)[e[2]][at_:at_ + R, e[1], :]
                            v.scalar_tensor_tensor(low, both[at_:at_ + R, :], 1 / WEIGHT_SCALE, low, ALU.mult, ALU.subtract).then_inc(v_took, 1)
                        elif name == "project1":
                            highs += 1
                            v.wait_ge(high_taken, highs)
                            if e[1] == 0:
                                v.tensor_copy(q1s[0:D, :], q1[0:D, :])
                                v.tensor_tensor(q1[D:2 * D, :], both[D:2 * D, :], q1[D:2 * D, :], ALU.subtract).then_inc(v_took, 1)
                            else:
                                v.tensor_tensor(k1s[0:D, :], both[0:D, :], k1[0:D, :], ALU.subtract).then_inc(v_took, 1)
                        elif name == "values1":
                            v.tensor_copy(V1[:, :, 0:64], side[:, 0, :].rearrange("p (c e) -> p c e", e=D)).then_inc(v_took, 1)
                        elif name == "nodes":
                            v.tensor_copy(m.node[:, cols_of(-1), :], side[:, 0, 0:T * 24].rearrange("p (c f) -> p c f", f=24)).then_inc(v_took, 1)
                        elif e == ("gate", 0):
                            v.tensor_tensor(logit[:], side[:, 0, 0:T * NE].rearrange("p (c e) -> p c e", e=NE),
                                            m.bg[:, None, :].to_broadcast([P, T, NE]), ALU.add).then_inc(v_took, 1)
                            v.drain()
                            v.tensor_reduce(small[:, 0, :], logit[:], X, ALU.max)
                            v.drain()
                            v.tensor_tensor(logit[:], logit[:], small[:, 0, :, None].to_broadcast([P, T, NE]), ALU.subtract).then_inc(gated, 1)
                        elif e == ("gate", 1):
                            v.wait_ge(gate_exped, 1)
                            v.tensor_reduce(small[:, 1, :], logit[:], X, ALU.add)
                            v.drain()
                            v.reciprocal(small[:, 1, :], small[:, 1, :])
                            v.drain()
                            v.tensor_tensor(logit[:], logit[:], small[:, 1, :, None].to_broadcast([P, T, NE]), ALU.mult)
                            v.drain()
                        elif e == ("gate", 2):
                            v.tensor_reduce(small[:, 2, :], logit[:], X, ALU.max)
                            v.drain()
                            v.tensor_tensor(gate[:], logit[:], small[:, 2, :, None].to_broadcast([P, T, NE]), ALU.is_equal)
                            v.drain()
                            v.tensor_tensor(gate[:], gate[:], m.first_slot[:, None, 0:NE].to_broadcast([P, T, NE]), ALU.mult)
                            v.drain()
                            v.tensor_reduce(small[:, 3, :], gate[:], X, ALU.max)
                            v.drain()
                            v.tensor_tensor(gate[:], gate[:], small[:, 3, :, None].to_broadcast([P, T, NE]), ALU.is_equal)
                            v.drain()
                            v.tensor_tensor(gate[:], gate[:], logit[:], ALU.mult)
                            v.drain()
                        elif name == "routed":
                            c = e[1]
                            v.tensor_tensor(mixed[:], side[:, c % 2, :].rearrange("p (e d) -> p e d", d=D), m.bd[:], ALU.add).then_inc(v_took, 1)
                            v.drain()
                        elif name == "mix":
                            c = e[1]
                            v.tensor_tensor(mixed[:], mixed[:], gate[:, c, :, None].to_broadcast([P, NE, D]), ALU.mult)
                            v.drain()
                            v.tensor_reduce(routed_sum[:, c, :], mixed[:].rearrange("p e d -> p d e"), X, ALU.add)
                            v.drain()
                            if c == T - 1:
                                res = m.h[:, cols_of(-1), :]
                                v.tensor_tensor(res, res, routed_sum[:], ALU.add)
                        elif e == ("search", 0):
                            v.tensor_tensor(cmp[:], m.pivot1[:].bitcast(F32)[:, None, :].to_broadcast([P, QC, P]), queries(P), ALU.is_lt)
                            v.drain()
                        elif e == ("search", 1):
                            v.tensor_reduce(where[:, 0, :], cmp[:], X, ALU.add)
                            v.drain()
                            v.tensor_scalar(where[:, 0, :], where[:, 0, :], 1.0, 0.0, ALU.subtract, ALU.max)
                            v.drain()
                            v.tensor_copy(row_i[:], where[:, 0, :]).then_inc(where_ready, 1)
                        elif e == ("search", 2):
                            v.wait_ge(piv_in, 16 * QC)
                            v.tensor_tensor(cmp[:, :, 0:64], piv2[:].bitcast(F32), queries(64), ALU.is_lt)
                            v.drain()
                        elif e == ("search", 3):
                            v.tensor_reduce(where[:, 1, :], cmp[:, :, 0:64], X, ALU.add)
                            v.drain()
                            v.tensor_scalar(where[:, 1, :], where[:, 1, :], 1.0, 0.0, ALU.subtract, ALU.max)
                            v.drain()
                            v.scalar_tensor_tensor(where[:, 1, :], where[:, 0, :], 64.0, where[:, 1, :], ALU.mult, ALU.add)
                            v.drain()
                            v.tensor_copy(blk_i[:], where[:, 1, :]).then_inc(where_ready, 1)
                        elif e == ("search", 4):
                            v.wait_ge(blk_in, 16 * QC)
                            v.tensor_tensor(cmp[:, :, 0:32], blk[:].bitcast(F32), queries(32), ALU.is_lt)
                            v.drain()
                            v.tensor_reduce(where[:, 2, :], cmp[:, :, 0:32], X, ALU.add)
                            v.drain()
                            v.scalar_tensor_tensor(m.starts[:, bass.ts(row, 1), :].rearrange("p a b -> p (a b)"), where[:, 1, :], 32.0,
                                                   where[:, 2, :], ALU.mult, ALU.add)

            core.clear(counted, (piv_in, blk_in) if own else ())

        run("start", -1)
        run("first", 0)
        with nc.Fori(1, s.rows - 1) as b:
            run("middle", b)
        run("last", s.rows - 1)
        run_places(core, s, m, side)
        run("end", s.rows)


def run_places(core, s, m, ps):
    nc = core.nc
    C = s.cols
    start_line = core.dram("start_line", [s.rows * s.query_cols * P])
    sem = core.sem
    starts_turned = sem("starts_turned")
    starts_placed = sem("starts_placed")
    starts_written = sem("starts_written")
    starts_read = sem("starts_read")
    runs_turned = sem("runs_turned")
    NQ = s.rows * s.query_cols
    with ExitStack() as ctx:
        sb = lambda name, shape, dt=F32: core.sb("rp_" + name, shape, dt, ctx)
        startsT = sb("startsT", [P, 2, P])
        line = sb("line", [2 * C, 2, P])
        place = sb("place", [P, C])
        with nc.Block() as block:
            @block.vector
            def _(v):
                v.wait_ge(starts_turned, 1)
                v.tensor_copy(startsT[:, 0, :], ps[:, 0, 0:P])
                v.tensor_copy(startsT[0:NQ - P, 1, :], ps[0:NQ - P, 0, P:2 * P]).then_inc(starts_placed, 1)
                v.wait_ge(runs_turned, 1)
                v.tensor_copy(m.begin[:].rearrange("p i c -> p (i c)"), ps[:, 1, 0:2 * C])
                v.tensor_copy(m.after[:].rearrange("p i c -> p (i c)"), ps[:, 1, 2 * C:4 * C])
                v.drain()
                v.tensor_tensor(place[:], m.begin[:, 0, :], m.after[:, 0, :], ALU.is_equal)
                v.drain()
                v.scalar_tensor_tensor(place[:], place[:], 2.0 * s.edges, m.begin[:, 0, :], ALU.mult, ALU.add)
                v.drain()
                v.tensor_copy(m.place_i[:], place[:])
                v.tensor_copy(m.active[:], m.begin[:, 1, 0:1])
                v.drain()
                v.tensor_scalar(m.active[:], m.active[:], P * s.group_t - 1, None, ALU.add)
                v.drain()
                v.tensor_scalar(m.active[:], m.active[:], (P * s.group_t).bit_length() - 1, None, ALU.logical_shift_right)

            @block.tensor
            def _(pe):
                flat = m.starts[:].rearrange("p b j -> p (b j)")
                pe.transpose(ps[:, 0, 0:P], flat[:, 0:P], m.ident[:])
                pe.transpose(ps[0:NQ - P, 0, P:2 * P], flat[:, P:NQ], m.ident[:]).then_inc(starts_turned, 1)
                pe.wait_ge(starts_read, 32)
                pe.transpose(ps[:, 1, 0:2 * C], line[:, 0, :], m.ident[:])
                pe.transpose(ps[:, 1, 2 * C:4 * C], line[:, 1, :], m.ident[:]).then_inc(runs_turned, 1)

            @block.sync
            def _(sp):
                sp.wait_ge(starts_placed, 1)
                sp.dma_start(start_line[0:P * P].rearrange("(c p) -> c p", p=P), startsT[:, 0, :]).then_inc(starts_written, 16)
                sp.dma_start(start_line[P * P:NQ * P].rearrange("(c p) -> c p", p=P), startsT[0:NQ - P, 1, :]).then_inc(starts_written, 16)
                sp.wait_ge(starts_written, 32)
                sp.dma_start(line[:, 0, :], start_line[0:2 * s.nodes].rearrange("(c p) -> c p", p=P)).then_inc(starts_read, 16)
                sp.dma_start(line[:, 1, :], start_line[1:2 * s.nodes + 1].rearrange("(c p) -> c p", p=P)).then_inc(starts_read, 16)


def scatter_scores(pool, s, m, c, done):
    pool.indirect_dma_start(out=m.dst_line, out_offset=bass.IndirectOffsetOnAxis(ap=m.place_i[:, c:c + 1], axis=0),
                            in_=m.node[:, c, 20:24], in_offset=None, bounds_check=s.edges - 1,
                            oob_is_err=False).then_inc(done, 16)


def node_tables(core, s, m):
    nc = core.nc
    C = s.cols
    m.table = core.dram("table", [s.nodes, 24])
    m.dst_table = core.dram("dst_table", [s.nodes, 4])
    m.last_row = core.sb("last_row", [P, 24])
    sem = core.sem
    rows_built = sem("rows_built")
    written = sem("tables_written")
    scattered = sem("scattered")
    with ExitStack() as ctx:
        rows = core.sb("nt_rows", [P, C, 24], F32, ctx)
        with nc.Block() as block:
            @block.vector
            def _(v):
                for h in range(4):
                    v.tensor_copy(rows[:, :, 5 * h:5 * h + 4], m.node[:, :, 4 * h:4 * h + 4])
                    v.memset(rows[:, :, 5 * h + 4:5 * h + 5], 1.0)
                v.tensor_copy(rows[:, :, 20:24], m.node[:, :, 16:20])
                v.drain()
                v.nop().then_inc(rows_built, 1)

            @block.sync
            def _(sp):
                sp.dma_start(m.dst_table.rearrange("(c p) f -> p c f", p=P), m.node[:, :, 20:24]).then_inc(written, 16)
                sp.wait_ge(rows_built, 1)
                sp.dma_start(m.table.rearrange("(c p) f -> p c f", p=P), rows[:]).then_inc(written, 16)
                sp.wait_ge(written, 32)
                sp.dma_start(m.last_row[:], m.table[s.nodes - 1:s.nodes, :].to_broadcast([P, 24])).then_inc(written, 16)
                sp.wait_ge(written, 48)

            @block.gpsimd
            def _(pool):
                for c in range(C - s.tiles, C):
                    scatter_scores(pool, s, m, c, scattered)
                pool.wait_ge(scattered, 16 * s.tiles)


def edges(core, s, m, w):
    nc = core.nc
    TT, G = s.group_t, s.groups
    NX = s.experts1
    D = s.dim
    m.row_sum = core.sb("row_sum", [P, G, 20])
    m.row_max = core.sb("row_max", [P, G, 4])
    m.row_open = core.sb("row_open", [P, G])
    m.expert = core.sb("expert", [P, s.cols, NX, D])
    sem = core.sem
    keys_in = sem("ed_keys_in")
    fills_in = sem("ed_fills_in")
    stored = sem("ed_stored")
    src_ready = sem("ed_src_ready")
    gathered = sem("ed_gathered")
    row_dst_in = sem("ed_row_dst_in")
    logits_ready = sem("ed_logits_ready")
    exped = sem("ed_exped")
    row_built = sem("ed_row_built")
    hid_scored = sem("ed_hid_scored")
    hid_taken = sem("ed_hid_taken")
    exp_scored = sem("ed_exp_scored")
    tokens_copied = sem("ed_tokens_copied")
    exp_taken = sem("ed_exp_taken")
    base = 9
    rounds = base - 1
    CPG = s.cols // rounds
    half = CPG // 2
    with ExitStack() as ctx:
        sb = lambda name, shape, dt=F32: core.sb("ed_" + name, shape, dt, ctx)
        key = sb("key", [P, 2, TT], I32)
        before = sb("before", [P, 2, TT], I32)
        src = [sb(f"src{b}", [P, TT], I32) for b in range(2)]
        row_dst = [sb(f"row_dst{b}", [P, 1], I32) for b in range(2)]
        row_fill = [sb(f"row_fill{b}", [P, 4]) for b in range(2)]
        fill = sb("fill", [P, 2, TT, 4])
        got = [sb(f"got{b}", [P, TT, 24]) for b in range(2)]
        run = sb("run", [P, 2, TT], I32)
        start = sb("start", [P, TT])
        carry = sb("carry", [P, TT])
        reset = sb("reset", [P, 4, TT])
        carry4 = sb("carry4", [P, 4, TT])
        fillT = sb("fillT", [P, 4, TT])
        dstT = sb("dstT", [P, 4, TT])
        z = sb("z", [P, 4, TT])
        e = sb("e", [P, 4, TT])
        mx = sb("mx", [P, 4, TT])
        arg = sb("arg", [P, 2, 4, TT])
        weight = sb("weight", [P, 4, TT])
        decay = sb("decay", [P, 20, TT])
        msg = sb("msg", [P, 20, TT])
        acc = sb("acc", [P, 20, TT])
        rowout = sb("rowout", [P, TT, 24])
        one = sb("one", [P, 4])
        hidden_in = sb("hidden_in", [D, CPG * P])
        hid = sb("hid", [P, NX, half * P])
        ps_h = core.ps("ed_ps_h", [P, NX, 512], ctx)
        ps_y = core.ps("ed_ps_y", [P, half, 512], ctx)
        flat = lambda a: a[:].rearrange("p h t -> p (h t)")

        def load(sp, g, b):
            group = lambda a: a.rearrange("(g p t) -> g p t", g=G, p=P)[bass.ts(g, 1)].rearrange("o p t -> (o p) t")
            sp.dma_start(key[:, b, :], group(m.keys.rearrange("a f -> (a f)"))).then_inc(keys_in, 16)
            sp.dma_start(before[:, b, :], group(m.keys_before[0:s.edges])).then_inc(keys_in, 16)
            sp.dma_start(fill[:, b], m.dst_line.rearrange("(g p t) f -> g p t f", g=G, p=P)[bass.ts(g, 1)].rearrange("o p t f -> (o p) t f")).then_inc(fills_in, 16)

        def store(sp, g):
            sp.wait_ge(row_built, 1)
            sp.dma_start(m.results.rearrange("(g p t) f -> g p t f", g=G, p=P)[bass.ts(g, 1)].rearrange("o p t f -> (o p) t f"), rowout[:]).then_inc(stored, 16)

        def sources(v, b):
            v.wait_ge(keys_in, 32)
            v.tensor_scalar(src[b][:], key[:, b, :], s.nodes - 1, None, ALU.bitwise_and)
            v.tensor_scalar(run[:, 0, 0:1], key[:, b, 0:1], NODE_BITS, None, ALU.logical_shift_right)
            v.drain()
            v.tensor_scalar(row_dst[b][:], run[:, 0, 0:1], s.nodes - 1, None, ALU.bitwise_and)
            v.drain()

        def reduce_group(v, g, b, wait_gathers):
            v.tensor_scalar(run[:, 0, :], key[:, b, :], NODE_BITS, None, ALU.logical_shift_right)
            v.tensor_scalar(run[:, 1, :], before[:, b, :], NODE_BITS, None, ALU.logical_shift_right)
            v.drain()
            v.tensor_tensor(start[:], run[:, 0, :], run[:, 1, :], ALU.not_equal)
            v.drain()
            v.tensor_scalar(carry[:], start[:], -1.0, 1.0, ALU.mult, ALU.add)
            v.tensor_reduce(one[:, 0:1], start[:], X, ALU.max)
            v.drain()
            v.tensor_scalar(m.row_open[:, bass.ts(g, 1)], one[:, 0:1], -BIG, None, ALU.mult)
            v.tensor_copy(one[:, 1:2], carry[:, 0:1])
            v.drain()
            v.memset(carry[:, 0:1], 0.0)
            v.drain()
            v.tensor_copy(carry4[:], carry[:, None, :].to_broadcast([P, 4, TT]))
            v.tensor_copy(fillT[:], fill[:, b].rearrange("p t f -> p f t"))
            v.drain()
            v.tensor_scalar(reset[:], carry4[:], BIG, -BIG, ALU.mult, ALU.add)
            if wait_gathers:
                v.wait_ge(row_dst_in, 16)
            v.scalar_tensor_tensor(fillT[:, :, 0], row_fill[b][:], one[:, 1:2], fillT[:, :, 0], ALU.mult, ALU.add)
            v.drain()
            v.tensor_tensor_scan(flat(dstT), flat(carry4), flat(fillT), 0.0, ALU.mult, ALU.add)
            v.drain()
            if wait_gathers:
                v.wait_ge(gathered, 16 * TT)
            v.tensor_tensor(z[:], dstT[:], got[b][:, :, 20:24].rearrange("p t f -> p f t"), ALU.add)
            v.drain()
            v.scalar_tensor_tensor(flat(e), flat(z), 0.2, flat(z), ALU.mult, ALU.max)
            v.drain()
            v.tensor_tensor_scan(flat(mx), flat(reset), flat(e), 0.0, ALU.add, ALU.max)
            v.drain()
            v.tensor_tensor(arg[:, 0], e[:], mx[:], ALU.subtract)
            v.tensor_copy(arg[:, 1, :, 0:1], reset[:, :, 0:1])
            v.tensor_tensor(z[:, :, 1:TT], mx[:, :, 0:TT - 1], mx[:, :, 1:TT], ALU.subtract)
            v.drain()
            v.tensor_tensor(arg[:, 1, :, 1:TT], z[:, :, 1:TT], reset[:, :, 1:TT], ALU.add)
            v.drain()
            v.nop().then_inc(logits_ready, 1)
            v.wait_ge(exped, 1)
            v.tensor_tensor(msg[:].rearrange("p (h f) t -> p h f t", f=5),
                            got[b][:, :, 0:20].rearrange("p t (h f) -> p h f t", f=5),
                            weight[:, :, None, :].to_broadcast([P, 4, 5, TT]), ALU.mult)
            v.drain()
            v.tensor_tensor_scan(flat(acc), flat(decay), flat(msg), 0.0, ALU.mult, ALU.add)
            v.drain()
            v.tensor_copy(rowout[:, :, 0:20], acc[:].rearrange("p f t -> p t f"))
            v.tensor_copy(rowout[:, :, 20:24], mx[:].rearrange("p f t -> p t f"))
            v.tensor_copy(m.row_sum[:, bass.ts(g, 1), :], acc[:, :, TT - 1:TT].rearrange("p f o -> p o f"))
            v.tensor_copy(m.row_max[:, bass.ts(g, 1), :], mx[:, :, TT - 1:TT].rearrange("p f o -> p o f"))
            v.drain()
            v.nop().then_inc(row_built, 1)

        def weights(act):
            act.wait_ge(logits_ready, 1)
            act.activation(weight[:], arg[:, 0], ACT.Exp)
            act.activation(decay[:].rearrange("p (h f) t -> p h f t", f=5),
                           arg[:, 1, :, None, :].to_broadcast([P, 4, 5, TT]), ACT.Exp).then_inc(exped, 1)

        def gathers(pool, b):
            gather(pool, row_fill[b][:], m.dst_table, row_dst[b][:]).then_inc(row_dst_in, 16)
            for t in range(TT):
                gather(pool, got[b][:, t, :], m.table, src[b][:, t:t + 1]).then_inc(gathered, 16)
            pool.wait_ge(row_dst_in, 16)
            pool.wait_ge(gathered, 16 * TT)

        counted = [keys_in, fills_in, stored, src_ready, logits_ready, exped, row_built, hid_scored, hid_taken, exp_scored,
                   exp_taken, tokens_copied]

        def piped_round(g, b, share):
            with nc.Block() as block:
                @block.sync
                def _(sp):
                    store(sp, g - 1)
                    load(sp, g + 1, 1 - b)
                    sp.wait_ge(fills_in, 16)
                    sp.wait_ge(stored, 16)

                @block.gpsimd
                def _(pool):
                    gathers(pool, b)

                @block.tensor
                def _(pe):
                    pe.wait_ge(tokens_copied, 1)
                    for u in range(2):
                        if u:
                            pe.wait_ge(hid_taken, u)
                        for k in range(NX):
                            last = pe.matmul(ps_h[:, k, :], m.w1x[:, k, :], hidden_in[:, u * half * P:(u + 1) * half * P],
                                             start=True, stop=True)
                        last.then_inc(hid_scored, 1)
                        pe.wait_ge(hid_taken, u + 1)
                        if u:
                            pe.wait_ge(exp_taken, u)
                        for c in range(half):
                            for k in range(NX):
                                last = pe.matmul(ps_y[:, c, k * D:(k + 1) * D], hid[:, k, c * P:(c + 1) * P], m.w2x[:, k, :],
                                                 start=True, stop=True)
                        last.then_inc(exp_scored, 1)

                @block.scalar
                def _(act):
                    act.copy(hidden_in[:], m.x4T[:, bass.ts(share, CPG * P)]).then_inc(tokens_copied, 1)
                    weights(act)
                    for u in range(2):
                        act.wait_ge(hid_scored, u + 1)
                        for k in range(NX):
                            last = act.activation(hid[:, k, :], ps_h[:, k, :], ACT.Gelu, bias=m.b1x[:, k:k + 1])
                        last.then_inc(hid_taken, 1)

                @block.vector
                def _(v):
                    reduce_group(v, g - 1, 1 - b, False)
                    sources(v, 1 - b)
                    for u in range(2):
                        v.wait_ge(exp_scored, u + 1)
                        v.tensor_tensor(m.expert[:, bass.ds(share * CPG + u * half, half), :, :].rearrange("p c e d -> p c (e d)"),
                                        ps_y[:, :, 0:NX * D],
                                        m.b2x[:].rearrange("p e d -> p (e d)")[:, None, :].to_broadcast([P, half, NX * D]), ALU.add).then_inc(exp_taken, 1)

            core.clear(counted, (row_dst_in, gathered))

        def whole_round(g):
            with nc.Block() as block:
                @block.sync
                def _(sp):
                    load(sp, g, 0)
                    sp.wait_ge(fills_in, 16)
                    store(sp, g)
                    sp.wait_ge(stored, 16)

                @block.gpsimd
                def _(pool):
                    pool.wait_ge(src_ready, 1)
                    gathers(pool, 0)

                @block.tensor
                def _(pe):
                    pe.nop()

                @block.scalar
                def _(act):
                    weights(act)

                @block.vector
                def _(v):
                    sources(v, 0)
                    v.nop().then_inc(src_ready, 1)
                    v.wait_ge(fills_in, 16)
                    reduce_group(v, g, 0, True)

            core.clear(counted, (row_dst_in, gathered))

        for b in range(2):
            with nc.Block() as block:
                @block.sync
                def _(sp):
                    load(sp, b, b)
                    sp.wait_ge(fills_in, 16)

                @block.vector
                def _(v):
                    sources(v, b)
                    if b == 0:
                        v.memset(m.row_sum[:], 0.0)
                        v.memset(m.row_max[:], -BIG)
                        v.memset(m.row_open[:], 0.0)

                @block.gpsimd
                def _(pool):
                    if b == 1:
                        gathers(pool, 0)
            core.clear(counted, (row_dst_in, gathered) if b else ())
        with nc.Fori(0, rounds // 2) as i:
            piped_round(2 * i + 1, 1, 2 * i)
            piped_round(2 * i + 2, 0, 2 * i + 1)
        with nc.Block() as block:
            @block.sync
            def _(sp):
                store(sp, base - 1)
                sp.wait_ge(stored, 16)

            @block.scalar
            def _(act):
                weights(act)

            @block.vector
            def _(v):
                reduce_group(v, base - 1, 0, False)
        core.clear(counted)

        active = nc.values_load(m.active[0:1, 0:1], min_val=0, max_val=G,
                                skip_runtime_bounds_check_because="a count of edges over the edges of a group")
        with nc.Fori(base, G) as g:
            with nc.If(g < active):
                whole_round(g)
            nc.end_ifs()


def finish(core, s, m, w, out):
    nc = core.nc
    G, C, D, NX, TT = s.groups, s.cols, s.dim, s.experts1, s.group_t
    rows = G * P
    HC = C // 2
    carried = core.dram("carried", [rows + 1, 24])
    sem = core.sem
    packed = sem("fi_packed")
    turned = sem("fi_turned")
    v_taken = sem("fi_v_taken")
    a_taken = sem("fi_a_taken")
    exp_wanted = sem("fi_exp_wanted")
    exped = sem("fi_exped")
    chained = sem("fi_chained")
    turned_back = sem("fi_turned_back")
    carry_built = sem("fi_carry_built")
    carry_out = sem("fi_carry_out")
    place_ready = sem("fi_place_ready")
    runs_in = sem("fi_runs_in")
    carries_in = sem("fi_carries_in")
    variance = sem("fi_variance")
    powed = sem("fi_powed")
    out_ready = sem("fi_out_ready")
    out_stored = sem("fi_out_stored")
    with ExitStack() as ctx:
        sb = lambda name, shape, dt=F32: core.sb("fi_" + name, shape, dt, ctx)
        value = [sb(f"value{i}", [P, C, 24]) for i in range(2)]
        place = sb("place", [P, 3, C])
        place_i = sb("place_i", [P, 3, C], I32)
        with ExitStack() as ctx2:
            sb2 = lambda name, shape, dt=F32: core.sb("fi_" + name, shape, dt, ctx2)
            pack = sb2("pack", [P, G, 96])
            sums = m.x4T[0:20, 0:rows]
            maxs = m.x4T[0:20, rows:2 * rows]
            decay = sb2("decay", [20, rows])
            chain = sb2("chain", [20, rows])
            carry = sb2("carry", [P, G, 24])
            zero = sb2("zero", [1, 24])
            ps = core.ps("fi_ps", [P, 4, 512], ctx2)
            ps_back = core.ps("fi_back", [P, 4, 512], ctx2)
            per_round = 8
            rounds = G // per_round
            with nc.Block() as block:
                @block.sync
                def _(sp):
                    sp.wait_ge(carry_built, 1)
                    sp.dma_start(carried[0:1, :], zero[:]).then_inc(carry_out, 16)
                    sp.dma_start(carried[1:rows + 1, :].rearrange("(g p) f -> p g f", p=P), carry[:]).then_inc(carry_out, 16)
                    sp.wait_ge(carry_out, 32)

                @block.gpsimd
                def _(pool):
                    pool.wait_ge(place_ready, 1)
                    for c in range(C):
                        gather(pool, value[0][:, c, :], m.results, place_i[:, 0, c:c + 1]).then_inc(runs_in, 16)
                    pool.wait_ge(carry_out, 32)
                    for c in range(HC):
                        gather(pool, value[1][:, c, :], carried, place_i[:, 1, c:c + 1]).then_inc(carries_in, 16)
                    pool.wait_ge(runs_in, 16 * C)
                    pool.wait_ge(carries_in, 16 * HC)

                @block.tensor
                def _(pe):
                    pe.wait_ge(packed, 1)
                    for r in range(rounds):
                        if r >= 2:
                            pe.wait_ge(v_taken, r - 1)
                            pe.wait_ge(a_taken, r - 1)
                        for i in range(per_round):
                            last = pe.transpose(ps[0:96, 2 * (r % 2) + i // 4, (i % 4) * P:(i % 4 + 1) * P],
                                                pack[:, r * per_round + i, :], m.ident[:])
                        last.then_inc(turned, 1)
                    pe.wait_ge(chained, 1)
                    for i, of in enumerate((sums, chain)):
                        for g in range(G):
                            last = pe.transpose(ps_back[:, 2 * i + g // 16, (g % 16) * 20:(g % 16 + 1) * 20],
                                                of[:, g * P:(g + 1) * P], m.ident[0:20, 0:20])
                    last.then_inc(turned_back, 1)

                @block.scalar
                def _(act):
                    for r in range(rounds):
                        act.wait_ge(turned, r + 1)
                        act.wait_ge(v_taken, r + 1)
                        span = slice(r * per_round * P, (r + 1) * per_round * P)
                        bank = ps[:, 2 * (r % 2):2 * (r % 2) + 2, :].rearrange("p a b -> p (a b)")
                        act.copy(sums[:, span], bank[0:20, :]).then_inc(a_taken, 1)
                    act.wait_ge(exp_wanted, 1)
                    act.activation(maxs, maxs, ACT.Exp)
                    act.activation(decay[:], decay[:], ACT.Exp).then_inc(exped, 1)

                @block.vector
                def _(v):
                    v.memset(zero[:], 0.0)
                    v.tensor_scalar(place[:, 0, :], m.after[:, 0, :], 1.0, 0.0, ALU.subtract, ALU.max)
                    v.memset(pack[:], 0.0)
                    v.drain()
                    v.tensor_copy(place_i[:, 0, :], place[:, 0, :])
                    v.tensor_copy(pack[:, :, 0:20], m.row_sum[:])
                    v.tensor_copy(pack[:, :, 32:52].rearrange("p g (h f) -> p g h f", f=5), m.row_max[:, :, :, None].to_broadcast([P, G, 4, 5]))
                    v.tensor_copy(pack[:, :, 64:84], m.row_open[:, :, None].to_broadcast([P, G, 20]))
                    v.drain()
                    v.nop().then_inc(packed, 1)
                    v.tensor_scalar(place_i[:, 1, :], place_i[:, 0, :], TT.bit_length() - 1, None, ALU.logical_shift_right)
                    v.drain()
                    v.tensor_scalar(place_i[:, 2, :], place_i[:, 1, :], TT.bit_length() - 1, None, ALU.logical_shift_left)
                    v.nop().then_inc(place_ready, 1)
                    v.drain()
                    v.tensor_copy(place[:, 2, :], place_i[:, 2, :])
                    for r in range(rounds):
                        v.wait_ge(turned, r + 1)
                        span = slice(r * per_round * P, (r + 1) * per_round * P)
                        bank = ps[:, 2 * (r % 2):2 * (r % 2) + 2, :].rearrange("p a b -> p (a b)")
                        v.tensor_copy(maxs[:, span], bank[32:52, :])
                        v.tensor_copy(decay[:, span], bank[64:84, :]).then_inc(v_taken, 1)
                    v.drain()
                    v.tensor_tensor_scan(chain[:], decay[:], maxs, -BIG, ALU.add, ALU.max)
                    v.drain()
                    v.tensor_tensor(maxs, maxs, chain[:], ALU.subtract)
                    v.tensor_tensor(decay[:, 1:rows], decay[:, 1:rows], chain[:, 0:rows - 1], ALU.add)
                    v.drain()
                    v.tensor_tensor(decay[:, 1:rows], decay[:, 1:rows], chain[:, 1:rows], ALU.subtract)
                    v.drain()
                    v.nop().then_inc(exp_wanted, 1)
                    v.wait_ge(exped, 1)
                    v.wait_ge(a_taken, rounds)
                    v.tensor_tensor(maxs, maxs, sums, ALU.mult)
                    v.drain()
                    v.tensor_tensor_scan(sums, decay[:], maxs, 0.0, ALU.mult, ALU.add)
                    v.drain()
                    v.nop().then_inc(chained, 1)
                    v.wait_ge(turned_back, 1)
                    back = lambda i: ps_back[:, 2 * i:2 * i + 2, 0:320].rearrange("p a (g f) -> p a g f", f=20)
                    both = carry[:].rearrange("p (a g) f -> p a g f", a=2)
                    v.tensor_copy(both[:, :, :, 0:20], back(0))
                    v.tensor_copy(both[:, :, :, 20:24], back(1).rearrange("p a g (h f) -> p a g h f", f=5)[:, :, :, :, 0])
                    v.drain()
                    v.nop().then_inc(carry_built, 1)

        logit = sb("logit", [P, 4, HC, 4])
        mask = sb("mask", [P, 3, HC])
        count = sb("count", [P, HC])
        top = sb("top", [P, HC, 4])
        term = [sb(f"term{i}", [P, HC, 4, 5]) for i in range(2)]
        agg = sb("agg", [P, HC, 4, 4])
        sq = sb("sq", [P, HC, 4, 4])
        stat = sb("stat", [P, 4, HC])
        score = sb("score", [P, HC, 4])
        hot = sb("hot", [P, 2, HC, 4])
        gate = sb("gate", [P, HC, 4])
        best = sb("best", [P, 4, HC])
        one = sb("one", [P, HC, 4, 5])
        last = sb("last", [P, 4, 5])
        chunk = 8
        mix = sb("mix", [P, chunk, D])
        with nc.Block() as block:
            @block.gpsimd
            def _(pool):
                def gather_carries(columns):
                    for c in columns:
                        gather(pool, value[1][:, c, :], carried, place_i[:, 1, c:c + 1]).then_inc(carries_in, 16)

                gather_carries(range(HC, HC + HC // 2))
                for i in range(2):
                    pool.wait_ge(variance, i + 1)
                    pool.tensor_scalar(stat[:, 2, :], stat[:, 1, :], 1.0 / 16, 1e-5, ALU.mult, ALU.add)
                    pool.drain()
                    pool.tensor_tensor(stat[:, 3, :], stat[:, 2, :], m.minus_half[:, 0:HC], ALU.pow).then_inc(powed, 1)
                    if i == 0:
                        gather_carries(range(HC + HC // 2, C))
                pool.wait_ge(carries_in, 16 * C)

            @block.scalar
            def _(act):
                for i in range(2):
                    act.wait_ge(exp_wanted, 2 + 2 * i)
                    act.activation(logit[:], logit[:], ACT.Exp).then_inc(exped, 1)
                    act.wait_ge(exp_wanted, 3 + 2 * i)
                    act.activation(best[:, 2, :], best[:, 1, :], ACT.Exp).then_inc(exped, 1)

            @block.sync
            def _(sp):
                n_out = C // chunk
                rows_out = out.rearrange("b t d -> (b t) d").rearrange("(c p) d -> p c d", p=P)
                for i in range(n_out):
                    sp.wait_ge(out_ready, i + 1)
                    sp.dma_start(rows_out[:, i * chunk:(i + 1) * chunk, :], m.h[:, i * chunk:(i + 1) * chunk, :]).then_inc(out_stored, 16)
                sp.wait_ge(out_stored, 16 * n_out)

            @block.vector
            def _(v):
                for i in range(2):
                    mine = slice(i * HC, (i + 1) * HC)
                    if i:
                        v.wait_ge(carries_in, 16 * C)
                        v.drain()
                    wide = lambda a: a[:, :, None].to_broadcast([P, HC, 4])
                    v.tensor_tensor(count[:], m.after[:, 1, mine], m.begin[:, 1, mine], ALU.subtract)
                    v.tensor_tensor(mask[:, 0, :], m.after[:, 0, mine], m.begin[:, 0, mine], ALU.is_gt)
                    v.tensor_tensor(mask[:, 1, :], place[:, 2, mine], m.begin[:, 0, mine], ALU.is_gt)
                    v.tensor_tensor(mask[:, 2, :], m.after[:, 1, mine], m.begin[:, 1, mine], ALU.is_gt)
                    v.tensor_tensor(logit[:, 2], m.node[:, mine, 16:20], m.node[:, mine, 20:24], ALU.add)
                    v.tensor_tensor(logit[:, 3], m.node[:, mine, 20:24], m.last_row[:, None, 20:24].to_broadcast([P, HC, 4]), ALU.add)
                    v.tensor_copy(one[:, :, :, 0:4], m.node[:, mine, 0:16].rearrange("p c (h f) -> p c h f", h=4))
                    v.memset(one[:, :, :, 4:5], 1.0)
                    v.tensor_copy(last[:], m.last_row[:, 0:20].rearrange("p (h f) -> p h f", h=4))
                    v.drain()
                    v.tensor_tensor(mask[:, 1, :], mask[:, 1, :], mask[:, 0, :], ALU.mult)
                    v.scalar_tensor_tensor(logit[:, 2:4], logit[:, 2:4], 0.2, logit[:, 2:4], ALU.mult, ALU.max)
                    v.drain()
                    v.tensor_tensor(logit[:, 0], value[0][:, mine, 20:24], wide(mask[:, 0, :]), ALU.mult)
                    v.tensor_tensor(logit[:, 1], value[1][:, mine, 20:24], wide(mask[:, 1, :]), ALU.mult)
                    v.tensor_tensor(logit[:, 3], logit[:, 3], wide(mask[:, 2, :]), ALU.mult)
                    v.drain()
                    v.tensor_scalar(mask[:], mask[:], BIG, -BIG, ALU.mult, ALU.add)
                    v.drain()
                    for a, k in ((0, 0), (1, 1), (3, 2)):
                        v.tensor_tensor(logit[:, a], logit[:, a], wide(mask[:, k, :]), ALU.add)
                    v.drain()
                    v.tensor_reduce(top[:], logit[:].rearrange("p i c h -> p c h i"), X, ALU.max)
                    v.drain()
                    v.tensor_tensor(logit[:], logit[:], top[:, None, :, :].to_broadcast([P, 4, HC, 4]), ALU.subtract)
                    v.drain()
                    v.nop().then_inc(exp_wanted, 1)
                    v.wait_ge(exped, 2 + 2 * i)
                    v.tensor_tensor(logit[:, 3], logit[:, 3], wide(count[:]), ALU.mult)
                    v.drain()
                    weight = lambda i: logit[:, i, :, :, None].to_broadcast([P, HC, 4, 5])
                    rows = lambda a: a[:, :, 0:20].rearrange("p c (h f) -> p c h f", h=4)
                    v.tensor_tensor(term[0][:], rows(value[0][:, mine, :]), weight(0), ALU.mult)
                    v.tensor_tensor(term[1][:], rows(value[1][:, mine, :]), weight(1), ALU.mult)
                    v.tensor_tensor(one[:], one[:], weight(2), ALU.mult)
                    v.drain()
                    v.tensor_tensor(term[0][:], term[0][:], term[1][:], ALU.add)
                    v.drain()
                    v.tensor_tensor(term[1][:], last[:, None, :, :].to_broadcast([P, HC, 4, 5]), weight(3), ALU.mult)
                    v.tensor_tensor(term[0][:], term[0][:], one[:], ALU.add)
                    v.drain()
                    v.tensor_tensor(term[0][:], term[0][:], term[1][:], ALU.add)
                    v.drain()
                    v.tensor_scalar(top[:], term[0][:, :, :, 4], 1e-16, None, ALU.add)
                    v.drain()
                    v.reciprocal(top[:], top[:])
                    v.drain()
                    v.tensor_tensor(agg[:], term[0][:, :, :, 0:4], top[:, :, :, None].to_broadcast([P, HC, 4, 4]), ALU.mult)
                    v.drain()
                    flat = lambda a: a[:].rearrange("p c h f -> p c (h f)")
                    row16 = lambda a: a[:, None, :].to_broadcast([P, HC, 16])
                    v.tensor_tensor(flat(agg), flat(agg), row16(m.bgat), ALU.add)
                    v.drain()
                    v.tensor_reduce(stat[:, 0, :], flat(agg), X, ALU.add)
                    v.drain()
                    v.tensor_scalar(stat[:, 0, :], stat[:, 0, :], 1.0 / 16, None, ALU.mult)
                    v.drain()
                    v.tensor_tensor(flat(agg), flat(agg), stat[:, 0, :, None].to_broadcast([P, HC, 16]), ALU.subtract)
                    v.drain()
                    v.tensor_tensor(sq[:], agg[:], agg[:], ALU.mult)
                    v.drain()
                    v.tensor_reduce(stat[:, 1, :], flat(sq), X, ALU.add)
                    v.drain()
                    v.nop().then_inc(variance, 1)
                    v.wait_ge(powed, i + 1)
                    v.tensor_tensor(flat(agg), flat(agg), stat[:, 3, :, None].to_broadcast([P, HC, 16]), ALU.mult)
                    v.drain()
                    v.tensor_tensor(flat(agg), flat(agg), row16(m.gamma), ALU.mult)
                    v.drain()
                    v.tensor_tensor(flat(agg), flat(agg), row16(m.beta), ALU.add)
                    v.drain()
                    v.tensor_reduce(score[:], agg[:].rearrange("p c h f -> p c f h"), X, ALU.add)
                    v.drain()
                    v.tensor_scalar(score[:], score[:], 0.25, None, ALU.mult)
                    v.drain()
                    for k in range(2):
                        v.tensor_reduce(best[:, k, :], score[:], X, ALU.max)
                        v.drain()
                        v.tensor_tensor(hot[:, k], score[:], wide(best[:, k, :]), ALU.is_equal)
                        v.drain()
                        v.tensor_tensor(hot[:, k], hot[:, k], m.first_slot[:, None, 0:4].to_broadcast([P, HC, 4]), ALU.mult)
                        v.drain()
                        v.tensor_reduce(best[:, 3, :], hot[:, k], X, ALU.max)
                        v.drain()
                        v.tensor_tensor(hot[:, k], hot[:, k], wide(best[:, 3, :]), ALU.is_equal)
                        v.drain()
                        if k == 0:
                            v.scalar_tensor_tensor(score[:], hot[:, 0], -BIG, score[:], ALU.mult, ALU.add)
                            v.drain()
                    v.tensor_tensor(best[:, 1, :], best[:, 1, :], best[:, 0, :], ALU.subtract)
                    v.drain()
                    v.nop().then_inc(exp_wanted, 1)
                    v.wait_ge(exped, 3 + 2 * i)
                    v.tensor_scalar(best[:, 0, :], best[:, 2, :], 1.0, None, ALU.add)
                    v.drain()
                    v.reciprocal(best[:, 0, :], best[:, 0, :])
                    v.drain()
                    v.tensor_tensor(hot[:, 1], hot[:, 1], wide(best[:, 2, :]), ALU.mult)
                    v.drain()
                    v.tensor_tensor(gate[:], hot[:, 0], hot[:, 1], ALU.add)
                    v.drain()
                    v.tensor_tensor(gate[:], gate[:], wide(best[:, 0, :]), ALU.mult)
                    v.drain()
                    for n in range(HC // chunk):
                        cols = slice(i * HC + n * chunk, i * HC + (n + 1) * chunk)
                        part = m.expert[:, cols, :, :]
                        v.tensor_tensor(part, part, gate[:, n * chunk:(n + 1) * chunk, :, None].to_broadcast([P, chunk, NX, D]), ALU.mult)
                        v.drain()
                        v.tensor_reduce(mix[:], part.rearrange("p c e d -> p c d e"), X, ALU.add)
                        v.drain()
                        v.tensor_tensor(m.h[:, cols, :], m.h[:, cols, :], mix[:], ALU.add).then_inc(out_ready, 1)


def build(nc, w, out):
    with ExitStack() as ctx:
        core = Core(nc, ctx)
        s = Shapes(w["x"], w["L0_tok_emb"], w["L0_attn_Q"], w["L0_ffn_W1"], w["L0_ffn_Wd"], w["L1_ffn_W1"], w["L1_ffn_edge_index"])
        m = Store()
        m.turn_src = turn_sources(s)
        load_weights(core, s, m, w)
        embed_and_sort(core, s, m, w)
        tower(core, s, m, w)
        node_tables(core, s, m)
        edges(core, s, m, w)
        finish(core, s, m, w, out)


def kernel(**inputs):
    import numpy as _np
    import concourse.bacc as _bacc
    from concourse import mybir as _mybir
    from concourse.bass_utils import run_bass_kernel_spmd as _run

    nc = _bacc.Bacc("TRN2", target_bir_lowering=False, num_devices=1)
    arrays, aps = {}, {}
    for name, value in inputs.items():
        a = _np.ascontiguousarray(value)
        arrays[f"in_{name}_dram"] = a
        aps[name] = nc.dram_tensor(f"in_{name}_dram", a.shape, _mybir.dt.from_np(a.dtype), kind="ExternalInput").ap()
    shape = tuple(inputs["x"].shape) + (inputs["L0_tok_emb"].shape[1],)
    out = nc.dram_tensor("out_0_dram", shape, _mybir.dt.float32, kind="ExternalOutput").ap()
    build(nc, aps, out)
    r = _run(nc, [arrays], core_ids=[0])
    return r.results[0]["out_0_dram"]
```
